# Optimizing a Trainium2 kernel written in Bass

```python
import numpy as np
import jax
import jax.numpy as jnp

def _softmax(x, axis=-1):
    return jax.nn.softmax(x, axis=axis)

def _gelu(x):
    return jax.nn.gelu(x, approximate=True)

def _silu(x):
    return jax.nn.silu(x)

def _sigmoid(x):
    return jax.nn.sigmoid(x)

def _layernorm(x, axis=-1, eps=1e-05):
    m = jnp.mean(x, axis=axis, keepdims=True)
    v = jnp.var(x, axis=axis, keepdims=True)
    return (x - m) / jnp.sqrt(v + eps)

def _scatter_add(tgt, idx, src, axis=0):
    return tgt.at[idx].add(src)

def _segment_sum(src, seg, n):
    return jax.ops.segment_sum(src, seg, n)
kernel_name = 'mk_adj_resnorm_d4_adj_r2_2dee63'

def setup_inputs(seed: int=0):
    np.random.seed(seed)
    _w = jnp.asarray

    def _rec_inputs():
        import jax
        import jax.numpy as jnp
        _gk = jax.random.key(seed)
        x = -0.0003929 + 0.9999 * jax.random.normal(jax.random.fold_in(_gk, 1), (8, 1024, 256), jnp.float32)
        _a = jax.random.bernoulli(jax.random.fold_in(_gk, 2), 0.0078125, (8, 1024, 1024))
        _a = jnp.logical_or(_a, jnp.eye(1024, dtype=bool))
        _af = _a.astype(jnp.float32)
        _af = _af * jax.random.uniform(jax.random.fold_in(_gk, 3), (8, 1024, 1024), jnp.float32, 0.05, 1)
        adj = _af
        return (x, adj)
    x, adj = _rec_inputs()

    def _L0_gnn_setup():
        import jax, jax.numpy as jnp
        import numpy as np
        EPS = 1e-06
        key = jax.random.key(seed)
        k1, k2, k3 = jax.random.split(key, 3)
        B, N, F, O = (8, 2048, 256, 256)
        x = jax.random.normal(k1, (B, N, F), dtype=jnp.float32)
        adj = jax.random.uniform(k2, (B, N, N), dtype=jnp.float32)
        W = jax.random.normal(k3, (O, 2 * F), dtype=jnp.float32) * (1.0 / np.sqrt(2 * F))
        return {'x': x, 'adj': adj, 'W': W}
    _L0_gnn_all = _L0_gnn_setup()
    _L0_gnn_in = {k: v for k, v in _L0_gnn_all.items() if k in ('W',)}
    del _L0_gnn_all

    def _L1_gnn_setup():
        import jax, jax.numpy as jnp
        import numpy as np
        N = 4096
        F = 256
        C = 256
        key = jax.random.key(seed)
        k1, k2, k3 = jax.random.split(key, 3)
        X = jax.random.normal(k1, (1, N, F), dtype=jnp.float32)
        A = jax.random.uniform(k2, (1, N, N), dtype=jnp.float32)
        kernel = jax.random.normal(k3, (F, C), dtype=jnp.float32) * (1.0 / np.sqrt(F))
        bias = jnp.zeros((C,), dtype=jnp.float32)
        return {'X': X, 'A': A, 'kernel': kernel, 'bias': bias}
    _L1_gnn_all = _L1_gnn_setup()
    _L1_gnn_in = {k: v for k, v in _L1_gnn_all.items() if k in ('kernel', 'bias')}
    del _L1_gnn_all

    def _L2_gnn_setup():
        import jax, jax.numpy as jnp
        import numpy as np
        EPS_LN = 1e-05

        def hypergraph_conv(x, adj, W, b):
            N, C, _ = adj.shape
            H = (adj != 0).astype(x.dtype)
            w = adj.reshape(N, -1)[:, :C]
            xw = jnp.einsum('ncd,hd->nch', x, W)
            Dn = jnp.einsum('nce,ne->nc', H, w)
            Dn = jnp.where(Dn > 0, 1.0 / Dn, 0.0)
            Be = H.sum(axis=1)
            Be = jnp.where(Be > 0, 1.0 / Be, 0.0)
            m = Be[:, :, None] * jnp.einsum('nce,nch->neh', H, xw)
            out = Dn[:, :, None] * jnp.einsum('nce,neh->nch', H, m)
            return out + b

        def layer_norm(x, g, b):
            mu = jnp.mean(x, axis=-1, keepdims=True)
            var = jnp.var(x, axis=-1, keepdims=True)
            return (x - mu) * jax.lax.rsqrt(var + EPS_LN) * g + b
        key = jax.random.key(seed)
        ks = jax.random.split(key, 4)
        N, C, Din, Dh, Dout = (16, 512, 256, 512, 256)
        x = jax.random.normal(ks[0], (N, C, Din), dtype=jnp.float32)
        adj = jax.random.uniform(ks[1], (N, C, C), dtype=jnp.float32, minval=0.1, maxval=1.0)
        W1 = jax.random.normal(ks[2], (Dh, Din), dtype=jnp.float32) * (1.0 / np.sqrt(Din))
        b1 = jnp.zeros((Dh,), dtype=jnp.float32)
        gamma = jnp.ones((Dh,), dtype=jnp.float32)
        beta = jnp.zeros((Dh,), dtype=jnp.float32)
        W2 = jax.random.normal(ks[3], (Dout, Dh), dtype=jnp.float32) * (1.0 / np.sqrt(Dh))
        b2 = jnp.zeros((Dout,), dtype=jnp.float32)
        return {'x': x, 'adj': adj, 'W1': W1, 'b1': b1, 'gamma': gamma, 'beta': beta, 'W2': W2, 'b2': b2}
    _L2_gnn_all = _L2_gnn_setup()
    _L2_gnn_in = {k: v for k, v in _L2_gnn_all.items() if k in ('W1', 'b1', 'gamma', 'beta', 'W2', 'b2')}
    del _L2_gnn_all

    def _L3_gnn_setup():
        import jax, jax.numpy as jnp
        import numpy as np
        B, N, F_IN, F_HID, F_OUT = (32, 512, 256, 256, 256)

        def _gcn_layer(x, adj, W, b):
            support = jnp.einsum('bnf,fh->bnh', x, W)
            return jnp.einsum('bnm,bmh->bnh', adj, support) + b
        key = jax.random.key(seed)
        ks = jax.random.split(key, 8)

        def xavier(k, fan_in, fan_out):
            bound = float(np.sqrt(6.0 / (fan_in + fan_out)))
            return jax.random.uniform(k, (fan_in, fan_out), jnp.float32, -bound, bound)
        return {'batch_graph': jax.random.normal(ks[0], (B, N, F_IN), jnp.float32), 'adj': jax.random.uniform(ks[1], (B, N, N), jnp.float32), 'W1': xavier(ks[2], F_IN, F_HID), 'b1': jnp.zeros((F_HID,), jnp.float32), 'W2': xavier(ks[3], F_HID, F_HID), 'b2': jnp.zeros((F_HID,), jnp.float32), 'W3': xavier(ks[4], F_HID, F_OUT), 'b3': jnp.zeros((F_OUT,), jnp.float32)}
    _L3_gnn_all = _L3_gnn_setup()
    _L3_gnn_in = {k: v for k, v in _L3_gnn_all.items() if k in ('W1', 'b1', 'W2', 'b2', 'W3', 'b3')}
    del _L3_gnn_all
    return {'x': x, 'adj': adj, 'L0_gnn_W': _L0_gnn_in['W'], 'L1_gnn_kernel': _L1_gnn_in['kernel'], 'L1_gnn_bias': _L1_gnn_in['bias'], 'L2_gnn_W1': _L2_gnn_in['W1'], 'L2_gnn_b1': _L2_gnn_in['b1'], 'L2_gnn_gamma': _L2_gnn_in['gamma'], 'L2_gnn_beta': _L2_gnn_in['beta'], 'L2_gnn_W2': _L2_gnn_in['W2'], 'L2_gnn_b2': _L2_gnn_in['b2'], 'L3_gnn_W1': _L3_gnn_in['W1'], 'L3_gnn_b1': _L3_gnn_in['b1'], 'L3_gnn_W2': _L3_gnn_in['W2'], 'L3_gnn_b2': _L3_gnn_in['b2'], 'L3_gnn_W3': _L3_gnn_in['W3'], 'L3_gnn_b3': _L3_gnn_in['b3']}

def reference(x, adj, L0_gnn_W, L1_gnn_kernel, L1_gnn_bias, L2_gnn_W1, L2_gnn_b1, L2_gnn_gamma, L2_gnn_beta, L2_gnn_W2, L2_gnn_b2, L3_gnn_W1, L3_gnn_b1, L3_gnn_W2, L3_gnn_b2, L3_gnn_W3, L3_gnn_b3):
    import jax
    import jax.numpy as jnp

    def _L0_gnn_ref(x, adj, W):
        import jax, jax.numpy as jnp
        import numpy as np
        EPS = 1e-06
        deg = jnp.sum(adj, axis=-1, keepdims=True)
        agg = jnp.einsum('bij,bjf->bif', adj, x) / jnp.maximum(deg, EPS)
        cat = jnp.concatenate([x, agg], axis=2)
        out = jnp.einsum('bnf,of->bno', cat, W)
        return jax.nn.relu(out)

    def _L1_gnn_ref(X, A, kernel, bias):
        import jax, jax.numpy as jnp
        import numpy as np
        N = 4096
        F = 256
        C = 256
        Ah = A + jnp.eye(A.shape[-1], dtype=A.dtype)[None, :, :]
        dh = jax.lax.rsqrt(jnp.sum(Ah, axis=-1))
        An = dh[:, :, None] * Ah * dh[:, None, :]
        out = jnp.einsum('bnm,bmf,fc->bnc', An, X, kernel) + bias
        return jax.nn.relu(out)

    def _L2_gnn_ref(x, adj, W1, b1, gamma, beta, W2, b2):
        import jax, jax.numpy as jnp
        import numpy as np
        EPS_LN = 1e-05

        def hypergraph_conv(x, adj, W, b):
            N, C, _ = adj.shape
            H = (adj != 0).astype(x.dtype)
            w = adj.reshape(N, -1)[:, :C]
            xw = jnp.einsum('ncd,hd->nch', x, W)
            Dn = jnp.einsum('nce,ne->nc', H, w)
            Dn = jnp.where(Dn > 0, 1.0 / Dn, 0.0)
            Be = H.sum(axis=1)
            Be = jnp.where(Be > 0, 1.0 / Be, 0.0)
            m = Be[:, :, None] * jnp.einsum('nce,nch->neh', H, xw)
            out = Dn[:, :, None] * jnp.einsum('nce,neh->nch', H, m)
            return out + b

        def layer_norm(x, g, b):
            mu = jnp.mean(x, axis=-1, keepdims=True)
            var = jnp.var(x, axis=-1, keepdims=True)
            return (x - mu) * jax.lax.rsqrt(var + EPS_LN) * g + b
        h = jax.nn.relu(hypergraph_conv(x, adj, W1, b1))
        h = layer_norm(h, gamma, beta)
        y = hypergraph_conv(h, adj, W2, b2)
        return y + x

    def _L3_gnn_ref(batch_graph, adj, W1, b1, W2, b2, W3, b3):
        import jax, jax.numpy as jnp
        import numpy as np
        B, N, F_IN, F_HID, F_OUT = (32, 512, 256, 256, 256)

        def _gcn_layer(x, adj, W, b):
            support = jnp.einsum('bnf,fh->bnh', x, W)
            return jnp.einsum('bnm,bmh->bnh', adj, support) + b
        x = jax.nn.relu(_gcn_layer(batch_graph, adj, W1, b1))
        x = jax.nn.relu(_gcn_layer(x, adj, W2, b2))
        out = _gcn_layer(x, adj, W3, b3)
        return out
    x = _layernorm(x + _L0_gnn_ref(x, adj, L0_gnn_W), axis=-1)
    x = _layernorm(x + _L1_gnn_ref(x, adj, L1_gnn_kernel, L1_gnn_bias), axis=-1)
    x = _layernorm(x + _L2_gnn_ref(x, adj, L2_gnn_W1, L2_gnn_b1, L2_gnn_gamma, L2_gnn_beta, L2_gnn_W2, L2_gnn_b2), axis=-1)
    x = _layernorm(x + _L3_gnn_ref(x, adj, L3_gnn_W1, L3_gnn_b1, L3_gnn_W2, L3_gnn_b2, L3_gnn_W3, L3_gnn_b3), axis=-1)
    return x

_drawn_inputs = setup_inputs


def setup_inputs(seed=0):
    import zlib

    import numpy as np

    out = dict(_drawn_inputs(seed))
    spreads = {'L1_gnn_bias': (0.0, 0.1),
     'L2_gnn_b1': (0.0, 0.1),
     'L2_gnn_gamma': (1.0, 0.2),
     'L2_gnn_beta': (0.0, 0.283),
     'L2_gnn_b2': (0.0, 0.1),
     'L3_gnn_b1': (0.0, 0.1),
     'L3_gnn_b2': (0.0, 0.369),
     'L3_gnn_b3': (0.0, 0.635)}
    factors = {}
    for name, (base, spread) in spreads.items():
        noise = np.random.default_rng([zlib.crc32(name.encode()), seed]).standard_normal(out[name].shape)
        drawn = base * np.exp(spread * noise) if base else spread * noise
        out[name] = jnp.asarray(drawn.astype(out[name].dtype))
    for name, factor in factors.items():
        out[name] = (out[name] * factor).astype(out[name].dtype)
    return out
```

```python
from contextlib import ExitStack

import concourse.bass as bass
from concourse import mybir

ALU = mybir.AluOpType
ACT = mybir.ActivationFunctionType
F32 = mybir.dt.float32
F32R = mybir.dt.float32r

P = 128
B = 8
N = 1024
F = 256
HID = 512
NT = N // P
FC = F // P
HC = HID // P
HALF = N // 2
SLOTS = 4
HT_SLOTS = 3
WCH = 10
W_L0, W_L1, W_L2A, W_L2B, W_L3 = 0, 2, 3, 5, 7
CHUNKS = 4 + 2 * NT + 2 * NT
EPS_LN = 1e-5
EPS_DEG = 1e-6

PAIRS = range(NT // 2)
ADJ = [(h, m) for h in range(2) for m in range(NT)]
NAT = [(n, e) for n in range(NT) for e in range(2)]


class Signal:

    def __init__(self, sem, labels, before=0):
        self.sem, self.labels, self.before, self.said = sem, list(labels), before, 0

    def at(self, label, b):
        return b * len(self.labels) + (self.before + self.labels.index(label) + 1)

    def one(self, label):
        assert self.labels[self.said % len(self.labels)] == label, (label, self.labels[self.said % len(self.labels)])
        self.said += 1
        return 1


class Steps:

    def __init__(self, per_graph):
        self.per_graph, self.n = per_graph, 0

    def one(self):
        self.n += 1
        return 1

    def now(self, b):
        return b * self.per_graph + self.n


def job_labels():
    jobs = [("S0", g) for g in PAIRS]
    jobs += [("XW", 0), ("XW", 1), ("deg", 0), ("L0", 0), ("L0", 1)]
    jobs += [("XW", 2), ("XW", 3), ("deg", 1), ("L0", 2), ("L0", 3)]
    jobs += [("U", 0, 0), ("U", 0, 1), ("U", 1, 0), ("L1", 0), ("L1", 1), ("U", 1, 1), ("cnt",), ("L1", 2), ("L1", 3)]
    jobs += [("T", g) for g in PAIRS]
    jobs += [("Z", h, f) for h in range(2) for f in range(FC)]
    for s in range(NT + 3):
        if s < NT:
            jobs.append(("h", s))
        if 0 <= s - 2 < NT:
            jobs.append(("hT", s - 2))
        if 0 <= s - 3 < NT and (s - 3) % 2:
            jobs.append(("y", (s - 3) // 2))
    jobs += [("T2", g) for g in PAIRS]
    jobs += [("L2", g) for g in PAIRS]
    jobs += [("x3T", g) for g in PAIRS]
    for k in (1, 2):
        jobs += [("A%d" % k, g) for g in PAIRS]
        jobs += [("X%d" % k, h, f) for h in range(2) for f in range(FC)]
    jobs += [("A3", g) for g in PAIRS]
    jobs += [("L3", g) for g in PAIRS]
    return jobs


def split_labels():
    out = [("S0", g) for g in PAIRS]
    out += [("x1", t) for t in range(NT)]
    out += [("U", 0, 0), ("U", 0, 1), ("U", 1, 0)] + [("x2", t) for t in range(4)]
    out += [("U", 1, 1)] + [("x2", t) for t in range(4, NT)]
    out += [("T", t) for t in range(NT)]
    out += [("Z", h, f) for h in range(2) for f in range(FC)]
    out += [("hT", t) for t in range(NT)]
    out += [("T2", t) for t in range(NT)]
    out += [("x3T", g) for g in PAIRS]
    for k in (1, 2):
        out += [("A%d" % k, g) for g in PAIRS]
        out += [("X%d" % k, h, f) for h in range(2) for f in range(FC)]
    out += [("A3", g) for g in PAIRS]
    return out


def read_labels():
    out = [("deg", 0), ("L0", 0), ("L0", 1), ("L0", 2), ("L0", 3), ("deg", 1)] + [("L0", t) for t in range(4, NT)]
    out += [("L1", t) for t in range(4)] + [("L1", t) for t in range(4, NT)] + [("cnt",)]
    for s in range(NT + 3):
        if s < NT:
            out.append(("h", s))
        if 0 <= s - 3 < NT and (s - 3) % 2:
            out.append(("y", (s - 3) // 2))
    out += [("L2", t) for t in range(NT)]
    return out


NORMS = [("x1", (0, 1, 2, 3)), ("x1", (4, 5, 6, 7)), ("x2", (0, 1, 2, 3)), ("x2", (4, 5, 6, 7))]
NORMS += [("h", (t,)) for t in range(NT)]
NORMS += [("x3", (0, 1)), ("x3", (2, 3)), ("x3", (4, 5)), ("x3", (6, 7))]
NORMS += [("x4", (2 * g, 2 * g + 1)) for g in PAIRS]


def build(nc, x, xT, adj, adjT, weights, rows, cols, eye, out):
    ctx = ExitStack()
    with ctx:
        def sb(name, cols_, dt=F32):
            return ctx.enter_context(nc.sbuf_tensor(name, [P, cols_], dt))

        def sem(name):
            return ctx.enter_context(nc.semaphore(name))

        A_hi = sb("A_hi", NT * N, F32R)
        A_lo = sb("A_lo", NT * N, F32R)
        slab = sb("slab", NT * N, F32R)
        stage = sb("stage", SLOTS * HALF)
        ht = sb("ht", HT_SLOTS * HALF, F32R)
        W_hi = sb("W_hi", WCH * HALF, F32R)
        W_lo = sb("W_lo", WCH * HALF, F32R)
        P_hi = sb("P_hi", NT * F, F32R)
        P_lo = sb("P_lo", NT * F, F32R)
        Q_hi = sb("Q_hi", NT * F, F32R)
        Q_lo = sb("Q_lo", NT * F, F32R)
        xres = sb("xres", NT * F)
        colsum = sb("colsum", N)
        ytmp = sb("ytmp", 4 * F)
        eye_r = sb("eye_r", 3 * P, F32R)
        rows_sb = sb("rows_sb", 5 * F)
        betaW = sb("betaW", F)
        cols_sb = sb("cols_sb", 12)
        stats = sb("stats", 4 * 6)
        mv = sb("mv", 4 * 2)
        negm = sb("negm", 4)
        std = sb("std", 4)
        rstd = sb("rstd", 4)
        deg = sb("deg", NT)
        rdeg = sb("rdeg", NT)
        dh = sb("dh", NT)
        be = sb("be", NT)
        dn = sb("dn", NT)
        dmask = rdeg
        ones = sb("ones", 1)
        eps = sb("eps", 1)

        bank = [ctx.enter_context(nc.psum_tensor("bank%d" % i, [P, HALF], F32)) for i in range(8)]

        R_hi, R_lo, S_hi, S_lo = (slab[:, i * NT * F:(i + 1) * NT * F] for i in range(4))

        jobs = job_labels()
        place = {label: i % 8 for i, label in enumerate(jobs)}
        for i, label in enumerate(jobs[-8:]):
            place[label] = i
        order = jobs[:-8] + [None] * (-len(jobs) % 8) + jobs[-8:]
        bank_done = Signal(sem("bank_done"), jobs)
        split_ready = Signal(sem("split_ready"), split_labels())
        hi_ready = Signal(sem("hi_ready"), split_hi_labels())
        psum_read = Signal(sem("psum_read"), read_labels())
        last_read = Signal(sem("last_read"), [("L3", t) for t in range(NT)], before=1)
        xw_copied = Signal(sem("xw_copied"), PAIRS)
        relu_ready = Signal(sem("relu_ready"), [("h", t) for t in range(NT)] + [("X%d" % k, h, f) for k in (1, 2) for h in range(2) for f in range(FC)])
        var_ready = Signal(sem("var_ready"), NORMS)
        std_ready = Signal(sem("std_ready"), NORMS)
        rstd_ready = Signal(sem("rstd_ready"), NORMS)
        norm_ready = Signal(sem("norm_ready"), NORMS)
        deg_ready = Signal(sem("deg_ready"), range(2))
        sqdeg_ready = Signal(sem("sqdeg_ready"), range(2))
        dh_ready = Signal(sem("dh_ready"), range(2))
        be_ready = Signal(sem("be_ready"), range(1))
        ylo_ready = Signal(sem("ylo_ready"), PAIRS)
        biased = Signal(sem("biased"), range(NT))
        xt_hi = Signal(sem("xt_hi"), range(4))
        xt_split = Signal(sem("xt_split"), range(4))
        adj_hi = Signal(sem("adj_hi"), ADJ)
        adj_split = Signal(sem("adj_split"), ADJ)
        adj_summed = Signal(sem("adj_summed"), ADJ)
        h_made = Signal(sem("h_made"), NAT)
        h_summed = Signal(sem("h_summed"), NAT)
        ht_made = Signal(sem("ht_made"), [(k, c) for k in ("Z", "L2") for c in range(2 * NT)])
        ht_used = Signal(sem("ht_used"), [(k, c) for k in ("Z", "L2") for c in range(2 * NT) if c % NT != NT - 1])
        stage_full = [sem("stage_full%d" % i) for i in range(SLOTS)]
        w_hi_done, w_split, w_scaled = sem("w_hi_done"), sem("w_split"), sem("w_scaled")
        const_in, const_made, beta_made, beta_done = (sem(n) for n in ("const_in", "const_made", "beta_made", "beta_done"))
        x_in, w_in, stored = sem("x_in"), sem("w_in"), sem("stored")
        dve_step = sem("dve_step")

        def slot_of(j):
            return (WCH + j) % SLOTS

        def slot(i):
            return stage[:, i * HALF:(i + 1) * HALF]

        def landed(j, b):
            return b * (16 * CHUNKS // SLOTS) + 16 * ((WCH + j) // SLOTS + 1)

        def J_XT(q):
            return q

        def J_ADJ(h, m):
            return 4 + NT * h + m

        def J_NAT(n, e):
            return 4 + 2 * NT + 2 * n + e

        def reader(label):
            kind, g = label[0], label[-1]
            if kind in ("T", "T2"):
                return split_ready, (kind, 2 * g + 1)
            if kind == "XW":
                return psum_read, ("L0", 2 * g + 1)
            if kind in ("L0", "L1", "L2"):
                return psum_read, (kind, 2 * g + 1)
            if kind == "L3":
                return last_read, (kind, 2 * g + 1)
            if kind in ("deg", "cnt", "h", "y"):
                return psum_read, label
            return split_ready, label

        place = {label: i % 8 for i, label in enumerate(order) if label}

        def psum(label):
            return bank[place[label]]

        def apart(eng):
            eng.nop(nofuse=True)

        def adj_chunk(t, h, m):
            return t[:, N * m + HALF * h:N * m + HALF * (h + 1)]

        def fmajor(t, h, f):
            return t[:, 4 * F * h:4 * F * (h + 1)].rearrange("p (t f c) -> p t f c", t=4, f=FC)[:, :, f, :]

        def quad(ap):
            return ap.rearrange("p (t c) -> p t c", t=4)

        def ht_slot(c):
            return ht[:, (c % HT_SLOTS) * HALF:(c % HT_SLOTS + 1) * HALF]

        xlabels = [("X%d" % k, h, f) for k in (1, 2) for h in range(2) for f in range(FC)]

        block = ctx.enter_context(nc.Block())

        @block.sync
        def _(sp):
            sp.dma_start(cols_sb[:], cols).then_inc(const_in, 16)
            sp.dma_start(ytmp[:, 0:3 * P], eye).then_inc(const_in, 16)
            sp.dma_start(rows_sb[:], rows).then_inc(const_in, 16)
            for i in range(WCH):
                if i >= SLOTS:
                    sp.wait_ge(w_split, i - SLOTS + 1)
                sp.dma_start(slot(i % SLOTS), weights[i]).then_inc(stage_full[i % SLOTS], 16)

            def load_xT(b, first=False):
                for q in range(4):
                    if first:
                        sp.wait_ge(w_split, WCH - SLOTS + q + 1)
                    apart(sp)
                    sp.dma_start(slot(slot_of(J_XT(q))), xT[b, :, q * HALF:(q + 1) * HALF]).then_inc(stage_full[slot_of(J_XT(q))], 16)

            def load_adjT(b, h, m):
                j = J_ADJ(h, m)
                if j < 8:
                    sp.wait_ge(xt_split.sem, xt_split.at(j - 4, b))
                else:
                    before = ADJ[j - 8]
                    sp.wait_ge(adj_split.sem, adj_split.at(before, b))
                    sp.wait_ge(adj_summed.sem, adj_summed.at(before, b))
                apart(sp)
                sp.dma_start(slot(slot_of(j)), adjT[b, P * m:P * (m + 1), HALF * h:HALF * (h + 1)]).then_inc(stage_full[slot_of(j)], 16)

            def load_adj(b, n, e):
                j = J_NAT(n, e)
                if j < 4 + 2 * NT + SLOTS:
                    before = ADJ[j - 8]
                    sp.wait_ge(adj_split.sem, adj_split.at(before, b))
                    sp.wait_ge(adj_summed.sem, adj_summed.at(before, b))
                else:
                    sp.wait_ge(h_made.sem, h_made.at(NAT[j - 8 - 2 * NT], b))
                apart(sp)
                sp.dma_start(slot(slot_of(j)), adj[b, P * n:P * (n + 1), HALF * e:HALF * (e + 1)]).then_inc(stage_full[slot_of(j)], 16)

            def graph(b, last):
                for m in range(NT):
                    load_adjT(b, 1, m)
                for n, e in NAT:
                    load_adj(b, n, e)
                sp.wait_ge(psum_read.sem, psum_read.at(("cnt",), b))
                apart(sp)
                sp.dma_start(colsum[:], adj[b, 0:1, :].broadcast_to([P, N])).then_inc(w_in, 16)
                if not last:
                    sp.wait_ge(bank_done.sem, bank_done.at(("hT", NT - 1), b))
                    load_xT(b + 1)
                    for m in range(NT):
                        load_adjT(b + 1, 0, m)
                for g in PAIRS:
                    sp.wait_ge(norm_ready.sem, norm_ready.at(("x4", (2 * g, 2 * g + 1)), b))
                    apart(sp)
                    sp.dma_start(out[b, 2 * P * g:2 * P * (g + 1), :].rearrange("(t p) c -> p t c", p=P),
                                 xres[:, 2 * F * g:2 * F * (g + 1)].rearrange("p (t c) -> p t c", t=2)).then_inc(stored, 16)

                if not last:
                    sp.wait_ge(stored, (b + 1) * (16 * 4))
                    apart(sp)
                    load_x(b + 1)

            def load_x(b):
                sp.dma_start(xres[:].rearrange("p (t c) -> p t c", t=NT), x[b].rearrange("(t p) c -> p t c", p=P)).then_inc(x_in, 16)

            load_xT(0, first=True)
            for m in range(NT):
                load_adjT(0, 0, m)
            load_x(0)
            with sp.Fori(0, B - 1) as b:
                graph(b, False)
            graph(B - 1, True)
            sp.wait_ge(stored, 16 * 4 * B)

        @block.tensor
        def _(pe):
            def product(o, stat, mov, start, stop, signal=None):
                passes = [(s, v) for i, s in enumerate(stat) for k, v in enumerate(mov) if i + k < 2]
                for i, (s, v) in enumerate(passes):
                    mm = nc.tensor.matmul(o, s, v, start=(start and i == 0), stop=(stop and i == len(passes) - 1), skip_group_check=True)
                if signal:
                    mm.then_inc(signal[0].sem, signal[0].one(signal[1]))
                return mm

            def open_bank(label, b):
                i = order.index(label)
                if i >= 8:
                    before = order[i - 8]
                    if before:
                        s, what = reader(before)
                        pe.wait_ge(s.sem, s.at(what, b))

            def weight(k, c, width=F, at=0):
                a = (k + c) * HALF + at
                return W_hi[:, a:a + width], W_lo[:, a:a + width]

            def wpair(k, c):
                return weight(k, 0, F, c * F)

            def fm(x_hi, x_lo, t, f):
                a = F * t + P * f
                return x_hi[:, a:a + P], x_lo[:, a:a + P]

            def nm(x_hi, x_lo, t, at=0, width=F):
                a = F * t + at
                return x_hi[:, a:a + width], x_lo[:, a:a + width]

            def support(label, x_hi, x_lo, w, b):
                g = label[1]
                open_bank(label, b)
                for i in range(2):
                    for f in range(FC):
                        last = i == 1 and f == FC - 1
                        product(psum(label)[:, F * i:F * (i + 1)], fm(x_hi, x_lo, 2 * g + i, f), w(f), f == 0, f == FC - 1,
                                (bank_done, label) if last else None)

            def spread_T(label, s_hi, s_lo, b, split_of, identity=False):
                _, h, f = label
                open_bank(label, b)
                for m in range(NT):
                    if split_of(m):
                        pe.wait_ge(split_ready.sem, split_ready.at(split_of(m), b))
                    product(psum(label)[:], nm(s_hi, s_lo, m, P * f, P), (adj_chunk(A_hi, h, m), adj_chunk(A_lo, h, m)), m == 0, m == NT - 1 and not identity,
                            None if identity and m == NT - 1 else (bank_done, label) if m == NT - 1 else None)
                if identity:
                    for i in range(4):
                        a = P * min(i, 2)
                        w = 2 * P - (P * i - a)
                        move = eye_r[:, P - (P * i - a):P - (P * i - a) + 2 * P]
                        for k, s in enumerate(nm(s_hi, s_lo, 4 * h + i, P * f, P)):
                            mm = nc.tensor.matmul(psum(label)[:, a:a + 2 * P], s, move, start=False, stop=(i == 3 and k == 1), skip_group_check=True)
                    mm.then_inc(bank_done.sem, bank_done.one(label))

            def graph(b, last):
                for g in PAIRS:
                    pe.wait_ge(xt_split.sem, xt_split.at(g, b))
                    support(("S0", g), Q_hi, Q_lo, lambda f: weight(W_L0, f), b)
                pe.wait_ge(last_read.sem, b * NT + 1)
                for h in range(2):
                    for g in (2 * h, 2 * h + 1):
                        support(("XW", g), Q_hi, Q_lo, lambda f: weight(W_L0, f, F, F), b)
                    label = ("deg", h)
                    open_bank(label, b)
                    pe.wait_ge(adj_summed.sem, adj_summed.at((h, NT - 1), b))
                    for i in range(4):
                        a = HALF * h + P * i
                        mm = nc.tensor.matmul(psum(label)[:, i:i + 1], colsum[:, a:a + P], ones[:], start=True, stop=True)
                    mm.then_inc(bank_done.sem, bank_done.one(label))
                    for g in (2 * h, 2 * h + 1):
                        open_bank(("L0", g), b)
                    for m in range(NT):
                        if h == 0 and m % 2 == 0:
                            pe.wait_ge(split_ready.sem, split_ready.at(("S0", m // 2), b))
                        pe.wait_ge(adj_split.sem, adj_split.at((h, m), b))
                        for i in range(4):
                            label = ("L0", 2 * h + i // 2)
                            a = N * m + HALF * h + P * i
                            done = m == NT - 1 and i % 2 == 1
                            product(psum(label)[:, F * (i % 2):F * (i % 2 + 1)], (A_hi[:, a:a + P], A_lo[:, a:a + P]), nm(P_hi, P_lo, m),
                                    m == 0 and i % 2 == 0, m == NT - 1, (bank_done, label) if done else None)
                def u_source(label):
                    return lambda m: ("x1", m) if label == ("U", 0, 0) else None

                def l1(g):
                    pe.wait_ge(split_ready.sem, split_ready.at(("U", g // 2, 1), b))
                    support(("L1", g), P_hi, P_lo, lambda f: wpair(W_L1, f), b)

                for label in (("U", 0, 0), ("U", 0, 1), ("U", 1, 0)):
                    spread_T(label, Q_hi, Q_lo, b, u_source(label), identity=True)
                l1(0)
                l1(1)
                spread_T(("U", 1, 1), Q_hi, Q_lo, b, lambda m: None, identity=True)
                open_bank(("cnt",), b)
                pe.wait_ge(h_summed.sem, h_summed.at(NAT[-1], b))
                for e in range(NT):
                    mm = nc.tensor.matmul(psum(("cnt",))[:, e:e + 1], colsum[:, P * e:P * (e + 1)], ones[:], start=True, stop=True)
                mm.then_inc(bank_done.sem, bank_done.one(("cnt",)))
                l1(2)
                l1(3)

                def to_edges(kind):
                    for g in PAIRS:
                        open_bank((kind, g), b)
                    for n in range(NT):
                        if kind == "T":
                            pe.wait_ge(h_made.sem, h_made.at((n, 1), b))
                            pe.wait_ge(split_ready.sem, split_ready.at(("x2", n), b))
                        elif n % 2 == 0:
                            pe.wait_ge(ylo_ready.sem, ylo_ready.at(n // 2, b))
                        for e in range(NT):
                            label = (kind, e // 2)
                            done = n == NT - 1 and e % 2 == 1
                            product(psum(label)[:, F * (e % 2):F * (e % 2 + 1)], (slab[:, N * n + P * e:N * n + P * (e + 1)],), nm(P_hi, P_lo, n),
                                    n == 0 and e % 2 == 0, n == NT - 1, (bank_done, label) if done else None)

                to_edges("T")
                for h in range(2):
                    for f in range(FC):
                        open_bank(("Z", h, f), b)
                    for e in range(NT):
                        c = NT * h + e
                        if h == 0:
                            pe.wait_ge(split_ready.sem, split_ready.at(("T", e), b))
                        pe.wait_ge(ht_made.sem, ht_made.at(("Z", c), b))
                        for f in range(FC):
                            mine = (bank_done, ("Z", h, f)) if e == NT - 1 else (ht_used, ("Z", c)) if f == FC - 1 else None
                            st = nm(Q_hi, Q_lo, e, P * f, P)
                            for k in range(2):
                                mm = nc.tensor.matmul(psum(("Z", h, f))[:], st[k], ht_slot(c), start=(e == 0 and k == 0), stop=(e == NT - 1 and k == 1), skip_group_check=True)
                            if mine:
                                mm.then_inc(mine[0].sem, mine[0].one(mine[1]))
                for s in range(NT + 3):
                    if s < NT:
                        label = ("h", s)
                        open_bank(label, b)
                        if s % 4 == 0:
                            pe.wait_ge(split_ready.sem, split_ready.at(("Z", s // 4, 1), b))
                        for f in range(FC):
                            product(psum(label)[:], fm(P_hi, P_lo, s, f), weight(W_L2A, f, HID), f == 0, f == FC - 1, (bank_done, label) if f == FC - 1 else None)
                    t = s - 2
                    if 0 <= t < NT:
                        label = ("hT", t)
                        open_bank(label, b)
                        pe.wait_ge(norm_ready.sem, norm_ready.at(("h", (t,)), b))
                        for j in range(HC):
                            mm = nc.tensor.transpose(psum(label)[:, P * j:P * (j + 1)], slot(t % SLOTS)[:, P * j:P * (j + 1)], eye_r[:, P:2 * P].bitcast(F32))
                        mm.then_inc(bank_done.sem, bank_done.one(label))
                    t = s - 3
                    if 0 <= t < NT:
                        label = ("y", t // 2)
                        if t % 2 == 0:
                            open_bank(label, b)
                        pe.wait_ge(split_ready.sem, split_ready.at(("hT", t), b))
                        for j in range(HC):
                            a = HALF * (t % SLOTS) + P * j
                            product(psum(label)[:, F * (t % 2):F * (t % 2 + 1)], (Q_hi[:, a:a + P], Q_lo[:, a:a + P]), wpair(W_L2B + j // 2, j % 2),
                                    j == 0, j == HC - 1, (bank_done, label) if t % 2 and j == HC - 1 else None)
                to_edges("T2")
                for h in range(2):
                    for g in (2 * h, 2 * h + 1):
                        open_bank(("L2", g), b)
                    for e in range(NT):
                        c = NT * h + e
                        if h == 0:
                            pe.wait_ge(split_ready.sem, split_ready.at(("T2", e), b))
                        pe.wait_ge(ht_made.sem, ht_made.at(("L2", c), b))
                        for i in range(4):
                            label = ("L2", 2 * h + i // 2)
                            mine = (bank_done, label) if e == NT - 1 and i % 2 else (ht_used, ("L2", c)) if i == 3 else None
                            product(psum(label)[:, F * (i % 2):F * (i % 2 + 1)], (ht_slot(c)[:, P * i:P * (i + 1)],), nm(Q_hi, Q_lo, e),
                                    e == 0 and i % 2 == 0, e == NT - 1, mine)

                for g in PAIRS:
                    label = ("x3T", g)
                    open_bank(label, b)
                    pe.wait_ge(norm_ready.sem, norm_ready.at(("x3", (2 * g, 2 * g + 1)), b))
                    for i in range(2):
                        for f in range(FC):
                            a = F * (2 * g + i) + P * f
                            mm = nc.tensor.transpose(psum(label)[:, F * i + P * f:F * i + P * (f + 1)], xres[:, a:a + P], eye_r[:, P:2 * P].bitcast(F32))
                    mm.then_inc(bank_done.sem, bank_done.one(label))
                for k in (1, 2, 3):
                    for g in PAIRS:
                        source = ("x3T", g) if k == 1 else ("X%d" % (k - 1), g // 2, 1)
                        pe.wait_ge(split_ready.sem, split_ready.at(source, b))
                        support(("A%d" % k, g), R_hi, R_lo, lambda f: wpair(W_L3 + k - 1, f), b)
                    if k < 3:
                        for h in range(2):
                            for f in range(FC):
                                label = ("X%d" % k, h, f)
                                spread_T(label, S_hi, S_lo, b, lambda m: ("A%d" % k, m // 2) if (h, f) == (0, 0) and m % 2 == 0 else None)
                for g in PAIRS:
                    label = ("L3", g)
                    open_bank(label, b)
                    for i in range(2):
                        for m in range(NT):
                            if g == 0 and i == 0 and m % 2 == 0:
                                pe.wait_ge(split_ready.sem, split_ready.at(("A3", m // 2), b))
                            a = N * m + P * (2 * g + i)
                            product(psum(label)[:, F * i:F * (i + 1)], (A_hi[:, a:a + P], A_lo[:, a:a + P]), nm(S_hi, S_lo, m), m == 0, m == NT - 1,
                                    (bank_done, label) if i == 1 and m == NT - 1 else None)

            for i in range(2):
                pe.wait_ge(stage_full[(W_L2B + i) % SLOTS], 16 * ((W_L2B + i) // SLOTS + 1))
                if i == 0:
                    pe.wait_ge(beta_made, HC)
                for j in range(2):
                    mm = nc.tensor.matmul(bank[0][:, 0:F], ytmp[:, P * (2 * i + j):P * (2 * i + j + 1)], slot((W_L2B + i) % SLOTS)[:, F * j:F * (j + 1)],
                                          start=(i == 0 and j == 0), stop=(i == 1 and j == 1))
                mm.then_inc(beta_done, 1)
            pe.wait_ge(last_read.sem, 1)
            pe.wait_ge(w_split, WCH)
            with pe.Fori(0, B - 1) as b:
                graph(b, False)
            graph(B - 1, True)

        @block.scalar
        def _(act):
            def hi(label, dst, src, b, scale=1.0):
                nc.scalar.activation(dst, src, ACT.Identity if not isinstance(scale, float) else ACT.Copy, scale=scale).then_inc(hi_ready.sem, hi_ready.one(label))

            def hi_job(label, dst, b):
                act.wait_ge(bank_done.sem, bank_done.at(label, b))
                hi(label, dst, psum(label)[:] if len(label) == 2 else quad(psum(label)[:]), b)

            def refill(b, h, m):
                act.wait_ge(stage_full[slot_of(J_ADJ(h, m))], landed(J_ADJ(h, m), b))
                nc.scalar.copy(adj_chunk(A_hi, h, m), slot(slot_of(J_ADJ(h, m)))).then_inc(adj_hi.sem, adj_hi.one((h, m)))

            def split_xT(b, q):
                act.wait_ge(stage_full[slot_of(J_XT(q))], landed(J_XT(q), b))
                nc.scalar.copy(Q_hi[:, q * HALF:(q + 1) * HALF], slot(slot_of(J_XT(q)))).then_inc(xt_hi.sem, xt_hi.one(q))

            def root(norm, b):
                act.wait_ge(var_ready.sem, var_ready.at(norm, b))
                i = stat_slot(norm)
                v = mv[:, 2 * i:2 * (i + len(norm[1]))].rearrange("p (t k) -> p t k", k=2)[:, :, 1]
                nc.scalar.activation(std[:, i:i + len(norm[1])], v, ACT.Sqrt, bias=eps[:]).then_inc(std_ready.sem, std_ready.one(norm))

            def graph(b, last):
                for g in PAIRS:
                    hi_job(("S0", g), P_hi[:, 2 * F * g:2 * F * (g + 1)], b)
                    refill(b, 1, g)
                for h in range(2):
                    for g in (2 * h, 2 * h + 1):
                        if h == 0:
                            refill(b, 1, 4 + 2 * g)
                            refill(b, 1, 5 + 2 * g)
                        act.wait_ge(bank_done.sem, bank_done.at(("XW", g), b))
                        if h == 1 and g == 2:
                            act.wait_ge(norm_ready.sem, norm_ready.at(NORMS[0], b))
                        nc.scalar.copy(ytmp[:, 2 * F * (g % 2):2 * F * (g % 2 + 1)], psum(("XW", g))[:]).then_inc(xw_copied.sem, xw_copied.one(g))
                    act.wait_ge(deg_ready.sem, deg_ready.at(h, b))
                    nc.scalar.activation(dh[:, 4 * h:4 * h + 4], deg[:, 4 * h:4 * h + 4], ACT.Sqrt, bias=ones[:]).then_inc(sqdeg_ready.sem, sqdeg_ready.one(h))
                    root(NORMS[h], b)
                    act.wait_ge(dh_ready.sem, dh_ready.at(h, b))
                    act.wait_ge(norm_ready.sem, norm_ready.at(NORMS[h], b))
                    for t in range(4 * h, 4 * h + 4):
                        hi(("x1", t), Q_hi[:, F * t:F * (t + 1)], xres[:, F * t:F * (t + 1)], b, dh[:, t:t + 1])

                def x2(h):
                    root(NORMS[2 + h], b)
                    act.wait_ge(norm_ready.sem, norm_ready.at(NORMS[2 + h], b))
                    for t in range(4 * h, 4 * h + 4):
                        hi(("x2", t), P_hi[:, F * t:F * (t + 1)], xres[:, F * t:F * (t + 1)], b)

                for label in (("U", 0, 0), ("U", 0, 1), ("U", 1, 0)):
                    hi_job(label, fmajor(P_hi, label[1], label[2]), b)
                x2(0)
                hi_job(("U", 1, 1), fmajor(P_hi, 1, 1), b)
                x2(1)

                def edges(kind):
                    for e in range(NT):
                        if kind == "T" and e == 0:
                            act.wait_ge(be_ready.sem, be_ready.at(0, b))
                        act.wait_ge(bank_done.sem, bank_done.at((kind, e // 2), b))
                        hi((kind, e), Q_hi[:, F * e:F * (e + 1)], psum((kind, e // 2))[:, F * (e % 2):F * (e % 2 + 1)], b, be[:, e:e + 1])

                edges("T")
                for h in range(2):
                    for f in range(FC):
                        hi_job(("Z", h, f), fmajor(P_hi, h, f), b)
                for s in range(NT + 4):
                    if s < NT:
                        act.wait_ge(psum_read.sem, psum_read.at(("h", s), b))
                        nc.scalar.activation(slot(s % SLOTS), slot(s % SLOTS), ACT.Relu).then_inc(relu_ready.sem, relu_ready.one(("h", s)))
                    if 0 <= s - 2 < NT:
                        hi_job(("hT", s - 2), Q_hi[:, HALF * ((s - 2) % SLOTS):HALF * ((s - 2) % SLOTS + 1)], b)
                    if s < NT:
                        root(("h", (s,)), b)
                    if 0 <= s - 4 < NT and s % 2:
                        g = (s - 4) // 2
                        act.wait_ge(psum_read.sem, psum_read.at(("y", g), b))
                        hi(("y", g), P_hi[:, 2 * F * g:2 * F * (g + 1)], ytmp[:, 2 * F * (g % 2):2 * F * (g % 2 + 1)], b)
                edges("T2")
                for g in PAIRS:
                    root(("x3", (2 * g, 2 * g + 1)), b)
                    hi_job(("x3T", g), R_hi[:, 2 * F * g:2 * F * (g + 1)], b)
                i = 0
                for k in (1, 2, 3):
                    for g in PAIRS:
                        hi_job(("A%d" % k, g), S_hi[:, 2 * F * g:2 * F * (g + 1)], b)
                    if k == 2 and not last:
                        for q in range(4):
                            split_xT(b + 1, q)
                    if k < 3:
                        for h in range(2):
                            for f in range(FC):
                                label = ("X%d" % k, h, f)
                                y = ytmp[:, 2 * F * (i % 2):2 * F * (i % 2 + 1)]
                                act.wait_ge(bank_done.sem, bank_done.at(label, b))
                                if i >= 2:
                                    act.wait_ge(split_ready.sem, split_ready.at(xlabels[i - 2], b))
                                bias = cols_sb[:, 8 + 2 * (k - 1) + f:9 + 2 * (k - 1) + f]
                                nc.scalar.activation(y, psum(label)[:], ACT.Relu, bias=bias).then_inc(relu_ready.sem, relu_ready.one(label))
                                nc.scalar.activation(fmajor(R_hi, h, f), quad(psum(label)[:]), ACT.Relu, bias=bias).then_inc(hi_ready.sem, hi_ready.one(label))
                                i += 1
                for g in PAIRS:
                    if g >= 2 and not last:
                        if g == 2:
                            act.wait_ge(bank_done.sem, bank_done.at(("L3", 1), b))
                        for m in range(4 * (g - 2), 4 * (g - 1)):
                            refill(b + 1, 0, m)
                    root(("x4", (2 * g, 2 * g + 1)), b)

            for i in range(WCH):
                if i in (W_L2B, W_L2B + 1):
                    act.wait_ge(w_scaled, 2 * (i - W_L2B + 1))
                act.wait_ge(stage_full[i % SLOTS], 16 * (i // SLOTS + 1))
                nc.scalar.copy(W_hi[:, i * HALF:(i + 1) * HALF], slot(i % SLOTS)).then_inc(w_hi_done, 1)
            act.wait_ge(const_made, 3)
            for q in range(4):
                split_xT(0, q)
            for m in range(NT):
                refill(0, 0, m)
            with act.Fori(0, B - 1) as b:
                graph(b, False)
            graph(B - 1, True)

        @block.vector
        def _(dve):
            steps = Steps(DVE_STEPS)

            def link(ins, b):
                ins.then_inc(dve_step, steps.one())
                dve.wait_ge(dve_step, steps.now(b))

            def lo(label, hi_part, lo_part, src, b, scale=None, signal=None):
                dve.wait_ge(hi_ready.sem, hi_ready.at(label, b))
                if scale is None:
                    ins = nc.vector.tensor_tensor(lo_part, src, hi_part.bitcast(F32), ALU.subtract)
                else:
                    ins = nc.vector.scalar_tensor_tensor(out=lo_part, in0=src, scalar=scale, in1=hi_part.bitcast(F32), op0=ALU.mult, op1=ALU.subtract)
                ins.then_inc(split_ready.sem, split_ready.one(label))

            def lo_job(label, h_, l_, b):
                lo(label, h_, l_, psum(label)[:] if len(label) == 2 else quad(psum(label)[:]), b)

            def refill(b, h, m):
                dve.wait_ge(adj_hi.sem, adj_hi.at((h, m), b))
                nc.vector.tensor_tensor(adj_chunk(A_lo, h, m), slot(slot_of(J_ADJ(h, m))), adj_chunk(A_hi, h, m).bitcast(F32), ALU.subtract)\
                    .then_inc(adj_split.sem, adj_split.one((h, m)))

            def split_xT(b, q):
                dve.wait_ge(xt_hi.sem, xt_hi.at(q, b))
                c = slice(q * HALF, (q + 1) * HALF)
                nc.vector.tensor_tensor(Q_lo[:, c], slot(slot_of(J_XT(q))), Q_hi[:, c].bitcast(F32), ALU.subtract).then_inc(xt_split.sem, xt_split.one(q))

            def make_h(b, n, e):
                dve.wait_ge(stage_full[slot_of(J_NAT(n, e))], landed(J_NAT(n, e), b))
                nc.vector.tensor_scalar(slab[:, N * n + HALF * e:N * n + HALF * (e + 1)], slot(slot_of(J_NAT(n, e))), 0.0, None, ALU.not_equal)\
                    .then_inc(h_made.sem, h_made.one((n, e)))

            def make_ht(b, kind, c):
                if c >= HT_SLOTS:
                    d = c - HT_SLOTS
                    if d % NT == NT - 1:
                        dve.wait_ge(bank_done.sem, bank_done.at(("Z", d // NT, 1) if kind == "Z" else ("L2", 2 * (d // NT) + 1), b))
                    else:
                        dve.wait_ge(ht_used.sem, ht_used.at((kind, d), b))
                elif kind == "L2" and c == 0:
                    dve.wait_ge(bank_done.sem, bank_done.at(("Z", 1, 1), b))
                nc.vector.tensor_scalar(ht_slot(c), adj_chunk(A_hi, c // NT, c % NT).bitcast(F32), 0.0, None, ALU.not_equal)\
                    .then_inc(ht_made.sem, ht_made.one((kind, c)))

            def statistics(norm, srcs, b):
                i = stat_slot(norm)
                n = len(norm[1])
                for k, src in enumerate(srcs):
                    ins = nc.vector.bn_stats(stats[:, 6 * (i + k):6 * (i + k + 1)], src)
                    if k == n - 1:
                        ins.then_inc(dve_step, steps.one())
                        dve.wait_ge(dve_step, steps.now(b))
                        apart(dve)
                for k in range(n):
                    ins = nc.vector.bn_aggr(mv[:, 2 * (i + k):2 * (i + k + 1)], stats[:, 6 * (i + k):6 * (i + k + 1)])
                ins.then_inc(var_ready.sem, var_ready.one(norm))
                dve.wait_ge(var_ready.sem, var_ready.at(norm, b))
                m = mv[:, 2 * i:2 * (i + n)].rearrange("p (t k) -> p t k", k=2)[:, :, 0]
                nc.vector.tensor_scalar(negm[:, i:i + n], m, -1.0, None, ALU.mult)

            def invert(norm, b):
                dve.wait_ge(std_ready.sem, std_ready.at(norm, b))
                i = stat_slot(norm)
                n = len(norm[1])
                nc.vector.reciprocal(rstd[:, i:i + n], std[:, i:i + n]).then_inc(rstd_ready.sem, rstd_ready.one(norm))

            def tile_(t, i):
                return t[:, F * i:F * (i + 1)]

            def degrees(h, b):
                label = ("deg", h)
                c = slice(4 * h, 4 * h + 4)
                dve.wait_ge(bank_done.sem, bank_done.at(label, b))
                nc.vector.tensor_copy(deg[:, c], psum(label)[:, 0:4]).then_inc(psum_read.sem, psum_read.one(label))
                dve.wait_ge(psum_read.sem, psum_read.at(label, b))
                link(nc.vector.tensor_scalar(rdeg[:, c], deg[:, c], EPS_DEG, None, ALU.max), b)
                nc.vector.reciprocal(rdeg[:, c], rdeg[:, c]).then_inc(deg_ready.sem, deg_ready.one(h))
                dve.wait_ge(sqdeg_ready.sem, sqdeg_ready.at(h, b))
                dve.wait_ge(deg_ready.sem, deg_ready.at(h, b))
                nc.vector.reciprocal(dh[:, c], dh[:, c]).then_inc(dh_ready.sem, dh_ready.one(h))

            def graph(b, last):
                steps.n = 0
                for g in PAIRS:
                    c = slice(2 * F * g, 2 * F * (g + 1))
                    lo_job(("S0", g), P_hi[:, c], P_lo[:, c], b)
                    refill(b, 1, g)
                for m in range(4, NT):
                    refill(b, 1, m)
                for h in range(2):
                    degrees(h, b)
                    for g in (2 * h, 2 * h + 1):
                        dve.wait_ge(bank_done.sem, bank_done.at(("L0", g), b))
                        dve.wait_ge(xw_copied.sem, xw_copied.at(g, b))
                        for i in range(2):
                            t = 2 * g + i
                            y = tile_(ytmp, t % 4)
                            nc.vector.scalar_tensor_tensor(out=y, in0=psum(("L0", g))[:, F * i:F * (i + 1)], scalar=rdeg[:, t:t + 1], in1=y, op0=ALU.mult, op1=ALU.add)\
                                .then_inc(psum_read.sem, psum_read.one(("L0", t)))
                    dve.wait_ge(x_in, b * 16 + 16)
                    dve.wait_ge(psum_read.sem, psum_read.at(("L0", 4 * h + 3), b))
                    link(nc.vector.scalar_tensor_tensor(out=ytmp[:], in0=ytmp[:], scalar=0.0, in1=xres[:, 4 * F * h:4 * F * (h + 1)], op0=ALU.max, op1=ALU.add), b)
                    statistics(NORMS[h], [tile_(ytmp, i) for i in range(4)], b)
                    invert(NORMS[h], b)
                    for t in range(4 * h, 4 * h + 4):
                        lo(("x1", t), tile_(Q_hi, t), tile_(Q_lo, t), tile_(xres, t), b, dh[:, t:t + 1])

                def x2(h):
                    for t in range(4 * h, 4 * h + 4):
                        if t % 2 == 0:
                            dve.wait_ge(bank_done.sem, bank_done.at(("L1", t // 2), b))
                        nc.vector.scalar_tensor_tensor(out=tile_(ytmp, t % 4), in0=psum(("L1", t // 2))[:, F * (t % 2):F * (t % 2 + 1)], scalar=dh[:, t:t + 1],
                                                       in1=rows_sb[:, 0:F], op0=ALU.mult, op1=ALU.add).then_inc(psum_read.sem, psum_read.one(("L1", t)))
                    dve.wait_ge(psum_read.sem, psum_read.at(("L1", 4 * h + 3), b))
                    link(nc.vector.scalar_tensor_tensor(out=ytmp[:], in0=ytmp[:], scalar=0.0, in1=xres[:, 4 * F * h:4 * F * (h + 1)], op0=ALU.max, op1=ALU.add), b)
                    statistics(NORMS[2 + h], [tile_(ytmp, i) for i in range(4)], b)
                    invert(NORMS[2 + h], b)
                    for t in range(4 * h, 4 * h + 4):
                        lo(("x2", t), tile_(P_hi, t), tile_(P_lo, t), tile_(xres, t), b)

                for k, label in enumerate((("U", 0, 0), ("U", 0, 1), ("U", 1, 0))):
                    for n, e in NAT[6 * k:6 * k + 6]:
                        make_h(b, n, e)
                    lo_job(label, fmajor(P_hi, label[1], label[2]), fmajor(P_lo, label[1], label[2]), b)
                x2(0)
                lo_job(("U", 1, 1), fmajor(P_hi, 1, 1), fmajor(P_lo, 1, 1), b)
                x2(1)

                dve.wait_ge(bank_done.sem, bank_done.at(("cnt",), b))
                nc.vector.tensor_scalar(be[:], psum(("cnt",))[:, 0:NT], 1.0, None, ALU.max).then_inc(psum_read.sem, psum_read.one(("cnt",)))
                dve.wait_ge(psum_read.sem, psum_read.at(("cnt",), b))
                nc.vector.reciprocal(be[:], be[:]).then_inc(be_ready.sem, be_ready.one(0))
                dve.wait_ge(w_in, b * 16 + 16)
                dve.wait_ge(norm_ready.sem, norm_ready.at(NORMS[3], b))
                for n in range(NT):
                    link(nc.vector.tensor_tensor_reduce(ytmp[:], slab[:, N * n:N * (n + 1)].bitcast(F32), colsum[:], 1.0, 0.0, ALU.mult, ALU.add, dn[:, n:n + 1]), b)
                link(nc.vector.tensor_scalar(dmask[:], dn[:], 0.0, None, ALU.is_gt), b)
                link(nc.vector.tensor_tensor(dn[:], dn[:], dmask[:], ALU.mult), b)
                link(nc.vector.scalar_tensor_tensor(out=dn[:], in0=dn[:], scalar=1.0, in1=dmask[:], op0=ALU.add, op1=ALU.subtract), b)
                link(nc.vector.reciprocal(dn[:], dn[:]), b)
                link(nc.vector.tensor_tensor(dn[:], dn[:], dmask[:], ALU.mult), b)

                def edges(kind):
                    dve.wait_ge(be_ready.sem, be_ready.at(0, b))
                    for e in range(NT):
                        if e % 2 == 0:
                            dve.wait_ge(hi_ready.sem, hi_ready.at((kind, e + 1), b))
                        lo((kind, e), tile_(Q_hi, e), tile_(Q_lo, e), psum((kind, e // 2))[:, F * (e % 2):F * (e % 2 + 1)], b, be[:, e:e + 1])

                for c in range(HT_SLOTS):
                    make_ht(b, "Z", c)
                edges("T")
                for h in range(2):
                    for c in range(max(HT_SLOTS, NT * h), NT * (h + 1)):
                        make_ht(b, "Z", c)
                    for f in range(FC):
                        lo_job(("Z", h, f), fmajor(P_hi, h, f), fmajor(P_lo, h, f), b)
                for s in range(NT + 3):
                    if s < NT:
                        dve.wait_ge(bank_done.sem, bank_done.at(("h", s), b))
                        if s >= SLOTS:
                            dve.wait_ge(bank_done.sem, bank_done.at(("hT", s - SLOTS), b))
                        nc.vector.scalar_tensor_tensor(out=slot(s % SLOTS), in0=psum(("h", s))[:], scalar=dn[:, s:s + 1], in1=rows_sb[:, F:F + HID], op0=ALU.mult, op1=ALU.add)\
                            .then_inc(psum_read.sem, psum_read.one(("h", s)))
                    if 0 <= s - 2 < NT:
                        c = slice(HALF * ((s - 2) % SLOTS), HALF * ((s - 2) % SLOTS + 1))
                        lo_job(("hT", s - 2), Q_hi[:, c], Q_lo[:, c], b)
                    if s < NT:
                        dve.wait_ge(relu_ready.sem, relu_ready.at(("h", s), b))
                        statistics(("h", (s,)), [slot(s % SLOTS)], b)
                    if 0 <= s - 3 < NT and (s - 3) % 2:
                        g = (s - 3) // 2
                        dve.wait_ge(bank_done.sem, bank_done.at(("y", g), b))
                        if g >= 2:
                            dve.wait_ge(ylo_ready.sem, ylo_ready.at(g - 2, b))
                        nc.vector.tensor_tensor(ytmp[:, 2 * F * (g % 2):2 * F * (g % 2 + 1)].rearrange("p (t c) -> p t c", t=2), psum(("y", g))[:].rearrange("p (t c) -> p t c", t=2),
                                                betaW[:].unsqueeze(1).to_broadcast([P, 2, F]), ALU.add).then_inc(psum_read.sem, psum_read.one(("y", g)))
                    if s < NT:
                        invert(("h", (s,)), b)
                for c in range(HT_SLOTS):
                    make_ht(b, "L2", c)
                edges("T2")

                def x3(g):
                    norm = ("x3", (2 * g, 2 * g + 1))
                    dve.wait_ge(bank_done.sem, bank_done.at(("L2", g), b))
                    if g >= 2:
                        dve.wait_ge(norm_ready.sem, norm_ready.at(("x3", (2 * g - 4, 2 * g - 3)), b))
                    for t in norm[1]:
                        nc.vector.scalar_tensor_tensor(out=tile_(ytmp, t % 4), in0=psum(("L2", g))[:, F * (t % 2):F * (t % 2 + 1)], scalar=dn[:, t:t + 1],
                                                       in1=rows_sb[:, 3 * F:4 * F], op0=ALU.mult, op1=ALU.add).then_inc(psum_read.sem, psum_read.one(("L2", t)))
                    dve.wait_ge(psum_read.sem, psum_read.at(("L2", 2 * g + 1), b))
                    y = ytmp[:, 2 * F * (g % 2):2 * F * (g % 2 + 1)]
                    link(nc.vector.scalar_tensor_tensor(out=y, in0=xres[:, 2 * F * g:2 * F * (g + 1)], scalar=2.0, in1=y, op0=ALU.mult, op1=ALU.add), b)
                    statistics(norm, [tile_(ytmp, t % 4) for t in norm[1]], b)
                    invert(norm, b)

                for c in range(HT_SLOTS, NT):
                    make_ht(b, "L2", c)
                for c in range(NT, NT + 3):
                    make_ht(b, "L2", c)
                dve.wait_ge(ylo_ready.sem, ylo_ready.at(3, b))
                x3(0)
                for c in range(NT + 3, 2 * NT):
                    make_ht(b, "L2", c)
                x3(1)
                x3(2)
                x3(3)
                for g in PAIRS:
                    c = slice(2 * F * g, 2 * F * (g + 1))
                    lo_job(("x3T", g), R_hi[:, c], R_lo[:, c], b)
                i = 0
                for k in (1, 2, 3):
                    for g in PAIRS:
                        c = slice(2 * F * g, 2 * F * (g + 1))
                        lo_job(("A%d" % k, g), S_hi[:, c], S_lo[:, c], b)
                    if k == 2 and not last:
                        for q in range(4):
                            split_xT(b + 1, q)
                    if k < 3:
                        for h in range(2):
                            for f in range(FC):
                                label = ("X%d" % k, h, f)
                                dve.wait_ge(relu_ready.sem, relu_ready.at(label, b))
                                lo(label, fmajor(R_hi, h, f), fmajor(R_lo, h, f), quad(ytmp[:, 2 * F * (i % 2):2 * F * (i % 2 + 1)]), b)
                                i += 1
                for g in PAIRS:
                    norm = ("x4", (2 * g, 2 * g + 1))
                    if g >= 2 and not last:
                        for m in range(4 * (g - 2), 4 * (g - 1)):
                            refill(b + 1, 0, m)
                    dve.wait_ge(bank_done.sem, bank_done.at(("L3", g), b))
                    dve.wait_ge(biased.sem, biased.at(2 * g + 1, b))
                    if g >= 2:
                        dve.wait_ge(norm_ready.sem, norm_ready.at(("x4", (2 * g - 4, 2 * g - 3)), b))
                    for t in norm[1]:
                        nc.vector.tensor_tensor(tile_(ytmp, t % 4), psum(("L3", g))[:, F * (t % 2):F * (t % 2 + 1)], tile_(xres, t), ALU.add)\
                            .then_inc(last_read.sem, last_read.one(("L3", t)))
                    dve.wait_ge(last_read.sem, last_read.at(("L3", 2 * g + 1), b))
                    statistics(norm, [tile_(ytmp, t % 4) for t in norm[1]], b)
                    invert(norm, b)
                dve.wait_ge(norm_ready.sem, norm_ready.at(("x4", (6, 7)), b))
                assert steps.n == DVE_STEPS, steps.n

            dve.wait_ge(const_in, 48)
            nc.vector.tensor_copy(eye_r[:], ytmp[:, 0:3 * P]).then_inc(const_made, 1)
            nc.vector.memset(ones[:], 1.0).then_inc(const_made, 1)
            nc.vector.memset(eps[:], EPS_LN).then_inc(const_made, 1)
            dve.wait_ge(const_made, 3)
            for j in range(HC):
                nc.vector.tensor_scalar(ytmp[:, P * j:P * (j + 1)], cols_sb[:, 4 + j:5 + j].to_broadcast([P, P]), 1.0, None, ALU.mult).then_inc(beta_made, 1)
            for i in range(WCH):
                s = slot(i % SLOTS)
                if i in (W_L2B, W_L2B + 1):
                    dve.wait_ge(beta_done, i - W_L2B + 1)
                    for j in range(2):
                        g = 2 * (i - W_L2B) + j
                        nc.vector.tensor_scalar(s[:, F * j:F * (j + 1)], s[:, F * j:F * (j + 1)], cols_sb[:, g:g + 1], None, ALU.mult).then_inc(w_scaled, 1)
                dve.wait_ge(w_hi_done, i + 1)
                c = slice(i * HALF, (i + 1) * HALF)
                nc.vector.tensor_tensor(W_lo[:, c], s, W_hi[:, c].bitcast(F32), ALU.subtract).then_inc(w_split, 1)
            nc.vector.tensor_copy(betaW[:], bank[0][:, 0:F]).then_inc(last_read.sem, 1)
            for q in range(4):
                split_xT(0, q)
            for m in range(NT):
                refill(0, 0, m)
            with dve.Fori(0, B - 1) as b:
                graph(b, False)
            graph(B - 1, True)

        @block.gpsimd
        def _(pool):
            def sum_adj(b, h, m):
                pool.wait_ge(stage_full[slot_of(J_ADJ(h, m))], landed(J_ADJ(h, m), b))
                s = slot(slot_of(J_ADJ(h, m)))
                acc = colsum[:, HALF * h:HALF * (h + 1)]
                if m == 0:
                    apart(pool)
                    ins = nc.gpsimd.tensor_scalar(acc, s, 1.0, 0.0, ALU.mult, ALU.add)
                else:
                    pool.wait_ge(adj_summed.sem, adj_summed.at((h, m - 1), b))
                    ins = nc.gpsimd.tensor_tensor(acc, acc, s, ALU.add)
                ins.then_inc(adj_summed.sem, adj_summed.one((h, m)))

            def apply(norm, srcs, dsts, b):
                pool.wait_ge(rstd_ready.sem, rstd_ready.at(norm, b))
                apart(pool)
                i = stat_slot(norm)
                for k, (s, d) in enumerate(zip(srcs, dsts)):
                    ins = nc.gpsimd.tensor_scalar(d, s, negm[:, i + k:i + k + 1], rstd[:, i + k:i + k + 1], ALU.add, ALU.mult)
                ins.then_inc(norm_ready.sem, norm_ready.one(norm))

            def apply_tiles(norm, b):
                apply(norm, [ytmp[:, F * (t % 4):F * (t % 4 + 1)] for t in norm[1]], [xres[:, F * t:F * (t + 1)] for t in norm[1]], b)

            def graph(b, last):
                for m in range(NT):
                    sum_adj(b, 1, m)
                apply_tiles(NORMS[0], b)
                apply_tiles(NORMS[1], b)
                pool.wait_ge(bank_done.sem, bank_done.at(("deg", 1), b))
                for n, e in NAT:
                    pool.wait_ge(h_made.sem, h_made.at((n, e), b))
                    acc = colsum[:, HALF * e:HALF * (e + 1)]
                    src = slab[:, N * n + HALF * e:N * n + HALF * (e + 1)].bitcast(F32)
                    if n == 0:
                        apart(pool)
                        ins = nc.gpsimd.tensor_scalar(acc, src, 1.0, 0.0, ALU.mult, ALU.add)
                    else:
                        pool.wait_ge(h_summed.sem, h_summed.at((n - 1, e), b))
                        ins = nc.gpsimd.tensor_tensor(acc, acc, src, ALU.add)
                    ins.then_inc(h_summed.sem, h_summed.one((n, e)))
                apply_tiles(NORMS[2], b)
                apply_tiles(NORMS[3], b)
                for s in range(NT + 4):
                    if s < NT:
                        apply(("h", (s,)), [slot(s % SLOTS)], [slot(s % SLOTS)], b)
                    if 0 <= s - 4 < NT and s % 2:
                        g = (s - 4) // 2
                        pool.wait_ge(hi_ready.sem, hi_ready.at(("y", g), b))
                        c = slice(2 * F * g, 2 * F * (g + 1))
                        nc.gpsimd.tensor_tensor(P_lo[:, c], ytmp[:, 2 * F * (g % 2):2 * F * (g % 2 + 1)], P_hi[:, c].bitcast(F32), ALU.subtract)\
                            .then_inc(ylo_ready.sem, ylo_ready.one(g))
                for g in PAIRS:
                    apply_tiles(("x3", (2 * g, 2 * g + 1)), b)
                for t in range(NT):
                    if t % 2 == 0:
                        pool.wait_ge(bank_done.sem, bank_done.at(("x3T", t // 2), b))
                    pool.wait_ge(norm_ready.sem, norm_ready.at(("x3", (6, 7)), b))
                    c = slice(F * t, F * (t + 1))
                    nc.gpsimd.tensor_tensor(xres[:, c], xres[:, c], rows_sb[:, 4 * F:5 * F], ALU.add).then_inc(biased.sem, biased.one(t))
                for g in PAIRS:
                    if g >= 2 and not last:
                        for m in range(4 * (g - 2), 4 * (g - 1)):
                            sum_adj(b + 1, 0, m)
                    apply_tiles(("x4", (2 * g, 2 * g + 1)), b)

            for m in range(NT):
                sum_adj(0, 0, m)
            with pool.Fori(0, B - 1) as b:
                graph(b, False)
            graph(B - 1, True)


DVE_STEPS = 43


def split_hi_labels():
    out = []
    for label in split_labels():
        out.append(label)
    at = out.index(("hT", 0))
    out = [x for x in out if x[0] != "hT"]
    seq = []
    for s in range(NT + 4):
        if 0 <= s - 2 < NT:
            seq.append(("hT", s - 2))
        if 0 <= s - 4 < NT and s % 2:
            seq.append(("y", (s - 4) // 2))
    return out[:at] + seq + out[at:]


def stat_slot(norm):
    return norm[1][0] % 4


def kernel(**inputs):
    import numpy as np
    import concourse.bacc as bacc
    from concourse.bass_utils import run_bass_kernel_spmd

    g = {k: np.asarray(v) for k, v in inputs.items()}
    x, adj = g["x"], g["adj"]

    def chunk(w):
        return w.reshape(2, P, F).transpose(1, 0, 2).reshape(P, 2 * F)

    w0 = g["L0_gnn_W"]
    w0_x, w0_agg = w0[:, :F].T, w0[:, F:].T
    w1, w2 = g["L2_gnn_W1"].T, g["L2_gnn_W2"].T
    weights = [np.concatenate([w0_agg[P * c:P * (c + 1)], w0_x[P * c:P * (c + 1)]], axis=1) for c in range(2)]
    weights += [chunk(g["L1_gnn_kernel"])]
    weights += [w1[P * c:P * (c + 1)] for c in range(2)]
    weights += [chunk(w2[2 * P * c:2 * P * (c + 1)]) for c in range(2)]
    weights += [chunk(g["L3_gnn_W%d" % k]) for k in (1, 2, 3)]
    rows = np.concatenate([g["L1_gnn_bias"], g["L2_gnn_b1"], g["L2_gnn_b2"], g["L3_gnn_b3"]])
    arrays = {
        "x": x,
        "xT": x.reshape(B, NT, P, FC, P).transpose(0, 4, 1, 3, 2).reshape(B, P, NT * F),
        "adj": adj,
        "adjT": adj.transpose(0, 2, 1),
        "weights": np.stack(weights),
        "rows": np.broadcast_to(rows, (P, rows.size)),
        "cols": np.concatenate([g["L2_gnn_gamma"].reshape(HC, P).T, g["L2_gnn_beta"].reshape(HC, P).T,
                                g["L3_gnn_b1"].reshape(FC, P).T, g["L3_gnn_b2"].reshape(FC, P).T], axis=1),
        "eye": np.concatenate([np.zeros((P, P), np.float32), np.eye(P, dtype=np.float32), np.zeros((P, P), np.float32)], axis=1),
    }
    arrays = {k: np.ascontiguousarray(v) for k, v in arrays.items()}
    nc = bacc.Bacc("TRN2", target_bir_lowering=False, num_devices=1)
    aps = [nc.dram_tensor(k + "_dram", v.shape, F32, kind="ExternalInput").ap() for k, v in arrays.items()]
    out = nc.dram_tensor("out_dram", (B, N, F), F32, kind="ExternalOutput").ap()
    build(nc, *aps, out)
    r = run_bass_kernel_spmd(nc, [{k + "_dram": v for k, v in arrays.items()}], core_ids=[0])
    return r.results[0]["out_dram"]
```

```python
from contextlib import ExitStack

import concourse.bass as bass
from concourse import mybir

ALU = mybir.AluOpType
ACT = mybir.ActivationFunctionType
F32 = mybir.dt.float32
F32R = mybir.dt.float32r

P = 128
B = 8
N = 1024
F = 256
HID = 512
NT = N // P
FC = F // P
HC = HID // P
HALF = N // 2
SLOTS = 4
HT_SLOTS = 3
WCH = 10
W_L0, W_L1, W_L2A, W_L2B, W_L3 = 0, 2, 3, 5, 7
CHUNKS = 4 + 2 * NT + 2 * NT
T_LAG, Y_LAG = 3, 4
STEPS = NT + Y_LAG
EARLY_H = 2
EPS_LN = 1e-5
EPS_DEG = 1e-6

PAIRS = range(NT // 2)
ADJ = [(h, m) for h in range(2) for m in range(NT)]
NAT = [(n, e) for n in range(NT) for e in range(2)]


class Signal:

    def __init__(self, sem, labels, before=0):
        self.sem, self.labels, self.before, self.said = sem, list(labels), before, 0

    def at(self, label, b):
        return b * len(self.labels) + (self.before + self.labels.index(label) + 1)

    def one(self, label):
        assert self.labels[self.said % len(self.labels)] == label, (label, self.labels[self.said % len(self.labels)])
        self.said += 1
        return 1


class Steps:

    def __init__(self, per_graph):
        self.per_graph, self.n = per_graph, 0

    def one(self):
        self.n += 1
        return 1

    def now(self, b):
        return b * self.per_graph + self.n


def job_labels():
    taken, ended = [], []

    def job(*labels):
        taken.extend(labels)
        ended.extend(labels)

    job(*(("S0", g) for g in PAIRS))
    job(("XW", 0), ("XW", 1), ("deg", 0), ("L0", 0), ("L0", 1))
    job(("XW", 2), ("XW", 3))
    taken += [("L0", 2), ("L0", 3), ("deg", 1)]
    ended += [("L0", 2), ("deg", 1), ("L0", 3)]
    job(("U", 0, 0), ("U", 0, 1), ("U", 1, 0), ("L1", 0), ("U", 1, 1), ("L1", 1), ("L1", 2), ("L1", 3), ("cnt",))
    job(*(("T", g) for g in PAIRS))
    taken += [("Z", h, f) for h in range(2) for f in range(FC)]
    ended += [("Z", 0, f) for f in range(FC)]
    for s in range(STEPS):
        if s == EARLY_H:
            ended += [("Z", 1, f) for f in range(FC)]
        if s < NT:
            job(("h", s))
        if 0 <= s - T_LAG < NT:
            job(("hT", s - T_LAG))
        if 0 <= s - Y_LAG < NT:
            (taken if (s - Y_LAG) % 2 == 0 else ended).append(("y", (s - Y_LAG) // 2))
        if s == NT:
            taken += [("T2", g) for g in PAIRS]
    ended += [("T2", g) for g in PAIRS]
    job(("L2", 0), ("L2", 1), ("L2", 2))
    taken += [("L2", 3), ("x3T", 0)]
    taken += [("x3T", 1)]
    ended += [("x3T", 0), ("x3T", 1), ("L2", 3)]
    job(("A1", 0), ("A1", 1))
    for h in range(2):
        taken += [("X1", h, 0), ("x3T", 2 + h), ("X1", h, 1), ("A1", 2 + h)]
        ended += [("x3T", 2 + h), ("A1", 2 + h)]
    ended += [("X1", h, f) for h in range(2) for f in range(FC)]
    job(*(("A2", g) for g in PAIRS))
    job(*(("X2", h, f) for h in range(2) for f in range(FC)))
    taken += [None] * (-len(taken) % 8)
    job(*(("A3", g) for g in PAIRS))
    job(*(("L3", g) for g in PAIRS))
    return taken, ended


def split_labels():
    out = [("S0", g) for g in PAIRS]
    out += [("x1", t) for t in range(NT)]
    out += [("U", h, f) for h in range(2) for f in range(FC)]
    out += [("x2", t) for t in range(NT)]
    out += [("T", t) for t in range(NT)]
    out += [("Z", h, f) for h in range(2) for f in range(FC)]
    out += [("hT", t) for t in range(NT)]
    out += [("T2", t) for t in range(NT)]
    out += [("x3T", 0), ("x3T", 1), ("A1", 0), ("A1", 1), ("x3T", 2), ("A1", 2), ("x3T", 3), ("A1", 3)]
    out += [("X1", h, f) for h in range(2) for f in range(FC)]
    out += [("A2", g) for g in PAIRS]
    out += [("X2", h, f) for h in range(2) for f in range(FC)]
    out += [("A3", g) for g in PAIRS]
    return out


def split_hi_labels():
    out = split_labels()
    at = out.index(("hT", 0))
    seq = []
    for s in range(STEPS):
        if 0 <= s - T_LAG < NT:
            seq.append(("hT", s - T_LAG))
        if 0 <= s - Y_LAG < NT and (s - Y_LAG) % 2:
            seq.append(("y", (s - Y_LAG) // 2))
    return out[:at] + seq + out[at + NT:]


def read_labels():
    out = [("deg", 0)] + [("L0", t) for t in range(4)] + [("deg", 1)] + [("L0", t) for t in range(4, NT)]
    out += [("L1", t) for t in range(NT)] + [("cnt",)]
    for s in range(STEPS):
        if s < NT:
            out.append(("h", s))
        if 0 <= s - Y_LAG < NT and (s - Y_LAG) % 2:
            out.append(("y", (s - Y_LAG) // 2))
    out += [("L2", t) for t in range(NT)]
    return out


NORMS = [("x1", (0, 1, 2, 3)), ("x1", (4, 5)), ("x1", (6, 7))]
NORMS += [("x2", (2 * g, 2 * g + 1)) for g in PAIRS]
NORMS += [("h", (t,)) for t in range(NT)]
NORMS += [(k, (2 * g, 2 * g + 1)) for k in ("x3", "x4") for g in PAIRS]


def build(nc, x, xT, adj, adjT, weights, rows, cols, eye, out):
    ctx = ExitStack()
    with ctx:
        def sb(name, cols_, dt=F32):
            return ctx.enter_context(nc.sbuf_tensor(name, [P, cols_], dt))

        def sem(name):
            return ctx.enter_context(nc.semaphore(name))

        A_hi = sb("A_hi", NT * N, F32R)
        A_lo = sb("A_lo", NT * N, F32R)
        with nc.sbuf_tensor("y0", [P, NT * F], F32) as y0:
            pass
        slab = sb("slab", NT * N, F32R)
        stage = sb("stage", SLOTS * HALF)
        with nc.sbuf_tensor("w_row", [P, N], F32) as w_row:
            pass
        ht = sb("ht", HT_SLOTS * HALF, F32R)
        W_hi = sb("W_hi", WCH * HALF, F32R)
        W_lo = sb("W_lo", WCH * HALF, F32R)
        P_hi = sb("P_hi", NT * F, F32R)
        P_lo = sb("P_lo", NT * F, F32R)
        Q_hi = sb("Q_hi", NT * F, F32R)
        Q_lo = sb("Q_lo", NT * F, F32R)
        xres = sb("xres", NT * F)
        colsum = sb("colsum", N)
        ytmp = sb("ytmp", 4 * F)
        eye_r = sb("eye_r", 3 * P, F32R)
        rows_sb = sb("rows_sb", 5 * F)
        betaW = sb("betaW", F)
        cols_sb = sb("cols_sb", 12)
        stats = sb("stats", 4 * 6)
        mv = sb("mv", 4 * 2)
        negm = sb("negm", 4)
        std = sb("std", 4)
        rstd = sb("rstd", 4)
        deg = sb("deg", NT)
        rdeg = sb("rdeg", NT)
        dh = sb("dh", NT)
        be = sb("be", NT)
        dn = sb("dn", NT)
        dmask = rdeg
        ones = sb("ones", 1)
        eps = sb("eps", 1)

        bank = [ctx.enter_context(nc.psum_tensor("bank%d" % i, [P, HALF], F32)) for i in range(8)]

        R_hi, R_lo, S_hi, S_lo = (slab[:, i * NT * F:(i + 1) * NT * F] for i in range(4))

        order, jobs = job_labels()
        bank_done = Signal(sem("bank_done"), jobs)
        split_ready = Signal(sem("split_ready"), split_labels())
        hi_ready = Signal(sem("hi_ready"), split_hi_labels())
        psum_read = Signal(sem("psum_read"), read_labels())
        last_read = Signal(sem("last_read"), [("L3", t) for t in range(NT)], before=1)
        xw_copied = Signal(sem("xw_copied"), PAIRS)
        relu_ready = Signal(sem("relu_ready"), [("h", t) for t in range(NT)] + [("X%d" % k, h, f) for k in (1, 2) for h in range(2) for f in range(FC)])
        var_ready = Signal(sem("var_ready"), NORMS)
        std_ready = Signal(sem("std_ready"), NORMS)
        rstd_ready = Signal(sem("rstd_ready"), NORMS)
        norm_ready = Signal(sem("norm_ready"), NORMS)
        deg_ready = Signal(sem("deg_ready"), range(2))
        sqdeg_ready = Signal(sem("sqdeg_ready"), range(2))
        dh_ready = Signal(sem("dh_ready"), range(2))
        be_ready = Signal(sem("be_ready"), range(1))
        ylo_ready = Signal(sem("ylo_ready"), PAIRS)
        biased = Signal(sem("biased"), range(NT))
        xt_hi = Signal(sem("xt_hi"), range(4))
        xt_split = Signal(sem("xt_split"), range(4))
        adj_hi = Signal(sem("adj_hi"), ADJ)
        adj_split = Signal(sem("adj_split"), ADJ)
        adj_summed = Signal(sem("adj_summed"), ADJ)
        h_made = Signal(sem("h_made"), NAT)
        h_summed = Signal(sem("h_summed"), NAT)
        ht_made = Signal(sem("ht_made"), range(2 * NT))
        ht_used = Signal(sem("ht_used"), [c for c in range(2 * NT) if c % NT != NT - 1])
        htl_made = Signal(sem("htl_made"), [(g, e) for g in PAIRS for e in range(NT)])
        stage_full = [sem("stage_full%d" % i) for i in range(SLOTS)]
        w_hi_done, w_split, w_scaled = sem("w_hi_done"), sem("w_split"), sem("w_scaled")
        const_in, const_made, beta_made, beta_done = (sem(n) for n in ("const_in", "const_made", "beta_made", "beta_done"))
        x_in, w_in, stored = sem("x_in"), sem("w_in"), sem("stored")
        dve_step = sem("dve_step")

        def slot_of(j):
            return (WCH + j) % SLOTS

        def slot(i):
            return stage[:, i * HALF:(i + 1) * HALF]

        def landed(j, b):
            return b * (16 * CHUNKS // SLOTS) + 16 * ((WCH + j) // SLOTS + 1)

        def J_XT(q):
            return q

        def J_ADJ(h, m):
            return 4 + NT * h + m

        def J_NAT(n, e):
            return 4 + 2 * NT + 2 * n + e

        def reader(label):
            kind, g = label[0], label[-1]
            if kind in ("T", "T2"):
                return split_ready, (kind, 2 * g + 1)
            if kind == "XW":
                return xw_copied, g
            if kind in ("L0", "L1", "L2"):
                return psum_read, (kind, 2 * g + 1)
            if kind == "L3":
                return last_read, (kind, 2 * g + 1)
            if kind in ("deg", "cnt", "h", "y"):
                return psum_read, label
            return split_ready, label

        place = {label: i % 8 for i, label in enumerate(order) if label}

        def psum(label):
            return bank[place[label]]

        def apart(eng):
            eng.nop(nofuse=True)

        def adj_chunk(t, h, m):
            return t[:, N * m + HALF * h:N * m + HALF * (h + 1)]

        def fmajor(t, h, f):
            return t[:, 4 * F * h:4 * F * (h + 1)].rearrange("p (t f c) -> p t f c", t=4, f=FC)[:, :, f, :]

        def quad(ap):
            return ap.rearrange("p (t c) -> p t c", t=4)

        def ht_slot(c):
            return ht[:, (c % HT_SLOTS) * HALF:(c % HT_SLOTS + 1) * HALF]

        def htl_place(g, e):
            c = NT * g + e
            if c < 6 or 22 <= c < 28:
                return ht, c % 22
            return (P_lo, c - 14) if 14 <= c < 22 else (P_hi, (c - 6) % 22)

        def htl_slot(g, e):
            where, i = htl_place(g, e)
            return where[:, F * i:F * (i + 1)]

        xlabels = [("X%d" % k, h, f) for k in (1, 2) for h in range(2) for f in range(FC)]

        block = ctx.enter_context(nc.Block())

        @block.sync
        def _(sp):
            sp.dma_start(cols_sb[:], cols).then_inc(const_in, 16)
            sp.dma_start(ytmp[:, 0:3 * P], eye).then_inc(const_in, 16)
            sp.dma_start(rows_sb[:], rows).then_inc(const_in, 16)
            for i in range(WCH):
                if i >= SLOTS:
                    sp.wait_ge(w_split, i - SLOTS + 1)
                sp.dma_start(slot(i % SLOTS), weights[i]).then_inc(stage_full[i % SLOTS], 16)

            def load_xT(b, first=False):
                for q in range(4):
                    if first:
                        sp.wait_ge(w_split, WCH - SLOTS + q + 1)
                    apart(sp)
                    sp.dma_start(slot(slot_of(J_XT(q))), xT[b, :, q * HALF:(q + 1) * HALF]).then_inc(stage_full[slot_of(J_XT(q))], 16)

            def load_adjT(b, h, m):
                j = J_ADJ(h, m)
                if j < 8:
                    sp.wait_ge(xt_split.sem, xt_split.at(j - 4, b))
                else:
                    before = ADJ[j - 8]
                    sp.wait_ge(adj_split.sem, adj_split.at(before, b))
                    sp.wait_ge(adj_summed.sem, adj_summed.at(before, b))
                apart(sp)
                sp.dma_start(slot(slot_of(j)), adjT[b, P * m:P * (m + 1), HALF * h:HALF * (h + 1)]).then_inc(stage_full[slot_of(j)], 16)

            def load_adj(b, n, e):
                j = J_NAT(n, e)
                if j < 4 + 2 * NT + SLOTS:
                    before = ADJ[j - 8]
                    sp.wait_ge(adj_split.sem, adj_split.at(before, b))
                    sp.wait_ge(adj_summed.sem, adj_summed.at(before, b))
                else:
                    sp.wait_ge(h_made.sem, h_made.at(NAT[j - 8 - 2 * NT], b))
                apart(sp)
                sp.dma_start(slot(slot_of(j)), adj[b, P * n:P * (n + 1), HALF * e:HALF * (e + 1)]).then_inc(stage_full[slot_of(j)], 16)

            def graph(b, last):
                for m in range(NT):
                    load_adjT(b, 1, m)
                sp.wait_ge(bank_done.sem, bank_done.at(("S0", 0), b))
                apart(sp)
                sp.dma_start(w_row[:], adj[b, 0:1, :].broadcast_to([P, N])).then_inc(w_in, 16)
                for n, e in NAT:
                    load_adj(b, n, e)
                if not last:
                    sp.wait_ge(bank_done.sem, bank_done.at(("hT", NT - 1), b))
                    load_xT(b + 1)
                    for m in range(NT):
                        load_adjT(b + 1, 0, m)
                for g in PAIRS:
                    sp.wait_ge(norm_ready.sem, norm_ready.at(("x4", (2 * g, 2 * g + 1)), b))
                    apart(sp)
                    sp.dma_start(out[b, 2 * P * g:2 * P * (g + 1), :].rearrange("(t p) c -> p t c", p=P),
                                 xres[:, 2 * F * g:2 * F * (g + 1)].rearrange("p (t c) -> p t c", t=2)).then_inc(stored, 16)

                if not last:
                    sp.wait_ge(stored, (b + 1) * (16 * 4))
                    apart(sp)
                    load_x(b + 1)

            def load_x(b):
                sp.dma_start(xres[:].rearrange("p (t c) -> p t c", t=NT), x[b].rearrange("(t p) c -> p t c", p=P)).then_inc(x_in, 16)

            load_xT(0, first=True)
            for m in range(NT):
                load_adjT(0, 0, m)
            load_x(0)
            with sp.Fori(0, B - 1) as b:
                graph(b, False)
            graph(B - 1, True)
            sp.wait_ge(stored, 16 * 4 * B)

        @block.tensor
        def _(pe):
            def product(o, stat, mov, start, stop, signal=None):
                passes = [(s, v) for i, s in enumerate(stat) for k, v in enumerate(mov) if i + k < 2]
                for i, (s, v) in enumerate(passes):
                    mm = nc.tensor.matmul(o, s, v, start=(start and i == 0), stop=(stop and i == len(passes) - 1), skip_group_check=True)
                if signal:
                    mm.then_inc(signal[0].sem, signal[0].one(signal[1]))
                return mm

            def open_bank(label, b):
                i = order.index(label)
                if i >= 8:
                    before = order[i - 8]
                    if before:
                        assert before in jobs[:bank_done.said % len(jobs)]
                        s, what = reader(before)
                        pe.wait_ge(s.sem, s.at(what, b))

            def weight(k, c, width=F, at=0):
                a = (k + c) * HALF + at
                return W_hi[:, a:a + width], W_lo[:, a:a + width]

            def wpair(k, c):
                return weight(k, 0, F, c * F)

            def fm(x_hi, x_lo, t, f):
                a = F * t + P * f
                return x_hi[:, a:a + P], x_lo[:, a:a + P]

            def nm(x_hi, x_lo, t, at=0, width=F):
                a = F * t + at
                return x_hi[:, a:a + width], x_lo[:, a:a + width]

            def support(label, x_hi, x_lo, w, b):
                g = label[1]
                open_bank(label, b)
                for i in range(2):
                    for f in range(FC):
                        last = i == 1 and f == FC - 1
                        product(psum(label)[:, F * i:F * (i + 1)], fm(x_hi, x_lo, 2 * g + i, f), w(f), f == 0, f == FC - 1,
                                (bank_done, label) if last else None)

            def spread_T(label, s_hi, s_lo, b, split_of, identity=False, tiles=range(NT)):
                _, h, f = label
                if tiles[0] == 0:
                    open_bank(label, b)
                for m in tiles:
                    if split_of(m):
                        pe.wait_ge(split_ready.sem, split_ready.at(split_of(m), b))
                    last = m == NT - 1 and not identity
                    product(psum(label)[:], nm(s_hi, s_lo, m, P * f, P), (adj_chunk(A_hi, h, m), adj_chunk(A_lo, h, m)), m == 0, last, (bank_done, label) if last else None)
                if identity:
                    for i in range(4):
                        a = P * min(i, 2)
                        w = 2 * P - (P * i - a)
                        move = eye_r[:, P - (P * i - a):P - (P * i - a) + 2 * P]
                        for k, s in enumerate(nm(s_hi, s_lo, 4 * h + i, P * f, P)):
                            mm = nc.tensor.matmul(psum(label)[:, a:a + 2 * P], s, move, start=False, stop=(i == 3 and k == 1), skip_group_check=True)
                    mm.then_inc(bank_done.sem, bank_done.one(label))

            def graph(b, last):
                def degree(h):
                    label = ("deg", h)
                    open_bank(label, b)
                    pe.wait_ge(adj_summed.sem, adj_summed.at((h, NT - 1), b))
                    for i in range(4):
                        a = HALF * h + P * i
                        mm = nc.tensor.matmul(psum(label)[:, i:i + 1], colsum[:, a:a + P], ones[:], start=True, stop=True)
                    mm.then_inc(bank_done.sem, bank_done.one(label))

                for g in PAIRS:
                    pe.wait_ge(xt_split.sem, xt_split.at(g, b))
                    support(("S0", g), Q_hi, Q_lo, lambda f: weight(W_L0, f), b)
                pe.wait_ge(last_read.sem, b * NT + 1)
                for h in range(2):
                    for g in (2 * h, 2 * h + 1):
                        support(("XW", g), Q_hi, Q_lo, lambda f: weight(W_L0, f, F, F), b)
                    if h == 0:
                        degree(h)
                    for g in (2 * h, 2 * h + 1):
                        open_bank(("L0", g), b)
                    for m, tiles in [(m, range(4)) for m in range(NT)] if h == 0 else [(m, (i,)) for i in range(4) for m in range(NT)]:
                        if h == 0 and m % 2 == 0:
                            pe.wait_ge(split_ready.sem, split_ready.at(("S0", m // 2), b))
                        if tiles[0] == 0:
                            pe.wait_ge(adj_split.sem, adj_split.at((h, m), b))
                        for i in tiles:
                            label = ("L0", 2 * h + i // 2)
                            a = N * m + HALF * h + P * i
                            done = m == NT - 1 and i % 2 == 1
                            product(psum(label)[:, F * (i % 2):F * (i % 2 + 1)], (A_hi[:, a:a + P], A_lo[:, a:a + P]), nm(P_hi, P_lo, m),
                                    m == 0 and (i % 2 == 0 or h == 1), m == NT - 1, (bank_done, label) if done else None)
                        if h == 1 and tiles == (1,) and m == NT - 1:
                            degree(1)
                def l1(g):
                    pe.wait_ge(split_ready.sem, split_ready.at(("U", g // 2, 1), b))
                    support(("L1", g), P_hi, P_lo, lambda f: wpair(W_L1, f), b)

                for tiles in (range(0, 4), range(4, 6), range(6, NT)):
                    for label in (("U", 0, 0), ("U", 0, 1), ("U", 1, 0)):
                        spread_T(label, Q_hi, Q_lo, b, lambda m: ("x1", m) if label == ("U", 0, 0) else None, identity=tiles[-1] == NT - 1, tiles=tiles)
                l1(0)
                spread_T(("U", 1, 1), Q_hi, Q_lo, b, lambda m: None, identity=True)
                for g in (1, 2, 3):
                    l1(g)
                open_bank(("cnt",), b)
                pe.wait_ge(h_summed.sem, h_summed.at(NAT[-1], b))
                for e in range(NT):
                    mm = nc.tensor.matmul(psum(("cnt",))[:, e:e + 1], colsum[:, P * e:P * (e + 1)], ones[:], start=True, stop=True)
                mm.then_inc(bank_done.sem, bank_done.one(("cnt",)))
                def to_edges(kind, tiles):
                    if tiles[0] == 0:
                        for g in PAIRS:
                            open_bank((kind, g), b)
                    for n in tiles:
                        if kind == "T":
                            pe.wait_ge(h_made.sem, h_made.at((n, 1), b))
                            pe.wait_ge(split_ready.sem, split_ready.at(("x2", n), b))
                        elif n % 2 == 0:
                            pe.wait_ge(ylo_ready.sem, ylo_ready.at(n // 2, b))
                        for e in range(NT):
                            label = (kind, e // 2)
                            done = n == NT - 1 and e % 2 == 1
                            product(psum(label)[:, F * (e % 2):F * (e % 2 + 1)], (slab[:, N * n + P * e:N * n + P * (e + 1)],), nm(P_hi, P_lo, n),
                                    n == 0 and e % 2 == 0, n == NT - 1, (bank_done, label) if done else None)

                def transpose_x3(g):
                    label = ("x3T", g)
                    open_bank(label, b)
                    pe.wait_ge(norm_ready.sem, norm_ready.at(("x3", (2 * g, 2 * g + 1)), b))
                    for i in range(2):
                        for f in range(FC):
                            a = F * (2 * g + i) + P * f
                            mm = nc.tensor.transpose(psum(label)[:, F * i + P * f:F * i + P * (f + 1)], xres[:, a:a + P], eye_r[:, P:2 * P].bitcast(F32))
                    mm.then_inc(bank_done.sem, bank_done.one(label))

                to_edges("T", range(NT))
                def rows_step(s):
                    if s < NT:
                        label = ("h", s)
                        open_bank(label, b)
                        if s % 4 == 0:
                            pe.wait_ge(split_ready.sem, split_ready.at(("Z", s // 4, 1), b))
                        for f in range(FC):
                            product(psum(label)[:], fm(P_hi, P_lo, s, f), weight(W_L2A, f, HID), f == 0, f == FC - 1, (bank_done, label) if f == FC - 1 else None)
                    t = s - T_LAG
                    if 0 <= t < NT:
                        label = ("hT", t)
                        open_bank(label, b)
                        pe.wait_ge(norm_ready.sem, norm_ready.at(("h", (t,)), b))
                        for j in range(HC):
                            mm = nc.tensor.transpose(psum(label)[:, P * j:P * (j + 1)], slot(t % SLOTS)[:, P * j:P * (j + 1)], eye_r[:, P:2 * P].bitcast(F32))
                        mm.then_inc(bank_done.sem, bank_done.one(label))
                    t = s - Y_LAG
                    if 0 <= t < NT:
                        label = ("y", t // 2)
                        if t % 2 == 0:
                            open_bank(label, b)
                        pe.wait_ge(split_ready.sem, split_ready.at(("hT", t), b))
                        for j in range(HC):
                            a = HALF * (t % SLOTS) + P * j
                            product(psum(label)[:, F * (t % 2):F * (t % 2 + 1)], (Q_hi[:, a:a + P], Q_lo[:, a:a + P]), wpair(W_L2B + j // 2, j % 2),
                                    j == 0, j == HC - 1, (bank_done, label) if t % 2 and j == HC - 1 else None)
                for h in range(2):
                    for f in range(FC):
                        open_bank(("Z", h, f), b)
                    for e in range(NT):
                        c = NT * h + e
                        if h == 0:
                            pe.wait_ge(split_ready.sem, split_ready.at(("T", e), b))
                        pe.wait_ge(ht_made.sem, ht_made.at(c, b))
                        for f in range(FC):
                            mine = (bank_done, ("Z", h, f)) if e == NT - 1 else (ht_used, c) if f == FC - 1 else None
                            st = nm(Q_hi, Q_lo, e, P * f, P)
                            for k in range(2):
                                mm = nc.tensor.matmul(psum(("Z", h, f))[:], st[k], ht_slot(c), start=(e == 0 and k == 0), stop=(e == NT - 1 and k == 1), skip_group_check=True)
                            if mine:
                                mm.then_inc(mine[0].sem, mine[0].one(mine[1]))
                        if (h, e) in ((1, 2), (1, 5)):
                            rows_step(e // 3)
                for s in range(EARLY_H, STEPS):
                    rows_step(s)
                    if s in (NT, NT + 1):
                        to_edges("T2", (s - NT,))
                    elif s == NT + 2:
                        to_edges("T2", (2, 3))
                to_edges("T2", range(4, NT))
                for g in PAIRS:
                    label = ("L2", g)
                    open_bank(label, b)
                    for e in range(NT):
                        if g == 0:
                            pe.wait_ge(split_ready.sem, split_ready.at(("T2", e), b))
                        pe.wait_ge(htl_made.sem, htl_made.at((g, e), b))
                        for i in range(2):
                            product(psum(label)[:, F * i:F * (i + 1)], (htl_slot(g, e)[:, P * i:P * (i + 1)],), nm(Q_hi, Q_lo, e),
                                    e == 0 and i == 0, e == NT - 1, (bank_done, label) if e == NT - 1 and i == 1 else None)
                        if (g, e) in ((3, 1), (3, 6)):
                            transpose_x3(e // 6)

                def a_job(k, g):
                    source = ("x3T", g) if k == 1 else ("X%d" % (k - 1), g // 2, 1)
                    pe.wait_ge(split_ready.sem, split_ready.at(source, b))
                    support(("A%d" % k, g), R_hi, R_lo, lambda f: wpair(W_L3 + k - 1, f), b)

                def x_job(k, h, f, tiles=range(NT)):
                    spread_T(("X%d" % k, h, f), S_hi, S_lo, b, lambda m: ("A%d" % k, m // 2) if (h == 0 or k == 1) and f == 0 and m % 2 == 0 else None, tiles=tiles)

                a_job(1, 0)
                a_job(1, 1)
                for h in range(2):
                    x_job(1, h, 0, range(0, 4))
                    transpose_x3(2 + h)
                    x_job(1, h, 1, range(0, 4))
                    a_job(1, 2 + h)
                for h in range(2):
                    for f in range(FC):
                        x_job(1, h, f, range(4, NT))
                for k in (2, 3):
                    for g in PAIRS:
                        a_job(k, g)
                    if k == 2:
                        for h in range(2):
                            for f in range(FC):
                                x_job(k, h, f)
                for g in PAIRS:
                    label = ("L3", g)
                    open_bank(label, b)
                    for i in range(2):
                        for m in range(NT):
                            if g == 0 and i == 0 and m % 2 == 0:
                                pe.wait_ge(split_ready.sem, split_ready.at(("A3", m // 2), b))
                            a = N * m + P * (2 * g + i)
                            product(psum(label)[:, F * i:F * (i + 1)], (A_hi[:, a:a + P], A_lo[:, a:a + P]), nm(S_hi, S_lo, m), m == 0, m == NT - 1,
                                    (bank_done, label) if i == 1 and m == NT - 1 else None)

            for i in range(2):
                pe.wait_ge(stage_full[(W_L2B + i) % SLOTS], 16 * ((W_L2B + i) // SLOTS + 1))
                if i == 0:
                    pe.wait_ge(beta_made, HC)
                for j in range(2):
                    mm = nc.tensor.matmul(bank[0][:, 0:F], ytmp[:, P * (2 * i + j):P * (2 * i + j + 1)], slot((W_L2B + i) % SLOTS)[:, F * j:F * (j + 1)],
                                          start=(i == 0 and j == 0), stop=(i == 1 and j == 1))
                mm.then_inc(beta_done, 1)
            pe.wait_ge(last_read.sem, 1)
            pe.wait_ge(w_split, WCH)
            with pe.Fori(0, B - 1) as b:
                graph(b, False)
            graph(B - 1, True)

        @block.scalar
        def _(act):
            def hi(label, dst, src, b, scale=None):
                ins = nc.scalar.copy(dst, src) if scale is None else nc.scalar.activation(dst, src, ACT.Identity, scale=scale)
                ins.then_inc(hi_ready.sem, hi_ready.one(label))

            def hi_job(label, dst, b):
                act.wait_ge(bank_done.sem, bank_done.at(label, b))
                hi(label, dst, psum(label)[:] if len(label) == 2 else quad(psum(label)[:]), b)

            def refill(b, h, m):
                act.wait_ge(stage_full[slot_of(J_ADJ(h, m))], landed(J_ADJ(h, m), b))
                nc.scalar.copy(adj_chunk(A_hi, h, m), slot(slot_of(J_ADJ(h, m)))).then_inc(adj_hi.sem, adj_hi.one((h, m)))

            def split_xT(b, q):
                act.wait_ge(stage_full[slot_of(J_XT(q))], landed(J_XT(q), b))
                nc.scalar.copy(Q_hi[:, q * HALF:(q + 1) * HALF], slot(slot_of(J_XT(q)))).then_inc(xt_hi.sem, xt_hi.one(q))

            def root(norm, b):
                act.wait_ge(var_ready.sem, var_ready.at(norm, b))
                i = stat_slot(norm)
                v = mv[:, 2 * i:2 * (i + len(norm[1]))].rearrange("p (t k) -> p t k", k=2)[:, :, 1]
                nc.scalar.activation(std[:, i:i + len(norm[1])], v, ACT.Sqrt, bias=eps[:]).then_inc(std_ready.sem, std_ready.one(norm))

            def graph(b, last):
                for g in PAIRS:
                    hi_job(("S0", g), P_hi[:, 2 * F * g:2 * F * (g + 1)], b)

                def copy_xw(g):
                    act.wait_ge(bank_done.sem, bank_done.at(("XW", g), b))
                    nc.scalar.copy(y0[:, 2 * F * g:2 * F * (g + 1)], psum(("XW", g))[:]).then_inc(xw_copied.sem, xw_copied.one(g))

                def root_degrees(h):
                    act.wait_ge(deg_ready.sem, deg_ready.at(h, b))
                    nc.scalar.activation(dh[:, 4 * h:4 * h + 4], deg[:, 4 * h:4 * h + 4], ACT.Sqrt, bias=ones[:]).then_inc(sqdeg_ready.sem, sqdeg_ready.one(h))

                def x1_hi(norm):
                    act.wait_ge(dh_ready.sem, dh_ready.at(norm[1][0] // 4, b))
                    act.wait_ge(norm_ready.sem, norm_ready.at(norm, b))
                    for t in norm[1]:
                        hi(("x1", t), Q_hi[:, F * t:F * (t + 1)], xres[:, F * t:F * (t + 1)], b, dh[:, t:t + 1])

                copy_xw(0)
                copy_xw(1)
                root_degrees(0)
                for m in range(NT):
                    refill(b, 1, m)
                copy_xw(2)
                copy_xw(3)
                root(NORMS[0], b)
                root_degrees(1)
                x1_hi(NORMS[0])
                root(NORMS[1], b)
                root(NORMS[2], b)
                x1_hi(NORMS[1])
                x1_hi(NORMS[2])

                def x2(g):
                    norm = ("x2", (2 * g, 2 * g + 1))
                    act.wait_ge(norm_ready.sem, norm_ready.at(norm, b))
                    for t in norm[1]:
                        hi(("x2", t), P_hi[:, F * t:F * (t + 1)], xres[:, F * t:F * (t + 1)], b)

                for label in (("U", 0, 0), ("U", 0, 1), ("U", 1, 0)):
                    hi_job(label, fmajor(P_hi, label[1], label[2]), b)
                hi_job(("U", 1, 1), fmajor(P_hi, 1, 1), b)
                root(("x2", (0, 1)), b)
                for g in (1, 2, 3):
                    x2(g - 1)
                    root(("x2", (2 * g, 2 * g + 1)), b)
                x2(3)

                def edges(kind):
                    for e in range(NT):
                        if kind == "T" and e == 0:
                            act.wait_ge(be_ready.sem, be_ready.at(0, b))
                        act.wait_ge(bank_done.sem, bank_done.at((kind, e // 2), b))
                        hi((kind, e), Q_hi[:, F * e:F * (e + 1)], psum((kind, e // 2))[:, F * (e % 2):F * (e % 2 + 1)], b, be[:, e:e + 1])

                edges("T")
                for f in range(FC):
                    hi_job(("Z", 0, f), fmajor(P_hi, 0, f), b)
                for s in range(STEPS):
                    if s == EARLY_H:
                        for f in range(FC):
                            hi_job(("Z", 1, f), fmajor(P_hi, 1, f), b)
                    t = s - T_LAG
                    if 0 <= t < NT:
                        hi_job(("hT", t), Q_hi[:, HALF * (t % SLOTS):HALF * (t % SLOTS + 1)], b)
                    if s < NT:
                        act.wait_ge(psum_read.sem, psum_read.at(("h", s), b))
                        nc.scalar.activation(slot(s % SLOTS), slot(s % SLOTS), ACT.Relu).then_inc(relu_ready.sem, relu_ready.one(("h", s)))
                    if 1 <= s <= NT:
                        root(("h", (s - 1,)), b)
                    if 0 <= s - Y_LAG < NT and (s - Y_LAG) % 2:
                        g = (s - Y_LAG) // 2
                        act.wait_ge(psum_read.sem, psum_read.at(("y", g), b))
                        hi(("y", g), P_hi[:, 2 * F * g:2 * F * (g + 1)], ytmp[:, 2 * F * (g % 2):2 * F * (g % 2 + 1)], b)
                edges("T2")
                def x3T(g):
                    hi_job(("x3T", g), R_hi[:, 2 * F * g:2 * F * (g + 1)], b)

                def a_hi(k, g):
                    hi_job(("A%d" % k, g), S_hi[:, 2 * F * g:2 * F * (g + 1)], b)

                root(("x3", (0, 1)), b)
                root(("x3", (2, 3)), b)
                x3T(0)
                x3T(1)
                a_hi(1, 0)
                root(("x3", (4, 5)), b)
                a_hi(1, 1)
                root(("x3", (6, 7)), b)
                for g in (2, 3):
                    x3T(g)
                    a_hi(1, g)
                i = 0
                for k in (1, 2, 3):
                    if k > 1:
                        for g in PAIRS:
                            a_hi(k, g)
                    if k == 2 and not last:
                        for q in range(4):
                            split_xT(b + 1, q)
                    if k < 3:
                        for h in range(2):
                            for f in range(FC):
                                label = ("X%d" % k, h, f)
                                y = ytmp[:, 2 * F * (i % 2):2 * F * (i % 2 + 1)]
                                act.wait_ge(bank_done.sem, bank_done.at(label, b))
                                if i >= 2:
                                    act.wait_ge(split_ready.sem, split_ready.at(xlabels[i - 2], b))
                                bias = cols_sb[:, 8 + 2 * (k - 1) + f:9 + 2 * (k - 1) + f]
                                nc.scalar.activation(y, psum(label)[:], ACT.Relu, bias=bias).then_inc(relu_ready.sem, relu_ready.one(label))
                                nc.scalar.activation(fmajor(R_hi, h, f), quad(psum(label)[:]), ACT.Relu, bias=bias).then_inc(hi_ready.sem, hi_ready.one(label))
                                i += 1
                for g in PAIRS:
                    if g >= 2 and not last:
                        if g == 2:
                            act.wait_ge(bank_done.sem, bank_done.at(("L3", 1), b))
                        for m in range(4 * (g - 2), 4 * (g - 1)):
                            refill(b + 1, 0, m)
                    root(("x4", (2 * g, 2 * g + 1)), b)

            for i in range(WCH):
                if i in (W_L2B, W_L2B + 1):
                    act.wait_ge(w_scaled, 2 * (i - W_L2B + 1))
                act.wait_ge(stage_full[i % SLOTS], 16 * (i // SLOTS + 1))
                nc.scalar.copy(W_hi[:, i * HALF:(i + 1) * HALF], slot(i % SLOTS)).then_inc(w_hi_done, 1)
            act.wait_ge(const_made, 3)
            for q in range(4):
                split_xT(0, q)
            for m in range(NT):
                refill(0, 0, m)
            with act.Fori(0, B - 1) as b:
                graph(b, False)
            graph(B - 1, True)

        @block.vector
        def _(dve):
            steps = Steps(DVE_STEPS)

            def link(ins, b):
                ins.then_inc(dve_step, steps.one())
                dve.wait_ge(dve_step, steps.now(b))

            def lo(label, hi_part, lo_part, src, b, scale=None, signal=None):
                dve.wait_ge(hi_ready.sem, hi_ready.at(label, b))
                if scale is None:
                    ins = nc.vector.tensor_tensor(lo_part, src, hi_part.bitcast(F32), ALU.subtract)
                else:
                    ins = nc.vector.scalar_tensor_tensor(out=lo_part, in0=src, scalar=scale, in1=hi_part.bitcast(F32), op0=ALU.mult, op1=ALU.subtract)
                ins.then_inc(split_ready.sem, split_ready.one(label))

            def lo_job(label, h_, l_, b):
                lo(label, h_, l_, psum(label)[:] if len(label) == 2 else quad(psum(label)[:]), b)

            def refill(b, h, m):
                dve.wait_ge(adj_hi.sem, adj_hi.at((h, m), b))
                nc.vector.tensor_tensor(adj_chunk(A_lo, h, m), slot(slot_of(J_ADJ(h, m))), adj_chunk(A_hi, h, m).bitcast(F32), ALU.subtract)\
                    .then_inc(adj_split.sem, adj_split.one((h, m)))

            def split_xT(b, q):
                dve.wait_ge(xt_hi.sem, xt_hi.at(q, b))
                c = slice(q * HALF, (q + 1) * HALF)
                nc.vector.tensor_tensor(Q_lo[:, c], slot(slot_of(J_XT(q))), Q_hi[:, c].bitcast(F32), ALU.subtract).then_inc(xt_split.sem, xt_split.one(q))

            def make_h(b, n, e):
                dve.wait_ge(stage_full[slot_of(J_NAT(n, e))], landed(J_NAT(n, e), b))
                nc.vector.tensor_scalar(slab[:, N * n + HALF * e:N * n + HALF * (e + 1)], slot(slot_of(J_NAT(n, e))), 0.0, None, ALU.not_equal)\
                    .then_inc(h_made.sem, h_made.one((n, e)))

            def make_ht(b, c):
                if c >= HT_SLOTS:
                    d = c - HT_SLOTS
                    if d % NT == NT - 1:
                        dve.wait_ge(bank_done.sem, bank_done.at(("Z", d // NT, 1), b))
                    else:
                        dve.wait_ge(ht_used.sem, ht_used.at(d, b))
                nc.vector.tensor_scalar(ht_slot(c), adj_chunk(A_hi, c // NT, c % NT).bitcast(F32), 0.0, None, ALU.not_equal)\
                    .then_inc(ht_made.sem, ht_made.one(c))

            def make_htl(b, g, e):
                c = NT * g + e
                if c == 0:
                    dve.wait_ge(bank_done.sem, bank_done.at(("Z", 1, 1), b))
                elif c == 6:
                    dve.wait_ge(bank_done.sem, bank_done.at(("T2", 3), b))
                elif c in (22, 28):
                    dve.wait_ge(bank_done.sem, bank_done.at(("L2", 0 if c == 22 else 1), b))
                a = N * e + 2 * P * g
                nc.vector.tensor_scalar(htl_slot(g, e), A_hi[:, a:a + 2 * P].bitcast(F32), 0.0, None, ALU.not_equal)\
                    .then_inc(htl_made.sem, htl_made.one((g, e)))

            def gather(norm, srcs):
                for k, src in enumerate(srcs):
                    ins = nc.vector.bn_stats(stats[:, 6 * (stat_slot(norm) + k):6 * (stat_slot(norm) + k + 1)], src)
                ins.then_inc(dve_step, steps.one())

            def moments(norm, b):
                i = stat_slot(norm)
                n = len(norm[1])
                dve.wait_ge(dve_step, steps.now(b))
                apart(dve)
                for k in range(n):
                    ins = nc.vector.bn_aggr(mv[:, 2 * (i + k):2 * (i + k + 1)], stats[:, 6 * (i + k):6 * (i + k + 1)])
                ins.then_inc(var_ready.sem, var_ready.one(norm))
                dve.wait_ge(var_ready.sem, var_ready.at(norm, b))
                m = mv[:, 2 * i:2 * (i + n)].rearrange("p (t k) -> p t k", k=2)[:, :, 0]
                nc.vector.tensor_scalar(negm[:, i:i + n], m, -1.0, None, ALU.mult)

            def statistics(norm, srcs, b):
                gather(norm, srcs)
                moments(norm, b)

            def invert(norm, b):
                dve.wait_ge(std_ready.sem, std_ready.at(norm, b))
                i = stat_slot(norm)
                n = len(norm[1])
                nc.vector.reciprocal(rstd[:, i:i + n], std[:, i:i + n]).then_inc(rstd_ready.sem, rstd_ready.one(norm))

            def tile_(t, i):
                return t[:, F * i:F * (i + 1)]

            def degrees(h, b):
                label = ("deg", h)
                c = slice(4 * h, 4 * h + 4)
                dve.wait_ge(bank_done.sem, bank_done.at(label, b))
                nc.vector.tensor_copy(deg[:, c], psum(label)[:, 0:4]).then_inc(psum_read.sem, psum_read.one(label))
                dve.wait_ge(psum_read.sem, psum_read.at(label, b))
                link(nc.vector.tensor_scalar(rdeg[:, c], deg[:, c], EPS_DEG, None, ALU.max), b)
                nc.vector.reciprocal(rdeg[:, c], rdeg[:, c]).then_inc(deg_ready.sem, deg_ready.one(h))
                dve.wait_ge(sqdeg_ready.sem, sqdeg_ready.at(h, b))
                dve.wait_ge(deg_ready.sem, deg_ready.at(h, b))
                nc.vector.reciprocal(dh[:, c], dh[:, c]).then_inc(dh_ready.sem, dh_ready.one(h))

            def graph(b, last):
                steps.n = 0
                for g in PAIRS:
                    c = slice(2 * F * g, 2 * F * (g + 1))
                    lo_job(("S0", g), P_hi[:, c], P_lo[:, c], b)

                def x1_read(norm):
                    for t in norm[1]:
                        g = t // 2
                        if t % 2 == 0:
                            dve.wait_ge(bank_done.sem, bank_done.at(("L0", g), b))
                            dve.wait_ge(xw_copied.sem, xw_copied.at(g, b))
                        y = tile_(y0, t)
                        nc.vector.scalar_tensor_tensor(out=y, in0=psum(("L0", g))[:, F * (t % 2):F * (t % 2 + 1)], scalar=rdeg[:, t:t + 1], in1=y, op0=ALU.mult, op1=ALU.add)\
                            .then_inc(psum_read.sem, psum_read.one(("L0", t)))

                def x1_stat(norm):
                    dve.wait_ge(psum_read.sem, psum_read.at(("L0", norm[1][-1]), b))
                    relu_add(norm, y0, 0)
                    moments(norm, b)

                def relu_add(norm, y_all, skip):
                    t, n = norm[1][0], len(norm[1])
                    y = y_all[:, F * (t - skip):F * (t - skip + n)]
                    link(nc.vector.scalar_tensor_tensor(out=y, in0=y, scalar=0.0, in1=xres[:, F * t:F * (t + n)], op0=ALU.max, op1=ALU.add), b)
                    gather(norm, [tile_(y_all, i - skip) for i in norm[1]])

                def x1_split(norm):
                    for t in norm[1]:
                        lo(("x1", t), tile_(Q_hi, t), tile_(Q_lo, t), tile_(xres, t), b, dh[:, t:t + 1])

                degrees(0, b)
                for m in range(NT):
                    refill(b, 1, m)
                    if m == 5:
                        x1_read(NORMS[0])
                dve.wait_ge(x_in, b * 16 + 16)
                x1_stat(NORMS[0])
                invert(NORMS[0], b)
                degrees(1, b)
                x1_split(NORMS[0])
                x1_read(NORMS[1])
                x1_stat(NORMS[1])
                invert(NORMS[1], b)
                x1_read(NORMS[2])
                x1_stat(NORMS[2])
                invert(NORMS[2], b)
                x1_split(NORMS[1])
                x1_split(NORMS[2])

                def x2_sum(g):
                    norm = ("x2", (2 * g, 2 * g + 1))
                    dve.wait_ge(bank_done.sem, bank_done.at(("L1", g), b))
                    if g >= 2:
                        dve.wait_ge(norm_ready.sem, norm_ready.at(("x2", (2 * g - 4, 2 * g - 3)), b))
                    for t in norm[1]:
                        nc.vector.scalar_tensor_tensor(out=tile_(ytmp, t % 4), in0=psum(("L1", g))[:, F * (t % 2):F * (t % 2 + 1)], scalar=dh[:, t:t + 1],
                                                       in1=rows_sb[:, 0:F], op0=ALU.mult, op1=ALU.add).then_inc(psum_read.sem, psum_read.one(("L1", t)))

                def x2_gather(g):
                    dve.wait_ge(psum_read.sem, psum_read.at(("L1", 2 * g + 1), b))
                    relu_add(("x2", (2 * g, 2 * g + 1)), ytmp, 4 * (g // 2))

                def x2_invert(g):
                    invert(("x2", (2 * g, 2 * g + 1)), b)

                def x2_split(g):
                    for t in (2 * g, 2 * g + 1):
                        lo(("x2", t), tile_(P_hi, t), tile_(P_lo, t), tile_(xres, t), b)

                def weigh(n):
                    if n == 0:
                        dve.wait_ge(w_in, b * 16 + 16)
                        dve.wait_ge(h_made.sem, h_made.at((1, 1), b))
                    else:
                        dve.wait_ge(dve_step, steps.now(b))
                    junk = ytmp[:] if n < 5 else stage[:, 0:N]
                    nc.vector.tensor_tensor_reduce(junk, slab[:, N * n:N * (n + 1)].bitcast(F32), w_row[:], 1.0, 0.0, ALU.mult, ALU.add, dn[:, n:n + 1]).then_inc(dve_step, steps.one())

                for n in range(NT):
                    make_h(b, n, 0)
                    make_h(b, n, 1)
                    if n in (1, 2, 4, 5, 7):
                        weigh((1, 2, 4, 5, 7).index(n))
                    if n in (3, 4, 5):
                        f = n - 3
                        lo_job(("U", f // 2, f % 2), fmajor(P_hi, f // 2, f % 2), fmajor(P_lo, f // 2, f % 2), b)
                dve.wait_ge(dve_step, steps.now(b))
                x2_sum(0)
                x2_gather(0)
                lo_job(("U", 1, 1), fmajor(P_hi, 1, 1), fmajor(P_lo, 1, 1), b)
                moments(("x2", (0, 1)), b)
                x2_invert(0)
                for g in (1, 2, 3):
                    x2_sum(g)
                    x2_gather(g)
                    x2_split(g - 1)
                    moments(("x2", (2 * g, 2 * g + 1)), b)
                    x2_invert(g)
                dve.wait_ge(bank_done.sem, bank_done.at(("cnt",), b))
                nc.vector.tensor_scalar(be[:], psum(("cnt",))[:, 0:NT], 1.0, None, ALU.max).then_inc(psum_read.sem, psum_read.one(("cnt",)))
                dve.wait_ge(psum_read.sem, psum_read.at(("cnt",), b))
                nc.vector.reciprocal(be[:], be[:]).then_inc(be_ready.sem, be_ready.one(0))
                weigh(5)
                x2_split(3)
                weigh(6)
                weigh(7)
                dve.wait_ge(dve_step, steps.now(b))
                for c in range(HT_SLOTS):
                    make_ht(b, c)

                def edges(kind, tiles=range(NT)):
                    dve.wait_ge(be_ready.sem, be_ready.at(0, b))
                    for e in tiles:
                        if e % 2 == 0:
                            dve.wait_ge(hi_ready.sem, hi_ready.at((kind, e + 1), b))
                        lo((kind, e), tile_(Q_hi, e), tile_(Q_lo, e), psum((kind, e // 2))[:, F * (e % 2):F * (e % 2 + 1)], b, be[:, e:e + 1])

                edges("T", range(0, 4))
                make_ht(b, 3)
                edges("T", (4, 5))
                make_ht(b, 4)
                edges("T", (6, 7))
                make_ht(b, 5)
                link(nc.vector.tensor_scalar(dmask[:], dn[:], 0.0, None, ALU.is_gt), b)
                link(nc.vector.tensor_tensor(dn[:], dn[:], dmask[:], ALU.mult), b)
                link(nc.vector.scalar_tensor_tensor(out=dn[:], in0=dn[:], scalar=1.0, in1=dmask[:], op0=ALU.add, op1=ALU.subtract), b)
                link(nc.vector.reciprocal(dn[:], dn[:]), b)
                link(nc.vector.tensor_tensor(dn[:], dn[:], dmask[:], ALU.mult), b)
                for c in range(6, NT + 2):
                    make_ht(b, c)
                lo_job(("Z", 0, 0), fmajor(P_hi, 0, 0), fmajor(P_lo, 0, 0), b)
                make_ht(b, NT + 2)
                lo_job(("Z", 0, 1), fmajor(P_hi, 0, 1), fmajor(P_lo, 0, 1), b)
                for c in range(NT + 3, 2 * NT - 2):
                    make_ht(b, c)
                def rows_step(s):
                    if s < NT:
                        dve.wait_ge(bank_done.sem, bank_done.at(("h", s), b))
                        if s >= SLOTS:
                            dve.wait_ge(bank_done.sem, bank_done.at(("hT", s - SLOTS), b))
                        nc.vector.scalar_tensor_tensor(out=slot(s % SLOTS), in0=psum(("h", s))[:], scalar=dn[:, s:s + 1], in1=rows_sb[:, F:F + HID], op0=ALU.mult, op1=ALU.add)\
                            .then_inc(psum_read.sem, psum_read.one(("h", s)))
                    if 1 <= s <= NT:
                        dve.wait_ge(relu_ready.sem, relu_ready.at(("h", s - 1), b))
                        gather(("h", (s - 1,)), [slot((s - 1) % SLOTS)])
                    if 0 <= s - T_LAG < NT:
                        t = s - T_LAG
                        c = slice(HALF * (t % SLOTS), HALF * (t % SLOTS + 1))
                        lo_job(("hT", t), Q_hi[:, c], Q_lo[:, c], b)
                    if 1 <= s <= NT:
                        moments(("h", (s - 1,)), b)
                    if 0 <= s - Y_LAG < NT and (s - Y_LAG) % 2:
                        g = (s - Y_LAG) // 2
                        dve.wait_ge(bank_done.sem, bank_done.at(("y", g), b))
                        if g >= 2:
                            dve.wait_ge(ylo_ready.sem, ylo_ready.at(g - 2, b))
                        nc.vector.tensor_tensor(ytmp[:, 2 * F * (g % 2):2 * F * (g % 2 + 1)].rearrange("p (t c) -> p t c", t=2), psum(("y", g))[:].rearrange("p (t c) -> p t c", t=2),
                                                betaW[:].unsqueeze(1).to_broadcast([P, 2, F]), ALU.add).then_inc(psum_read.sem, psum_read.one(("y", g)))
                    if 1 <= s <= NT:
                        invert(("h", (s - 1,)), b)
                rows_step(0)
                make_ht(b, 2 * NT - 2)
                make_ht(b, 2 * NT - 1)
                rows_step(1)
                for f in range(FC):
                    lo_job(("Z", 1, f), fmajor(P_hi, 1, f), fmajor(P_lo, 1, f), b)
                for s in range(EARLY_H, STEPS):
                    rows_step(s)
                htl = [(g, e) for g in PAIRS for e in range(NT)]
                for g, e in htl[:6]:
                    make_htl(b, g, e)
                edges("T2", range(0, 6))
                make_htl(b, *htl[6])
                edges("T2", (6,))
                make_htl(b, *htl[7])
                edges("T2", (7,))
                for g, e in htl[8:14]:
                    make_htl(b, g, e)

                def x3_sum(g):
                    norm = ("x3", (2 * g, 2 * g + 1))
                    dve.wait_ge(bank_done.sem, bank_done.at(("L2", g), b))
                    if g >= 2:
                        dve.wait_ge(norm_ready.sem, norm_ready.at(("x3", (2 * g - 4, 2 * g - 3)), b))
                    for t in norm[1]:
                        nc.vector.scalar_tensor_tensor(out=tile_(ytmp, t % 4), in0=psum(("L2", g))[:, F * (t % 2):F * (t % 2 + 1)], scalar=dn[:, t:t + 1],
                                                       in1=rows_sb[:, 3 * F:4 * F], op0=ALU.mult, op1=ALU.add).then_inc(psum_read.sem, psum_read.one(("L2", t)))
                    dve.wait_ge(psum_read.sem, psum_read.at(("L2", 2 * g + 1), b))
                    y = ytmp[:, 2 * F * (g % 2):2 * F * (g % 2 + 1)]
                    link(nc.vector.scalar_tensor_tensor(out=y, in0=xres[:, 2 * F * g:2 * F * (g + 1)], scalar=2.0, in1=y, op0=ALU.mult, op1=ALU.add), b)

                def x3_gather(g):
                    gather(("x3", (2 * g, 2 * g + 1)), [tile_(ytmp, t % 4) for t in (2 * g, 2 * g + 1)])

                def x3_stat(g):
                    x3_gather(g)
                    moments(("x3", (2 * g, 2 * g + 1)), b)

                def x3_invert(g):
                    invert(("x3", (2 * g, 2 * g + 1)), b)

                def x3T(g):
                    c = slice(2 * F * g, 2 * F * (g + 1))
                    lo_job(("x3T", g), R_hi[:, c], R_lo[:, c], b)

                def a_lo(k, g):
                    c = slice(2 * F * g, 2 * F * (g + 1))
                    lo_job(("A%d" % k, g), S_hi[:, c], S_lo[:, c], b)

                dve.wait_ge(ylo_ready.sem, ylo_ready.at(3, b))
                x3_sum(0)
                for g, e in htl[14:18]:
                    make_htl(b, g, e)
                x3_stat(0)
                for g, e in htl[18:22]:
                    make_htl(b, g, e)
                x3_invert(0)
                x3_sum(1)
                for g, e in htl[22:28]:
                    make_htl(b, g, e)
                x3_stat(1)
                for g, e in htl[28:]:
                    make_htl(b, g, e)
                x3_invert(1)
                x3T(0)
                x3_sum(2)
                x3T(1)
                x3_gather(2)
                a_lo(1, 0)
                moments(("x3", (4, 5)), b)
                x3_invert(2)
                a_lo(1, 1)
                x3_sum(3)
                x3_stat(3)
                x3_invert(3)
                for g in (2, 3):
                    x3T(g)
                    a_lo(1, g)
                i = 0
                for k in (1, 2, 3):
                    if k > 1:
                        for g in PAIRS:
                            a_lo(k, g)
                    if k == 2 and not last:
                        for q in range(4):
                            split_xT(b + 1, q)
                    if k < 3:
                        for h in range(2):
                            for f in range(FC):
                                label = ("X%d" % k, h, f)
                                dve.wait_ge(relu_ready.sem, relu_ready.at(label, b))
                                lo(label, fmajor(R_hi, h, f), fmajor(R_lo, h, f), quad(ytmp[:, 2 * F * (i % 2):2 * F * (i % 2 + 1)]), b)
                                i += 1
                for g in PAIRS:
                    norm = ("x4", (2 * g, 2 * g + 1))
                    if g >= 2 and not last:
                        for m in range(4 * (g - 2), 4 * (g - 1)):
                            refill(b + 1, 0, m)
                    dve.wait_ge(bank_done.sem, bank_done.at(("L3", g), b))
                    dve.wait_ge(biased.sem, biased.at(2 * g + 1, b))
                    if g >= 2:
                        dve.wait_ge(norm_ready.sem, norm_ready.at(("x4", (2 * g - 4, 2 * g - 3)), b))
                    for t in norm[1]:
                        nc.vector.tensor_tensor(tile_(ytmp, t % 4), psum(("L3", g))[:, F * (t % 2):F * (t % 2 + 1)], tile_(xres, t), ALU.add)\
                            .then_inc(last_read.sem, last_read.one(("L3", t)))
                    dve.wait_ge(last_read.sem, last_read.at(("L3", 2 * g + 1), b))
                    statistics(norm, [tile_(ytmp, t % 4) for t in norm[1]], b)
                    invert(norm, b)
                assert steps.n == DVE_STEPS, steps.n

            dve.wait_ge(const_in, 48)
            nc.vector.tensor_copy(eye_r[:], ytmp[:, 0:3 * P]).then_inc(const_made, 1)
            nc.vector.memset(ones[:], 1.0).then_inc(const_made, 1)
            nc.vector.memset(eps[:], EPS_LN).then_inc(const_made, 1)
            dve.wait_ge(const_made, 3)
            for j in range(HC):
                nc.vector.tensor_scalar(ytmp[:, P * j:P * (j + 1)], cols_sb[:, 4 + j:5 + j].to_broadcast([P, P]), 1.0, None, ALU.mult).then_inc(beta_made, 1)
            for i in range(WCH):
                s = slot(i % SLOTS)
                if i in (W_L2B, W_L2B + 1):
                    dve.wait_ge(beta_done, i - W_L2B + 1)
                    for j in range(2):
                        g = 2 * (i - W_L2B) + j
                        nc.vector.tensor_scalar(s[:, F * j:F * (j + 1)], s[:, F * j:F * (j + 1)], cols_sb[:, g:g + 1], None, ALU.mult).then_inc(w_scaled, 1)
                dve.wait_ge(w_hi_done, i + 1)
                c = slice(i * HALF, (i + 1) * HALF)
                nc.vector.tensor_tensor(W_lo[:, c], s, W_hi[:, c].bitcast(F32), ALU.subtract).then_inc(w_split, 1)
            nc.vector.tensor_copy(betaW[:], bank[0][:, 0:F]).then_inc(last_read.sem, 1)
            for q in range(4):
                split_xT(0, q)
            for m in range(NT):
                refill(0, 0, m)
            with dve.Fori(0, B - 1) as b:
                graph(b, False)
            graph(B - 1, True)

        @block.gpsimd
        def _(pool):
            def sum_adj(b, h, m):
                pool.wait_ge(stage_full[slot_of(J_ADJ(h, m))], landed(J_ADJ(h, m), b))
                s = slot(slot_of(J_ADJ(h, m)))
                acc = colsum[:, HALF * h:HALF * (h + 1)]
                if m == 0:
                    apart(pool)
                    ins = nc.gpsimd.tensor_scalar(acc, s, 1.0, 0.0, ALU.mult, ALU.add)
                else:
                    pool.wait_ge(adj_summed.sem, adj_summed.at((h, m - 1), b))
                    ins = nc.gpsimd.tensor_tensor(acc, acc, s, ALU.add)
                ins.then_inc(adj_summed.sem, adj_summed.one((h, m)))

            def apply(norm, srcs, dsts, b):
                pool.wait_ge(rstd_ready.sem, rstd_ready.at(norm, b))
                apart(pool)
                i = stat_slot(norm)
                for k, (s, d) in enumerate(zip(srcs, dsts)):
                    ins = nc.gpsimd.tensor_scalar(d, s, negm[:, i + k:i + k + 1], rstd[:, i + k:i + k + 1], ALU.add, ALU.mult)
                ins.then_inc(norm_ready.sem, norm_ready.one(norm))

            def apply_tiles(norm, b):
                apply(norm, [ytmp[:, F * (t % 4):F * (t % 4 + 1)] for t in norm[1]], [xres[:, F * t:F * (t + 1)] for t in norm[1]], b)

            def graph(b, last):
                for m in range(NT):
                    sum_adj(b, 1, m)
                for norm in NORMS[:3]:
                    apply(norm, [y0[:, F * t:F * (t + 1)] for t in norm[1]], [xres[:, F * t:F * (t + 1)] for t in norm[1]], b)
                pool.wait_ge(bank_done.sem, bank_done.at(("deg", 1), b))
                for n, e in NAT:
                    pool.wait_ge(h_made.sem, h_made.at((n, e), b))
                    acc = colsum[:, HALF * e:HALF * (e + 1)]
                    src = slab[:, N * n + HALF * e:N * n + HALF * (e + 1)].bitcast(F32)
                    if n == 0:
                        apart(pool)
                        ins = nc.gpsimd.tensor_scalar(acc, src, 1.0, 0.0, ALU.mult, ALU.add)
                    else:
                        pool.wait_ge(h_summed.sem, h_summed.at((n - 1, e), b))
                        ins = nc.gpsimd.tensor_tensor(acc, acc, src, ALU.add)
                    ins.then_inc(h_summed.sem, h_summed.one((n, e)))
                for norm in NORMS[3:7]:
                    apply_tiles(norm, b)
                for s in range(STEPS):
                    if 1 <= s <= NT:
                        apply(("h", (s - 1,)), [slot((s - 1) % SLOTS)], [slot((s - 1) % SLOTS)], b)
                    if 0 <= s - Y_LAG < NT and (s - Y_LAG) % 2:
                        g = (s - Y_LAG) // 2
                        pool.wait_ge(hi_ready.sem, hi_ready.at(("y", g), b))
                        c = slice(2 * F * g, 2 * F * (g + 1))
                        nc.gpsimd.tensor_tensor(P_lo[:, c], ytmp[:, 2 * F * (g % 2):2 * F * (g % 2 + 1)], P_hi[:, c].bitcast(F32), ALU.subtract)\
                            .then_inc(ylo_ready.sem, ylo_ready.one(g))
                for g in PAIRS:
                    apply_tiles(("x3", (2 * g, 2 * g + 1)), b)
                for t in range(NT):
                    if t % 2 == 0:
                        pool.wait_ge(bank_done.sem, bank_done.at(("x3T", t // 2), b))
                    pool.wait_ge(norm_ready.sem, norm_ready.at(("x3", (6, 7)), b))
                    c = slice(F * t, F * (t + 1))
                    nc.gpsimd.tensor_tensor(xres[:, c], xres[:, c], rows_sb[:, 4 * F:5 * F], ALU.add).then_inc(biased.sem, biased.one(t))
                for g in PAIRS:
                    if g >= 2 and not last:
                        for m in range(4 * (g - 2), 4 * (g - 1)):
                            sum_adj(b + 1, 0, m)
                    apply_tiles(("x4", (2 * g, 2 * g + 1)), b)

            for m in range(NT):
                sum_adj(0, 0, m)
            with pool.Fori(0, B - 1) as b:
                graph(b, False)
            graph(B - 1, True)


DVE_STEPS = 49


def stat_slot(norm):
    return norm[1][0] % 4


def kernel(**inputs):
    import numpy as np
    import concourse.bacc as bacc
    from concourse.bass_utils import run_bass_kernel_spmd

    g = {k: np.asarray(v) for k, v in inputs.items()}
    x, adj = g["x"], g["adj"]

    def chunk(w):
        return w.reshape(2, P, F).transpose(1, 0, 2).reshape(P, 2 * F)

    w0 = g["L0_gnn_W"]
    w0_x, w0_agg = w0[:, :F].T, w0[:, F:].T
    w1, w2 = g["L2_gnn_W1"].T, g["L2_gnn_W2"].T
    weights = [np.concatenate([w0_agg[P * c:P * (c + 1)], w0_x[P * c:P * (c + 1)]], axis=1) for c in range(2)]
    weights += [chunk(g["L1_gnn_kernel"])]
    weights += [w1[P * c:P * (c + 1)] for c in range(2)]
    weights += [chunk(w2[2 * P * c:2 * P * (c + 1)]) for c in range(2)]
    weights += [chunk(g["L3_gnn_W%d" % k]) for k in (1, 2, 3)]
    rows = np.concatenate([g["L1_gnn_bias"], g["L2_gnn_b1"], g["L2_gnn_b2"], g["L3_gnn_b3"]])
    arrays = {
        "x": x,
        "xT": x.reshape(B, NT, P, FC, P).transpose(0, 4, 1, 3, 2).reshape(B, P, NT * F),
        "adj": adj,
        "adjT": adj.transpose(0, 2, 1),
        "weights": np.stack(weights),
        "rows": np.broadcast_to(rows, (P, rows.size)),
        "cols": np.concatenate([g["L2_gnn_gamma"].reshape(HC, P).T, g["L2_gnn_beta"].reshape(HC, P).T,
                                g["L3_gnn_b1"].reshape(FC, P).T, g["L3_gnn_b2"].reshape(FC, P).T], axis=1),
        "eye": np.concatenate([np.zeros((P, P), np.float32), np.eye(P, dtype=np.float32), np.zeros((P, P), np.float32)], axis=1),
    }
    arrays = {k: np.ascontiguousarray(v) for k, v in arrays.items()}
    nc = bacc.Bacc("TRN2", target_bir_lowering=False, num_devices=1)
    aps = [nc.dram_tensor(k + "_dram", v.shape, F32, kind="ExternalInput").ap() for k, v in arrays.items()]
    out = nc.dram_tensor("out_dram", (B, N, F), F32, kind="ExternalOutput").ap()
    build(nc, *aps, out)
    r = run_bass_kernel_spmd(nc, [{k + "_dram": v for k, v in arrays.items()}], core_ids=[0])
    return r.results[0]["out_dram"]
```

```python
from contextlib import ExitStack

import concourse.bass as bass
from concourse import mybir

ALU = mybir.AluOpType
ACT = mybir.ActivationFunctionType
F32 = mybir.dt.float32
F32R = mybir.dt.float32r

P = 128
B = 8
N = 1024
F = 256
HID = 512
NT = N // P
FC = F // P
HC = HID // P
HALF = N // 2
SLOTS = 4
HT_SLOTS = 3
WCH = 10
W_FIRST, W_THEN, W_LAST = [0, 1], [5, 6, 2, 3], [4, 7, 8, 9]
W_ORDER = W_FIRST + W_THEN + W_LAST
W_L0, W_L1, W_L2A, W_L2B, W_L3 = 0, 2, 3, 5, 7
CHUNKS = 4 + 2 * NT + 2 * NT
T_LAG, Y_LAG = 3, 4
STEPS = NT + Y_LAG
EARLY_H = 2
WEIGHED_IN_Y = 8
WEIGHED_WITH = ((8, 9), (10, 11), (12, 13), (14, 15))
EPS_LN = 1e-5
EPS_DEG = 1e-6

PAIRS = range(NT // 2)
ADJ = [(h, m) for h in range(2) for m in range(NT)]
COUNTED = [4, 5, 6, 7, 0, 1, 2, 3]
NAT = [(n, e) for n in range(NT) for e in range(2)]


class Signal:

    def __init__(self, sem, labels, before=0):
        self.sem, self.labels, self.before, self.said = sem, list(labels), before, 0

    def at(self, label, b):
        return b * len(self.labels) + (self.before + self.labels.index(label) + 1)

    def one(self, label):
        assert self.labels[self.said % len(self.labels)] == label, (label, self.labels[self.said % len(self.labels)])
        self.said += 1
        return 1


class Steps:

    def __init__(self, per_graph):
        self.per_graph, self.n = per_graph, 0

    def one(self):
        self.n += 1
        return 1

    def now(self, b):
        return b * self.per_graph + self.n


def job_labels():
    taken, ended = [], []

    def job(*labels):
        taken.extend(labels)
        ended.extend(labels)

    job(*(("S0", g) for g in PAIRS))
    job(("XW", 0), ("XW", 1), ("deg", 0), ("L0", 0), ("L0", 1))
    job(("XW", 2), ("XW", 3))
    taken += [("L0", 2), ("L0", 3), ("deg", 1)]
    ended += [("L0", 2), ("deg", 1), ("L0", 3)]
    job(("U", 0, 0), ("U", 0, 1), ("U", 1, 0), ("L1", 0), ("U", 1, 1), ("L1", 1), ("L1", 2), ("L1", 3))
    job(*(("T", g) for g in PAIRS))
    taken += [("Z", h, f) for h in range(2) for f in range(FC)]
    ended += [("Z", 0, f) for f in range(FC)]
    for s in range(STEPS):
        if s == EARLY_H:
            ended += [("Z", 1, f) for f in range(FC)]
        if s < NT:
            job(("h", s))
        if 0 <= s - T_LAG < NT:
            job(("hT", s - T_LAG))
        if 0 <= s - Y_LAG < NT:
            (taken if (s - Y_LAG) % 2 == 0 else ended).append(("y", (s - Y_LAG) // 2))
        if s == NT:
            taken += [("T2", g) for g in PAIRS]
    ended += [("T2", g) for g in PAIRS]
    job(("L2", 0), ("L2", 1), ("L2", 2))
    taken += [("L2", 3), ("x3T", 0)]
    taken += [("x3T", 1)]
    ended += [("x3T", 0), ("x3T", 1), ("L2", 3)]
    job(("A1", 0), ("A1", 1))
    for h in range(2):
        taken += [("X1", h, 0), ("x3T", 2 + h), ("X1", h, 1), ("A1", 2 + h)]
        ended += [("x3T", 2 + h), ("A1", 2 + h)]
    ended += [("X1", h, f) for h in range(2) for f in range(FC)]
    job(*(("A2", g) for g in PAIRS))
    job(*(("X2", h, f) for h in range(2) for f in range(FC)))
    taken += [None] * (-len(taken) % 8)
    job(*(("A3", g) for g in PAIRS))
    job(*(("L3", g) for g in PAIRS))
    return taken, ended


def split_labels():
    out = [("S0", g) for g in PAIRS]
    out += [("x1", t) for t in range(NT)]
    out += [("U", h, f) for h in range(2) for f in range(FC)]
    out += [("x2", t) for t in range(NT)]
    out += [("T", t) for t in range(NT)]
    out += [("Z", h, f) for h in range(2) for f in range(FC)]
    out += [("hT", t) for t in range(NT)]
    out += [("T2", t) for t in range(NT)]
    out += [("x3T", 0), ("x3T", 1), ("A1", 0), ("A1", 1), ("x3T", 2), ("A1", 2), ("x3T", 3), ("A1", 3)]
    out += [("X1", h, f) for h in range(2) for f in range(FC)]
    out += [("A2", g) for g in PAIRS]
    out += [("X2", h, f) for h in range(2) for f in range(FC)]
    out += [("A3", g) for g in PAIRS]
    return out


def split_hi_labels():
    out = split_labels()
    at = out.index(("hT", 0))
    seq = []
    for s in range(STEPS):
        if 0 <= s - T_LAG < NT:
            seq.append(("hT", s - T_LAG))
        if 0 <= s - Y_LAG < NT and (s - Y_LAG) % 2:
            seq.append(("y", (s - Y_LAG) // 2))
    return out[:at] + seq + out[at + NT:]


def read_labels():
    out = [("deg", 0)] + [("L0", t) for t in range(4)] + [("deg", 1)] + [("L0", t) for t in range(4, NT)]
    out += [("L1", t) for t in range(NT)]
    for s in range(STEPS):
        if s < NT:
            out.append(("h", s))
        if 0 <= s - Y_LAG < NT and (s - Y_LAG) % 2:
            out.append(("y", (s - Y_LAG) // 2))
    out += [("L2", t) for t in range(NT)]
    return out


NORMS = [("x1", (0, 1, 2, 3)), ("x1", (4, 5)), ("x1", (6, 7))]
NORMS += [("x2", (2 * g, 2 * g + 1)) for g in PAIRS]
NORMS += [("h", (t,)) for t in range(NT)]
NORMS += [(k, (2 * g, 2 * g + 1)) for k in ("x3", "x4") for g in PAIRS]


def build(nc, x, xT, adj, adjT, weights, rows, cols, eye, out):
    ctx = ExitStack()
    with ctx:
        def sb(name, cols_, dt=F32):
            return ctx.enter_context(nc.sbuf_tensor(name, [P, cols_], dt))

        def sem(name):
            return ctx.enter_context(nc.semaphore(name))

        A_hi = sb("A_hi", NT * N, F32R)
        A_lo = sb("A_lo", NT * N, F32R)
        with nc.sbuf_tensor("y0", [P, NT * F + NT * HALF], F32) as y0:
            pass
        with nc.sbuf_tensor("w_stage", [P, WCH * HALF], F32) as w_stage:
            pass
        slab = sb("slab", NT * N, F32R)
        stage = sb("stage", SLOTS * HALF)
        with nc.sbuf_tensor("w_row", [P, N], F32) as w_row:
            pass
        ht = sb("ht", HT_SLOTS * HALF, F32R)
        W_hi = sb("W_hi", WCH * HALF, F32R)
        W_lo = sb("W_lo", WCH * HALF, F32R)
        P_hi = sb("P_hi", NT * F, F32R)
        P_lo = sb("P_lo", NT * F, F32R)
        Q_hi = sb("Q_hi", NT * F, F32R)
        Q_lo = sb("Q_lo", NT * F, F32R)
        xres = sb("xres", NT * F)
        colsum = sb("colsum", N)
        ytmp = sb("ytmp", 4 * F)
        eye_r = sb("eye_r", P, F32R)
        rows_sb = sb("rows_sb", 5 * F)
        betaW = sb("betaW", F)
        cols_sb = sb("cols_sb", 12)
        stats = sb("stats", 4 * 6)
        mv = sb("mv", 4 * 2)
        negm = sb("negm", 4)
        std = sb("std", 4)
        rstd = sb("rstd", 4)
        deg = sb("deg", NT)
        rdeg = sb("rdeg", NT)
        cnt = sb("cnt", 2 * NT)
        dh = sb("dh", NT)
        be = sb("be", NT)
        weight_of = sb("weight_of", 2 * NT)
        dn = sb("dn", NT)
        dmask = rdeg
        ones = sb("ones", 1)
        eps = sb("eps", 1)

        bank = [ctx.enter_context(nc.psum_tensor("bank%d" % i, [P, HALF], F32)) for i in range(8)]

        R_hi, R_lo, S_hi, S_lo = (slab[:, i * NT * F:(i + 1) * NT * F] for i in range(4))

        order, jobs = job_labels()
        bank_done = Signal(sem("bank_done"), jobs)
        split_ready = Signal(sem("split_ready"), split_labels())
        hi_ready = Signal(sem("hi_ready"), split_hi_labels())
        psum_read = Signal(sem("psum_read"), read_labels())
        last_read = Signal(sem("last_read"), [("L3", t) for t in range(NT)], before=1)
        xw_copied = Signal(sem("xw_copied"), PAIRS)
        relu_ready = Signal(sem("relu_ready"), [("h", t) for t in range(NT)] + [("X%d" % k, h, f) for k in (1, 2) for h in range(2) for f in range(FC)])
        var_ready = Signal(sem("var_ready"), NORMS)
        std_ready = Signal(sem("std_ready"), NORMS)
        rstd_ready = Signal(sem("rstd_ready"), NORMS)
        norm_ready = Signal(sem("norm_ready"), NORMS)
        deg_ready = Signal(sem("deg_ready"), range(2))
        sqdeg_ready = Signal(sem("sqdeg_ready"), range(2))
        dh_ready = Signal(sem("dh_ready"), range(2))
        be_ready = Signal(sem("be_ready"), range(1))
        ylo_ready = Signal(sem("ylo_ready"), PAIRS)
        biased = Signal(sem("biased"), range(NT))
        xt_hi = Signal(sem("xt_hi"), range(4))
        xt_split = Signal(sem("xt_split"), range(4))
        adj_hi = Signal(sem("adj_hi"), ADJ)
        adj_split = Signal(sem("adj_split"), ADJ)
        adj_summed = Signal(sem("adj_summed"), ADJ)
        h_made = Signal(sem("h_made"), NAT)
        diag_saved = Signal(sem("diag_saved"), range(2))
        diag_added = Signal(sem("diag_added"), range(2))
        diag_hi = Signal(sem("diag_hi"), range(2))
        diag_split = Signal(sem("diag_split"), range(2))
        marked = Signal(sem("marked"), COUNTED)
        counted = Signal(sem("counted"), COUNTED)
        weighed = Signal(sem("weighed"), NAT)
        weight_summed = Signal(sem("weight_summed"), NAT)
        back_hi = Signal(sem("back_hi"), range(2))
        back_split = Signal(sem("back_split"), range(2))
        ht_made = Signal(sem("ht_made"), range(2 * NT))
        ht_used = Signal(sem("ht_used"), [c for c in range(2 * NT) if c % NT != NT - 1])
        htl_made = Signal(sem("htl_made"), [(g, e) for g in PAIRS for e in range(NT)])
        w_full = [sem("w_full%d" % i) for i in range(WCH)]
        stage_full = [sem("stage_full%d" % i) for i in range(SLOTS)]
        w_hi_done, w_split, w_scaled = sem("w_hi_done"), sem("w_split"), sem("w_scaled")
        const_in, const_made, beta_made, beta_done = (sem(n) for n in ("const_in", "const_made", "beta_made", "beta_done"))
        x_in, w_in, stored = sem("x_in"), sem("w_in"), sem("stored")
        dve_step = sem("dve_step")

        def slot_of(j):
            return j % SLOTS

        def slot(i):
            return stage[:, i * HALF:(i + 1) * HALF]

        def landed(j, b):
            return b * (16 * CHUNKS // SLOTS) + 16 * (j // SLOTS + 1)

        def J_XT(q):
            return q

        def J_ADJ(h, m):
            return 4 + NT * h + m

        def J_NAT(n, e):
            return 4 + 2 * NT + 2 * n + e

        def reader(label):
            kind, g = label[0], label[-1]
            if kind in ("T", "T2"):
                return split_ready, (kind, 2 * g + 1)
            if kind == "XW":
                return xw_copied, g
            if kind in ("L0", "L1", "L2"):
                return psum_read, (kind, 2 * g + 1)
            if kind == "L3":
                return last_read, (kind, 2 * g + 1)
            if kind in ("deg", "h", "y"):
                return psum_read, label
            return split_ready, label

        place = {label: i % 8 for i, label in enumerate(order) if label}

        def psum(label):
            return bank[place[label]]

        def apart(eng):
            eng.nop(nofuse=True)

        def adj_chunk(t, h, m):
            return t[:, N * m + HALF * h:N * m + HALF * (h + 1)]

        def diagonal(t, h):
            shift = N * h
            a = 4 * (N + P) * h - shift
            return t[:, a:a + 4 * (N + P)].rearrange("p (t c) -> p t c", t=4)[:, :, shift:shift + P]

        def marks(m):
            return y0[:, NT * F + HALF * m:NT * F + HALF * (m + 1)]

        def weighed_in(k):
            if k < WEIGHED_IN_Y:
                i = k % 2 if k < 6 else 1
                return ytmp[:, HALF * i:HALF * (i + 1)]
            return slot(k % SLOTS)

        def fmajor(t, h, f):
            return t[:, 4 * F * h:4 * F * (h + 1)].rearrange("p (t f c) -> p t f c", t=4, f=FC)[:, :, f, :]

        def quad(ap):
            return ap.rearrange("p (t c) -> p t c", t=4)

        def raw_weight(i):
            return w_stage[:, i * HALF:(i + 1) * HALF]

        def ht_slot(c):
            return ht[:, (c % HT_SLOTS) * HALF:(c % HT_SLOTS + 1) * HALF]

        def htl_place(g, e):
            c = NT * g + e
            if c < 6 or 22 <= c < 28:
                return ht, c % 22
            return (P_lo, c - 14) if 14 <= c < 22 else (P_hi, (c - 6) % 22)

        def htl_slot(g, e):
            where, i = htl_place(g, e)
            return where[:, F * i:F * (i + 1)]

        xlabels = [("X%d" % k, h, f) for k in (1, 2) for h in range(2) for f in range(FC)]

        block = ctx.enter_context(nc.Block())

        @block.sync
        def _(sp):
            sp.dma_start(cols_sb[:], cols).then_inc(const_in, 16)
            sp.dma_start(ytmp[:, 0:P], eye).then_inc(const_in, 16)
            sp.dma_start(rows_sb[:], rows).then_inc(const_in, 16)
            def load_weights(chunks):
                for i in chunks:
                    sp.dma_start(raw_weight(i), weights[i]).then_inc(w_full[i], 16)

            def load_xT(b):
                for q in range(4):
                    apart(sp)
                    sp.dma_start(slot(slot_of(J_XT(q))), xT[b, :, q * HALF:(q + 1) * HALF]).then_inc(stage_full[slot_of(J_XT(q))], 16)

            def load_adjT(b, h, m):
                j = J_ADJ(h, m)
                if j < 8:
                    sp.wait_ge(xt_split.sem, xt_split.at(j - 4, b))
                else:
                    before = ADJ[j - 8]
                    sp.wait_ge(adj_split.sem, adj_split.at(before, b))
                    sp.wait_ge(adj_summed.sem, adj_summed.at(before, b))
                apart(sp)
                sp.dma_start(slot(slot_of(j)), adjT[b, P * m:P * (m + 1), HALF * h:HALF * (h + 1)]).then_inc(stage_full[slot_of(j)], 16)

            def load_adj(b, n, e):
                j = J_NAT(n, e)
                if j < 4 + 2 * NT + SLOTS:
                    before = ADJ[j - 8]
                    sp.wait_ge(adj_split.sem, adj_split.at(before, b))
                    sp.wait_ge(adj_summed.sem, adj_summed.at(before, b))
                else:
                    sp.wait_ge(h_made.sem, h_made.at(NAT[j - 8 - 2 * NT], b))
                apart(sp)
                sp.dma_start(slot(slot_of(j)), adj[b, P * n:P * (n + 1), HALF * e:HALF * (e + 1)]).then_inc(stage_full[slot_of(j)], 16)

            def graph(b, last):
                for m in range(NT):
                    load_adjT(b, 1, m)
                sp.wait_ge(bank_done.sem, bank_done.at(("S0", 0), b))
                apart(sp)
                sp.dma_start(w_row[:], adj[b, 0:1, :].broadcast_to([P, N])).then_inc(w_in, 16)
                for n, e in NAT:
                    load_adj(b, n, e)
                if not last:
                    sp.wait_ge(bank_done.sem, bank_done.at(("hT", NT - 1), b))
                    load_xT(b + 1)
                    for m in range(NT):
                        load_adjT(b + 1, 0, m)
                for g in PAIRS:
                    sp.wait_ge(norm_ready.sem, norm_ready.at(("x4", (2 * g, 2 * g + 1)), b))
                    apart(sp)
                    sp.dma_start(out[b, 2 * P * g:2 * P * (g + 1), :].rearrange("(t p) c -> p t c", p=P),
                                 xres[:, 2 * F * g:2 * F * (g + 1)].rearrange("p (t c) -> p t c", t=2)).then_inc(stored, 16)

                if not last:
                    sp.wait_ge(stored, (b + 1) * (16 * 4))
                    apart(sp)
                    load_x(b + 1)

            def load_x(b):
                sp.dma_start(xres[:].rearrange("p (t c) -> p t c", t=NT), x[b].rearrange("(t p) c -> p t c", p=P)).then_inc(x_in, 16)

            load_weights(W_FIRST)
            load_xT(0)
            load_weights(W_THEN)
            for m in range(0, 4):
                load_adjT(0, 0, m)
            load_weights(W_LAST)
            for m in range(4, NT):
                load_adjT(0, 0, m)
            load_x(0)
            with sp.Fori(0, B - 1) as b:
                graph(b, False)
            graph(B - 1, True)
            sp.wait_ge(stored, 16 * 4 * B)

        @block.tensor
        def _(pe):
            def product(o, stat, mov, start, stop, signal=None):
                passes = [(s, v) for i, s in enumerate(stat) for k, v in enumerate(mov) if i + k < 2]
                for i, (s, v) in enumerate(passes):
                    mm = nc.tensor.matmul(o, s, v, start=(start and i == 0), stop=(stop and i == len(passes) - 1), skip_group_check=True)
                if signal:
                    mm.then_inc(signal[0].sem, signal[0].one(signal[1]))
                return mm

            def open_bank(label, b):
                i = order.index(label)
                if i >= 8:
                    before = order[i - 8]
                    if before:
                        assert before in jobs[:bank_done.said % len(jobs)]
                        s, what = reader(before)
                        pe.wait_ge(s.sem, s.at(what, b))

            def weight(k, c, width=F, at=0):
                a = (k + c) * HALF + at
                return W_hi[:, a:a + width], W_lo[:, a:a + width]

            def wpair(k, c):
                return weight(k, 0, F, c * F)

            def fm(x_hi, x_lo, t, f):
                a = F * t + P * f
                return x_hi[:, a:a + P], x_lo[:, a:a + P]

            def nm(x_hi, x_lo, t, at=0, width=F):
                a = F * t + at
                return x_hi[:, a:a + width], x_lo[:, a:a + width]

            def support(label, x_hi, x_lo, w, b):
                g = label[1]
                open_bank(label, b)
                for i in range(2):
                    for f in range(FC):
                        last = i == 1 and f == FC - 1
                        product(psum(label)[:, F * i:F * (i + 1)], fm(x_hi, x_lo, 2 * g + i, f), w(f), f == 0, f == FC - 1,
                                (bank_done, label) if last else None)

            def spread_T(label, s_hi, s_lo, b, split_of, tiles=range(NT)):
                _, h, f = label
                if tiles[0] == 0:
                    open_bank(label, b)
                for m in tiles:
                    if split_of(m):
                        pe.wait_ge(split_ready.sem, split_ready.at(split_of(m), b))
                    product(psum(label)[:], nm(s_hi, s_lo, m, P * f, P), (adj_chunk(A_hi, h, m), adj_chunk(A_lo, h, m)), m == 0, m == NT - 1,
                            (bank_done, label) if m == NT - 1 else None)

            def graph(b, last):
                def degree(h):
                    label = ("deg", h)
                    open_bank(label, b)
                    pe.wait_ge(adj_summed.sem, adj_summed.at((h, NT - 1), b))
                    for i in range(4):
                        a = HALF * h + P * i
                        mm = nc.tensor.matmul(psum(label)[:, i:i + 1], colsum[:, a:a + P], ones[:], start=True, stop=True)
                    mm.then_inc(bank_done.sem, bank_done.one(label))

                for g in PAIRS:
                    pe.wait_ge(xt_split.sem, xt_split.at(g, b))
                    support(("S0", g), Q_hi, Q_lo, lambda f: weight(W_L0, f), b)
                pe.wait_ge(last_read.sem, b * NT + 1)
                for h in range(2):
                    for g in (2 * h, 2 * h + 1):
                        support(("XW", g), Q_hi, Q_lo, lambda f: weight(W_L0, f, F, F), b)
                    if h == 0:
                        degree(h)
                    for g in (2 * h, 2 * h + 1):
                        open_bank(("L0", g), b)
                    for m, tiles in [(m, range(4)) for m in range(NT)] if h == 0 else [(m, (i,)) for i in range(4) for m in range(NT)]:
                        if h == 0 and m % 2 == 0:
                            pe.wait_ge(split_ready.sem, split_ready.at(("S0", m // 2), b))
                        if tiles[0] == 0:
                            pe.wait_ge(adj_split.sem, adj_split.at((h, m), b))
                        for i in tiles:
                            label = ("L0", 2 * h + i // 2)
                            a = N * m + HALF * h + P * i
                            done = m == NT - 1 and i % 2 == 1
                            product(psum(label)[:, F * (i % 2):F * (i % 2 + 1)], (A_hi[:, a:a + P], A_lo[:, a:a + P]), nm(P_hi, P_lo, m),
                                    m == 0 and (i % 2 == 0 or h == 1), m == NT - 1, (bank_done, label) if done else None)
                        if h == 1 and tiles == (1,) and m == NT - 1:
                            degree(1)
                def l1(g):
                    pe.wait_ge(split_ready.sem, split_ready.at(("U", g // 2, 1), b))
                    support(("L1", g), P_hi, P_lo, lambda f: wpair(W_L1, f), b)

                pe.wait_ge(w_split, WCH)
                pe.wait_ge(diag_split.sem, diag_split.at(0, b))
                for tiles in (range(0, 4), range(4, 6), range(6, NT)):
                    for label in (("U", 0, 0), ("U", 0, 1), ("U", 1, 0)):
                        if tiles[0] == 4 and label[1] == 1:
                            pe.wait_ge(diag_split.sem, diag_split.at(1, b))
                        spread_T(label, Q_hi, Q_lo, b, lambda m: ("x1", m) if label == ("U", 0, 0) else None, tiles=tiles)
                l1(0)
                spread_T(("U", 1, 1), Q_hi, Q_lo, b, lambda m: None)
                for g in (1, 2, 3):
                    l1(g)
                def to_edges(kind, tiles):
                    if tiles[0] == 0:
                        for g in PAIRS:
                            open_bank((kind, g), b)
                    for n in tiles:
                        if kind == "T":
                            pe.wait_ge(h_made.sem, h_made.at((n, 1), b))
                            pe.wait_ge(split_ready.sem, split_ready.at(("x2", n), b))
                        elif n % 2 == 0:
                            pe.wait_ge(ylo_ready.sem, ylo_ready.at(n // 2, b))
                        for e in range(NT):
                            label = (kind, e // 2)
                            done = n == NT - 1 and e % 2 == 1
                            product(psum(label)[:, F * (e % 2):F * (e % 2 + 1)], (slab[:, N * n + P * e:N * n + P * (e + 1)],), nm(P_hi, P_lo, n),
                                    n == 0 and e % 2 == 0, n == NT - 1, (bank_done, label) if done else None)

                def transpose_x3(g):
                    label = ("x3T", g)
                    open_bank(label, b)
                    pe.wait_ge(norm_ready.sem, norm_ready.at(("x3", (2 * g, 2 * g + 1)), b))
                    for i in range(2):
                        for f in range(FC):
                            a = F * (2 * g + i) + P * f
                            mm = nc.tensor.transpose(psum(label)[:, F * i + P * f:F * i + P * (f + 1)], xres[:, a:a + P], eye_r[:].bitcast(F32))
                    mm.then_inc(bank_done.sem, bank_done.one(label))

                to_edges("T", range(NT))
                def rows_step(s):
                    if s < NT:
                        label = ("h", s)
                        open_bank(label, b)
                        if s % 4 == 0:
                            pe.wait_ge(split_ready.sem, split_ready.at(("Z", s // 4, 1), b))
                        for f in range(FC):
                            product(psum(label)[:], fm(P_hi, P_lo, s, f), weight(W_L2A, f, HID), f == 0, f == FC - 1, (bank_done, label) if f == FC - 1 else None)
                    t = s - T_LAG
                    if 0 <= t < NT:
                        label = ("hT", t)
                        open_bank(label, b)
                        pe.wait_ge(norm_ready.sem, norm_ready.at(("h", (t,)), b))
                        for j in range(HC):
                            mm = nc.tensor.transpose(psum(label)[:, P * j:P * (j + 1)], slot(t % SLOTS)[:, P * j:P * (j + 1)], eye_r[:].bitcast(F32))
                        mm.then_inc(bank_done.sem, bank_done.one(label))
                    t = s - Y_LAG
                    if 0 <= t < NT:
                        label = ("y", t // 2)
                        if t % 2 == 0:
                            open_bank(label, b)
                        pe.wait_ge(split_ready.sem, split_ready.at(("hT", t), b))
                        for j in range(HC):
                            a = HALF * (t % SLOTS) + P * j
                            product(psum(label)[:, F * (t % 2):F * (t % 2 + 1)], (Q_hi[:, a:a + P], Q_lo[:, a:a + P]), wpair(W_L2B + j // 2, j % 2),
                                    j == 0, j == HC - 1, (bank_done, label) if t % 2 and j == HC - 1 else None)
                for h in range(2):
                    for f in range(FC):
                        open_bank(("Z", h, f), b)
                    for e in range(NT):
                        c = NT * h + e
                        if h == 0:
                            pe.wait_ge(split_ready.sem, split_ready.at(("T", e), b))
                        pe.wait_ge(ht_made.sem, ht_made.at(c, b))
                        for f in range(FC):
                            mine = (bank_done, ("Z", h, f)) if e == NT - 1 else (ht_used, c) if f == FC - 1 else None
                            st = nm(Q_hi, Q_lo, e, P * f, P)
                            for k in range(2):
                                mm = nc.tensor.matmul(psum(("Z", h, f))[:], st[k], ht_slot(c), start=(e == 0 and k == 0), stop=(e == NT - 1 and k == 1), skip_group_check=True)
                            if mine:
                                mm.then_inc(mine[0].sem, mine[0].one(mine[1]))
                        if (h, e) in ((1, 2), (1, 5)):
                            rows_step(e // 3)
                for s in range(EARLY_H, STEPS):
                    rows_step(s)
                    if s in (NT, NT + 1):
                        to_edges("T2", (s - NT,))
                    elif s == NT + 2:
                        to_edges("T2", (2, 3))
                to_edges("T2", range(4, NT))
                for g in PAIRS:
                    label = ("L2", g)
                    open_bank(label, b)
                    for e in range(NT):
                        if g == 0:
                            pe.wait_ge(split_ready.sem, split_ready.at(("T2", e), b))
                        pe.wait_ge(htl_made.sem, htl_made.at((g, e), b))
                        for i in range(2):
                            product(psum(label)[:, F * i:F * (i + 1)], (htl_slot(g, e)[:, P * i:P * (i + 1)],), nm(Q_hi, Q_lo, e),
                                    e == 0 and i == 0, e == NT - 1, (bank_done, label) if e == NT - 1 and i == 1 else None)
                        if (g, e) in ((3, 1), (3, 6)):
                            transpose_x3(e // 6)

                def a_job(k, g):
                    source = ("x3T", g) if k == 1 else ("X%d" % (k - 1), g // 2, 1)
                    pe.wait_ge(split_ready.sem, split_ready.at(source, b))
                    support(("A%d" % k, g), R_hi, R_lo, lambda f: wpair(W_L3 + k - 1, f), b)

                def x_job(k, h, f, tiles=range(NT)):
                    spread_T(("X%d" % k, h, f), S_hi, S_lo, b, lambda m: ("A%d" % k, m // 2) if (h == 0 or k == 1) and f == 0 and m % 2 == 0 else None, tiles=tiles)

                a_job(1, 0)
                a_job(1, 1)
                pe.wait_ge(back_split.sem, back_split.at(1, b))
                for h in range(2):
                    x_job(1, h, 0, range(0, 4))
                    transpose_x3(2 + h)
                    x_job(1, h, 1, range(0, 4))
                    a_job(1, 2 + h)
                for h in range(2):
                    for f in range(FC):
                        x_job(1, h, f, range(4, NT))
                for k in (2, 3):
                    for g in PAIRS:
                        a_job(k, g)
                    if k == 2:
                        for h in range(2):
                            for f in range(FC):
                                x_job(k, h, f)
                for g in PAIRS:
                    label = ("L3", g)
                    open_bank(label, b)
                    for i in range(2):
                        for m in range(NT):
                            if g == 0 and i == 0 and m % 2 == 0:
                                pe.wait_ge(split_ready.sem, split_ready.at(("A3", m // 2), b))
                            a = N * m + P * (2 * g + i)
                            product(psum(label)[:, F * i:F * (i + 1)], (A_hi[:, a:a + P], A_lo[:, a:a + P]), nm(S_hi, S_lo, m), m == 0, m == NT - 1,
                                    (bank_done, label) if i == 1 and m == NT - 1 else None)

            for i in range(2):
                pe.wait_ge(w_full[W_L2B + i], 16)
                if i == 0:
                    pe.wait_ge(beta_made, HC)
                for j in range(2):
                    mm = nc.tensor.matmul(bank[7][:, 0:F], ytmp[:, P * (2 * i + j):P * (2 * i + j + 1)], raw_weight(W_L2B + i)[:, F * j:F * (j + 1)],
                                          start=(i == 0 and j == 0), stop=(i == 1 and j == 1))
                mm.then_inc(beta_done, 1)
            pe.wait_ge(w_split, len(W_FIRST))
            with pe.Fori(0, B - 1) as b:
                graph(b, False)
            graph(B - 1, True)

        @block.scalar
        def _(act):
            def hi(label, dst, src, b, scale=None):
                ins = nc.scalar.copy(dst, src) if scale is None else nc.scalar.activation(dst, src, ACT.Identity, scale=scale)
                ins.then_inc(hi_ready.sem, hi_ready.one(label))

            def hi_job(label, dst, b):
                act.wait_ge(bank_done.sem, bank_done.at(label, b))
                hi(label, dst, psum(label)[:] if len(label) == 2 else quad(psum(label)[:]), b)

            def refill(b, h, m):
                act.wait_ge(stage_full[slot_of(J_ADJ(h, m))], landed(J_ADJ(h, m), b))
                nc.scalar.copy(adj_chunk(A_hi, h, m), slot(slot_of(J_ADJ(h, m)))).then_inc(adj_hi.sem, adj_hi.one((h, m)))

            def split_xT(b, q):
                act.wait_ge(stage_full[slot_of(J_XT(q))], landed(J_XT(q), b))
                nc.scalar.copy(Q_hi[:, q * HALF:(q + 1) * HALF], slot(slot_of(J_XT(q)))).then_inc(xt_hi.sem, xt_hi.one(q))

            def root(norm, b):
                act.wait_ge(var_ready.sem, var_ready.at(norm, b))
                i = stat_slot(norm)
                v = mv[:, 2 * i:2 * (i + len(norm[1]))].rearrange("p (t k) -> p t k", k=2)[:, :, 1]
                nc.scalar.activation(std[:, i:i + len(norm[1])], v, ACT.Sqrt, bias=eps[:]).then_inc(std_ready.sem, std_ready.one(norm))

            def graph(b, last):
                for g in PAIRS:
                    hi_job(("S0", g), P_hi[:, 2 * F * g:2 * F * (g + 1)], b)

                def copy_xw(g):
                    act.wait_ge(bank_done.sem, bank_done.at(("XW", g), b))
                    nc.scalar.copy(y0[:, 2 * F * g:2 * F * (g + 1)], psum(("XW", g))[:]).then_inc(xw_copied.sem, xw_copied.one(g))

                def root_degrees(h):
                    act.wait_ge(deg_ready.sem, deg_ready.at(h, b))
                    nc.scalar.activation(dh[:, 4 * h:4 * h + 4], deg[:, 4 * h:4 * h + 4], ACT.Sqrt, bias=ones[:]).then_inc(sqdeg_ready.sem, sqdeg_ready.one(h))

                def x1_hi(norm):
                    act.wait_ge(dh_ready.sem, dh_ready.at(norm[1][0] // 4, b))
                    act.wait_ge(norm_ready.sem, norm_ready.at(norm, b))
                    for t in norm[1]:
                        hi(("x1", t), Q_hi[:, F * t:F * (t + 1)], xres[:, F * t:F * (t + 1)], b, dh[:, t:t + 1])

                act.wait_ge(w_split, WCH)
                copy_xw(0)
                copy_xw(1)
                root_degrees(0)
                for m in range(NT):
                    refill(b, 1, m)
                copy_xw(2)
                copy_xw(3)
                root(NORMS[0], b)

                def diag(h):
                    act.wait_ge(diag_added.sem, diag_added.at(h, b))
                    nc.scalar.copy(diagonal(A_hi, h), quad(ytmp[:, 0:HALF])).then_inc(diag_hi.sem, diag_hi.one(h))

                diag(0)
                root_degrees(1)
                x1_hi(NORMS[0])
                for m in COUNTED:
                    act.wait_ge(marked.sem, marked.at(m, b))
                    nc.scalar.activation(marks(m), marks(m), ACT.Copy, accum_out=cnt[:, NT + m:NT + m + 1]).then_inc(counted.sem, counted.one(m))
                root(NORMS[1], b)
                root(NORMS[2], b)
                x1_hi(NORMS[1])
                diag(1)
                x1_hi(NORMS[2])

                def x2(g):
                    norm = ("x2", (2 * g, 2 * g + 1))
                    act.wait_ge(norm_ready.sem, norm_ready.at(norm, b))
                    for t in norm[1]:
                        hi(("x2", t), P_hi[:, F * t:F * (t + 1)], xres[:, F * t:F * (t + 1)], b)

                def sum_weight(k):
                    act.wait_ge(weighed.sem, weighed.at(NAT[k], b))
                    nc.scalar.activation(weighed_in(k), weighed_in(k), ACT.Copy, accum_out=weight_of[:, NT * (k % 2) + k // 2:NT * (k % 2) + k // 2 + 1])\
                        .then_inc(weight_summed.sem, weight_summed.one(NAT[k]))

                def utile(h, f):
                    hi_job(("U", h, f), fmajor(P_hi, h, f), b)

                for k in range(3):
                    sum_weight(k)
                    utile(k // 2, k % 2)
                for k in range(3, WEIGHED_IN_Y - 1):
                    sum_weight(k)
                root(("x2", (0, 1)), b)
                utile(1, 1)
                sum_weight(WEIGHED_IN_Y - 1)
                for g in PAIRS:
                    x2(g)
                    for k in WEIGHED_WITH[g][:-1]:
                        sum_weight(k)
                    if g + 1 in PAIRS:
                        root(("x2", (2 * g + 2, 2 * g + 3)), b)
                    sum_weight(WEIGHED_WITH[g][-1])
                    if g == 1:
                        for h in range(2):
                            nc.scalar.copy(diagonal(A_hi, h), quad(colsum[:, HALF * h:HALF * (h + 1)])).then_inc(back_hi.sem, back_hi.one(h))

                def edges(kind):
                    for e in range(NT):
                        if kind == "T" and e == 0:
                            act.wait_ge(be_ready.sem, be_ready.at(0, b))
                        act.wait_ge(bank_done.sem, bank_done.at((kind, e // 2), b))
                        hi((kind, e), Q_hi[:, F * e:F * (e + 1)], psum((kind, e // 2))[:, F * (e % 2):F * (e % 2 + 1)], b, be[:, e:e + 1])

                edges("T")
                for f in range(FC):
                    hi_job(("Z", 0, f), fmajor(P_hi, 0, f), b)
                for s in range(STEPS):
                    if s == EARLY_H:
                        for f in range(FC):
                            hi_job(("Z", 1, f), fmajor(P_hi, 1, f), b)
                    t = s - T_LAG
                    if 0 <= t < NT:
                        hi_job(("hT", t), Q_hi[:, HALF * (t % SLOTS):HALF * (t % SLOTS + 1)], b)
                    if s < NT:
                        act.wait_ge(psum_read.sem, psum_read.at(("h", s), b))
                        nc.scalar.activation(slot(s % SLOTS), slot(s % SLOTS), ACT.Relu).then_inc(relu_ready.sem, relu_ready.one(("h", s)))
                    if 1 <= s <= NT:
                        root(("h", (s - 1,)), b)
                    if 0 <= s - Y_LAG < NT and (s - Y_LAG) % 2:
                        g = (s - Y_LAG) // 2
                        act.wait_ge(psum_read.sem, psum_read.at(("y", g), b))
                        hi(("y", g), P_hi[:, 2 * F * g:2 * F * (g + 1)], ytmp[:, 2 * F * (g % 2):2 * F * (g % 2 + 1)], b)
                edges("T2")
                def x3T(g):
                    hi_job(("x3T", g), R_hi[:, 2 * F * g:2 * F * (g + 1)], b)

                def a_hi(k, g):
                    hi_job(("A%d" % k, g), S_hi[:, 2 * F * g:2 * F * (g + 1)], b)

                root(("x3", (0, 1)), b)
                root(("x3", (2, 3)), b)
                x3T(0)
                x3T(1)
                a_hi(1, 0)
                root(("x3", (4, 5)), b)
                a_hi(1, 1)
                root(("x3", (6, 7)), b)
                for g in (2, 3):
                    x3T(g)
                    a_hi(1, g)
                i = 0
                for k in (1, 2, 3):
                    if k > 1:
                        for g in PAIRS:
                            a_hi(k, g)
                    if k == 2 and not last:
                        for q in range(4):
                            split_xT(b + 1, q)
                    if k < 3:
                        for h in range(2):
                            for f in range(FC):
                                label = ("X%d" % k, h, f)
                                y = ytmp[:, 2 * F * (i % 2):2 * F * (i % 2 + 1)]
                                act.wait_ge(bank_done.sem, bank_done.at(label, b))
                                if i >= 2:
                                    act.wait_ge(split_ready.sem, split_ready.at(xlabels[i - 2], b))
                                bias = cols_sb[:, 8 + 2 * (k - 1) + f:9 + 2 * (k - 1) + f]
                                nc.scalar.activation(y, psum(label)[:], ACT.Relu, bias=bias).then_inc(relu_ready.sem, relu_ready.one(label))
                                nc.scalar.activation(fmajor(R_hi, h, f), quad(psum(label)[:]), ACT.Relu, bias=bias).then_inc(hi_ready.sem, hi_ready.one(label))
                                i += 1
                for g in PAIRS:
                    if g >= 2 and not last:
                        if g == 2:
                            act.wait_ge(bank_done.sem, bank_done.at(("L3", 1), b))
                        for m in range(4 * (g - 2), 4 * (g - 1)):
                            refill(b + 1, 0, m)
                    root(("x4", (2 * g, 2 * g + 1)), b)

            def split_weights(chunks):
                for i in chunks:
                    act.wait_ge(w_full[i], 16)
                    if i in (W_L2B, W_L2B + 1):
                        act.wait_ge(w_scaled, 2 * (i - W_L2B + 1))
                    nc.scalar.copy(W_hi[:, i * HALF:(i + 1) * HALF], raw_weight(i)).then_inc(w_hi_done, 1)

            split_weights(W_FIRST)
            act.wait_ge(const_made, 3)
            for q in range(4):
                split_xT(0, q)
            split_weights(W_THEN)
            for m in range(0, 4):
                refill(0, 0, m)
            split_weights(W_LAST)
            for m in range(4, NT):
                refill(0, 0, m)
            with act.Fori(0, B - 1) as b:
                graph(b, False)
            graph(B - 1, True)

        @block.vector
        def _(dve):
            steps = Steps(DVE_STEPS)

            def link(ins, b):
                ins.then_inc(dve_step, steps.one())
                dve.wait_ge(dve_step, steps.now(b))

            def lo(label, hi_part, lo_part, src, b, scale=None, signal=None):
                dve.wait_ge(hi_ready.sem, hi_ready.at(label, b))
                if scale is None:
                    ins = nc.vector.tensor_tensor(lo_part, src, hi_part.bitcast(F32), ALU.subtract)
                else:
                    ins = nc.vector.scalar_tensor_tensor(out=lo_part, in0=src, scalar=scale, in1=hi_part.bitcast(F32), op0=ALU.mult, op1=ALU.subtract)
                ins.then_inc(split_ready.sem, split_ready.one(label))

            def lo_job(label, h_, l_, b):
                lo(label, h_, l_, psum(label)[:] if len(label) == 2 else quad(psum(label)[:]), b)

            def refill(b, h, m):
                dve.wait_ge(adj_hi.sem, adj_hi.at((h, m), b))
                nc.vector.tensor_tensor(adj_chunk(A_lo, h, m), slot(slot_of(J_ADJ(h, m))), adj_chunk(A_hi, h, m).bitcast(F32), ALU.subtract)\
                    .then_inc(adj_split.sem, adj_split.one((h, m)))

            def split_xT(b, q):
                dve.wait_ge(xt_hi.sem, xt_hi.at(q, b))
                c = slice(q * HALF, (q + 1) * HALF)
                nc.vector.tensor_tensor(Q_lo[:, c], slot(slot_of(J_XT(q))), Q_hi[:, c].bitcast(F32), ALU.subtract).then_inc(xt_split.sem, xt_split.one(q))

            def make_h(b, n, e):
                dve.wait_ge(stage_full[slot_of(J_NAT(n, e))], landed(J_NAT(n, e), b))
                nc.vector.tensor_scalar(slab[:, N * n + HALF * e:N * n + HALF * (e + 1)], slot(slot_of(J_NAT(n, e))), 0.0, None, ALU.not_equal)\
                    .then_inc(h_made.sem, h_made.one((n, e)))

            def make_ht(b, c):
                if c >= HT_SLOTS:
                    d = c - HT_SLOTS
                    if d % NT == NT - 1:
                        dve.wait_ge(bank_done.sem, bank_done.at(("Z", d // NT, 1), b))
                    else:
                        dve.wait_ge(ht_used.sem, ht_used.at(d, b))
                nc.vector.tensor_scalar(ht_slot(c), adj_chunk(A_hi, c // NT, c % NT).bitcast(F32), 0.0, None, ALU.not_equal)\
                    .then_inc(ht_made.sem, ht_made.one(c))

            def make_htl(b, g, e):
                c = NT * g + e
                if c == 0:
                    dve.wait_ge(bank_done.sem, bank_done.at(("Z", 1, 1), b))
                elif c == 6:
                    dve.wait_ge(bank_done.sem, bank_done.at(("T2", 3), b))
                elif c in (22, 28):
                    dve.wait_ge(bank_done.sem, bank_done.at(("L2", 0 if c == 22 else 1), b))
                a = N * e + 2 * P * g
                nc.vector.tensor_scalar(htl_slot(g, e), A_hi[:, a:a + 2 * P].bitcast(F32), 0.0, None, ALU.not_equal)\
                    .then_inc(htl_made.sem, htl_made.one((g, e)))

            def gather(norm, srcs):
                for k, src in enumerate(srcs):
                    ins = nc.vector.bn_stats(stats[:, 6 * (stat_slot(norm) + k):6 * (stat_slot(norm) + k + 1)], src)
                ins.then_inc(dve_step, steps.one())

            def moments(norm, b):
                i = stat_slot(norm)
                n = len(norm[1])
                dve.wait_ge(dve_step, steps.now(b))
                apart(dve)
                for k in range(n):
                    ins = nc.vector.bn_aggr(mv[:, 2 * (i + k):2 * (i + k + 1)], stats[:, 6 * (i + k):6 * (i + k + 1)])
                ins.then_inc(var_ready.sem, var_ready.one(norm))
                dve.wait_ge(var_ready.sem, var_ready.at(norm, b))
                m = mv[:, 2 * i:2 * (i + n)].rearrange("p (t k) -> p t k", k=2)[:, :, 0]
                nc.vector.tensor_scalar(negm[:, i:i + n], m, -1.0, None, ALU.mult)

            def statistics(norm, srcs, b):
                gather(norm, srcs)
                moments(norm, b)

            def invert(norm, b):
                dve.wait_ge(std_ready.sem, std_ready.at(norm, b))
                i = stat_slot(norm)
                n = len(norm[1])
                nc.vector.reciprocal(rstd[:, i:i + n], std[:, i:i + n]).then_inc(rstd_ready.sem, rstd_ready.one(norm))

            def tile_(t, i):
                return t[:, F * i:F * (i + 1)]

            def degrees(h, b):
                label = ("deg", h)
                c = slice(4 * h, 4 * h + 4)
                dve.wait_ge(bank_done.sem, bank_done.at(label, b))
                nc.vector.tensor_copy(deg[:, c], psum(label)[:, 0:4]).then_inc(psum_read.sem, psum_read.one(label))
                dve.wait_ge(psum_read.sem, psum_read.at(label, b))
                link(nc.vector.tensor_scalar(rdeg[:, c], deg[:, c], EPS_DEG, None, ALU.max), b)
                nc.vector.reciprocal(rdeg[:, c], rdeg[:, c]).then_inc(deg_ready.sem, deg_ready.one(h))
                dve.wait_ge(sqdeg_ready.sem, sqdeg_ready.at(h, b))
                dve.wait_ge(deg_ready.sem, deg_ready.at(h, b))
                nc.vector.reciprocal(dh[:, c], dh[:, c]).then_inc(dh_ready.sem, dh_ready.one(h))

            def graph(b, last):
                steps.n = 0
                for g in PAIRS:
                    c = slice(2 * F * g, 2 * F * (g + 1))
                    lo_job(("S0", g), P_hi[:, c], P_lo[:, c], b)

                def x1_read(norm):
                    for t in norm[1]:
                        g = t // 2
                        if t % 2 == 0:
                            dve.wait_ge(bank_done.sem, bank_done.at(("L0", g), b))
                            dve.wait_ge(xw_copied.sem, xw_copied.at(g, b))
                        y = tile_(y0, t)
                        nc.vector.scalar_tensor_tensor(out=y, in0=psum(("L0", g))[:, F * (t % 2):F * (t % 2 + 1)], scalar=rdeg[:, t:t + 1], in1=y, op0=ALU.mult, op1=ALU.add)\
                            .then_inc(psum_read.sem, psum_read.one(("L0", t)))

                def x1_stat(norm):
                    dve.wait_ge(psum_read.sem, psum_read.at(("L0", norm[1][-1]), b))
                    relu_add(norm, y0, 0)
                    moments(norm, b)

                def relu_add(norm, y_all, skip):
                    t, n = norm[1][0], len(norm[1])
                    y = y_all[:, F * (t - skip):F * (t - skip + n)]
                    link(nc.vector.scalar_tensor_tensor(out=y, in0=y, scalar=0.0, in1=xres[:, F * t:F * (t + n)], op0=ALU.max, op1=ALU.add), b)
                    gather(norm, [tile_(y_all, i - skip) for i in norm[1]])

                def x1_split(norm):
                    for t in norm[1]:
                        lo(("x1", t), tile_(Q_hi, t), tile_(Q_lo, t), tile_(xres, t), b, dh[:, t:t + 1])

                def count(m):
                    nc.vector.tensor_scalar(marks(m), adj_chunk(A_hi, 0, m).bitcast(F32), 0.0, 0.0, ALU.not_equal, ALU.add, accum_out=cnt[:, m:m + 1])\
                        .then_inc(dve_step, steps.one())

                def mark(m):
                    nc.vector.tensor_scalar(marks(m), adj_chunk(A_hi, 1, m).bitcast(F32), 0.0, None, ALU.not_equal).then_inc(marked.sem, marked.one(m))

                def diag(h):
                    dve.wait_ge(diag_hi.sem, diag_hi.at(h, b))
                    nc.vector.tensor_tensor(diagonal(A_lo, h), quad(ytmp[:, 0:HALF]), diagonal(A_hi, h).bitcast(F32), ALU.subtract).then_inc(diag_split.sem, diag_split.one(h))

                degrees(0, b)
                for m in range(NT):
                    count(m)
                for m in range(NT):
                    refill(b, 1, m)
                    if m == 5:
                        x1_read(NORMS[0])
                dve.wait_ge(x_in, b * 16 + 16)
                x1_stat(NORMS[0])
                invert(NORMS[0], b)
                dve.wait_ge(dve_step, steps.now(b))
                for m in COUNTED[:4]:
                    mark(m)
                degrees(1, b)
                diag(0)
                x1_split(NORMS[0])
                for m in COUNTED[4:]:
                    mark(m)
                x1_read(NORMS[1])
                x1_stat(NORMS[1])
                invert(NORMS[1], b)
                x1_read(NORMS[2])
                x1_stat(NORMS[2])
                invert(NORMS[2], b)
                x1_split(NORMS[1])
                diag(1)
                x1_split(NORMS[2])

                def x2_sum(g):
                    norm = ("x2", (2 * g, 2 * g + 1))
                    dve.wait_ge(bank_done.sem, bank_done.at(("L1", g), b))
                    if g >= 2:
                        dve.wait_ge(norm_ready.sem, norm_ready.at(("x2", (2 * g - 4, 2 * g - 3)), b))
                    for t in norm[1]:
                        nc.vector.scalar_tensor_tensor(out=tile_(ytmp, t % 4), in0=psum(("L1", g))[:, F * (t % 2):F * (t % 2 + 1)], scalar=dh[:, t:t + 1],
                                                       in1=rows_sb[:, 0:F], op0=ALU.mult, op1=ALU.add).then_inc(psum_read.sem, psum_read.one(("L1", t)))

                def x2_gather(g):
                    dve.wait_ge(psum_read.sem, psum_read.at(("L1", 2 * g + 1), b))
                    relu_add(("x2", (2 * g, 2 * g + 1)), ytmp, 4 * (g // 2))

                def x2_invert(g):
                    invert(("x2", (2 * g, 2 * g + 1)), b)

                def x2_split(g):
                    for t in (2 * g, 2 * g + 1):
                        lo(("x2", t), tile_(P_hi, t), tile_(P_lo, t), tile_(xres, t), b)

                dve.wait_ge(counted.sem, counted.at(COUNTED[-1], b))
                for k, (n, e) in enumerate(NAT):
                    make_h(b, n, e)
                    if k in (3, 5, 6):
                        i = (3, 5, 6).index(k)
                        lo_job(("U", i // 2, i % 2), fmajor(P_hi, i // 2, i % 2), fmajor(P_lo, i // 2, i % 2), b)
                    if k == 9:
                        dve.wait_ge(weight_summed.sem, weight_summed.at(NAT[4], b))
                        x2_sum(0)
                    if k == 11:
                        x2_gather(0)
                        moments(("x2", (0, 1)), b)
                    if k == 12:
                        x2_invert(0)
                        lo_job(("U", 1, 1), fmajor(P_hi, 1, 1), fmajor(P_lo, 1, 1), b)
                    if k == 13:
                        dve.wait_ge(weight_summed.sem, weight_summed.at(NAT[WEIGHED_IN_Y - 1], b))
                        x2_sum(1)
                        x2_gather(1)
                        x2_split(0)
                        moments(("x2", (2, 3)), b)
                x2_invert(1)
                for g in (2, 3):
                    x2_sum(g)
                    x2_gather(g)
                    x2_split(g - 1)
                    moments(("x2", (2 * g, 2 * g + 1)), b)
                    x2_invert(g)
                link(nc.vector.tensor_tensor(be[:], cnt[:, 0:NT], cnt[:, NT:2 * NT], ALU.add), b)
                link(nc.vector.tensor_scalar(be[:], be[:], 1.0, None, ALU.max), b)
                nc.vector.reciprocal(be[:], be[:]).then_inc(be_ready.sem, be_ready.one(0))
                x2_split(3)
                dve.wait_ge(weighed.sem, weighed.at(NAT[-1], b))
                dve.wait_ge(back_hi.sem, back_hi.at(1, b))
                for c in range(HT_SLOTS):
                    make_ht(b, c)

                def edges(kind, tiles=range(NT)):
                    dve.wait_ge(be_ready.sem, be_ready.at(0, b))
                    for e in tiles:
                        if e % 2 == 0:
                            dve.wait_ge(hi_ready.sem, hi_ready.at((kind, e + 1), b))
                        lo((kind, e), tile_(Q_hi, e), tile_(Q_lo, e), psum((kind, e // 2))[:, F * (e % 2):F * (e % 2 + 1)], b, be[:, e:e + 1])

                edges("T", range(0, 4))
                make_ht(b, 3)
                edges("T", (4, 5))
                make_ht(b, 4)
                edges("T", (6, 7))
                make_ht(b, 5)
                dve.wait_ge(weight_summed.sem, weight_summed.at(NAT[-1], b))
                link(nc.vector.tensor_tensor(dn[:], weight_of[:, 0:NT], weight_of[:, NT:2 * NT], ALU.add), b)
                link(nc.vector.tensor_scalar(dmask[:], dn[:], 0.0, None, ALU.is_gt), b)
                link(nc.vector.tensor_tensor(dn[:], dn[:], dmask[:], ALU.mult), b)
                link(nc.vector.scalar_tensor_tensor(out=dn[:], in0=dn[:], scalar=1.0, in1=dmask[:], op0=ALU.add, op1=ALU.subtract), b)
                link(nc.vector.reciprocal(dn[:], dn[:]), b)
                link(nc.vector.tensor_tensor(dn[:], dn[:], dmask[:], ALU.mult), b)
                for c in range(6, NT + 2):
                    make_ht(b, c)
                for h in range(2):
                    nc.vector.tensor_tensor(diagonal(A_lo, h), quad(colsum[:, HALF * h:HALF * (h + 1)]), diagonal(A_hi, h).bitcast(F32), ALU.subtract)\
                        .then_inc(back_split.sem, back_split.one(h))
                lo_job(("Z", 0, 0), fmajor(P_hi, 0, 0), fmajor(P_lo, 0, 0), b)
                make_ht(b, NT + 2)
                lo_job(("Z", 0, 1), fmajor(P_hi, 0, 1), fmajor(P_lo, 0, 1), b)
                for c in range(NT + 3, 2 * NT - 2):
                    make_ht(b, c)
                def rows_step(s):
                    if s < NT:
                        dve.wait_ge(bank_done.sem, bank_done.at(("h", s), b))
                        if s >= SLOTS:
                            dve.wait_ge(bank_done.sem, bank_done.at(("hT", s - SLOTS), b))
                        nc.vector.scalar_tensor_tensor(out=slot(s % SLOTS), in0=psum(("h", s))[:], scalar=dn[:, s:s + 1], in1=rows_sb[:, F:F + HID], op0=ALU.mult, op1=ALU.add)\
                            .then_inc(psum_read.sem, psum_read.one(("h", s)))
                    if 1 <= s <= NT:
                        dve.wait_ge(relu_ready.sem, relu_ready.at(("h", s - 1), b))
                        gather(("h", (s - 1,)), [slot((s - 1) % SLOTS)])
                    if 0 <= s - T_LAG < NT:
                        t = s - T_LAG
                        c = slice(HALF * (t % SLOTS), HALF * (t % SLOTS + 1))
                        lo_job(("hT", t), Q_hi[:, c], Q_lo[:, c], b)
                    if 1 <= s <= NT:
                        moments(("h", (s - 1,)), b)
                    if 0 <= s - Y_LAG < NT and (s - Y_LAG) % 2:
                        g = (s - Y_LAG) // 2
                        dve.wait_ge(bank_done.sem, bank_done.at(("y", g), b))
                        if g >= 2:
                            dve.wait_ge(ylo_ready.sem, ylo_ready.at(g - 2, b))
                        nc.vector.tensor_tensor(ytmp[:, 2 * F * (g % 2):2 * F * (g % 2 + 1)].rearrange("p (t c) -> p t c", t=2), psum(("y", g))[:].rearrange("p (t c) -> p t c", t=2),
                                                betaW[:].unsqueeze(1).to_broadcast([P, 2, F]), ALU.add).then_inc(psum_read.sem, psum_read.one(("y", g)))
                    if 1 <= s <= NT:
                        invert(("h", (s - 1,)), b)
                rows_step(0)
                make_ht(b, 2 * NT - 2)
                make_ht(b, 2 * NT - 1)
                rows_step(1)
                for f in range(FC):
                    lo_job(("Z", 1, f), fmajor(P_hi, 1, f), fmajor(P_lo, 1, f), b)
                for s in range(EARLY_H, STEPS):
                    rows_step(s)
                htl = [(g, e) for g in PAIRS for e in range(NT)]
                for g, e in htl[:6]:
                    make_htl(b, g, e)
                edges("T2", range(0, 6))
                make_htl(b, *htl[6])
                edges("T2", (6,))
                make_htl(b, *htl[7])
                edges("T2", (7,))
                for g, e in htl[8:14]:
                    make_htl(b, g, e)

                def x3_sum(g):
                    norm = ("x3", (2 * g, 2 * g + 1))
                    dve.wait_ge(bank_done.sem, bank_done.at(("L2", g), b))
                    if g >= 2:
                        dve.wait_ge(norm_ready.sem, norm_ready.at(("x3", (2 * g - 4, 2 * g - 3)), b))
                    for t in norm[1]:
                        nc.vector.scalar_tensor_tensor(out=tile_(ytmp, t % 4), in0=psum(("L2", g))[:, F * (t % 2):F * (t % 2 + 1)], scalar=dn[:, t:t + 1],
                                                       in1=rows_sb[:, 3 * F:4 * F], op0=ALU.mult, op1=ALU.add).then_inc(psum_read.sem, psum_read.one(("L2", t)))
                    dve.wait_ge(psum_read.sem, psum_read.at(("L2", 2 * g + 1), b))
                    y = ytmp[:, 2 * F * (g % 2):2 * F * (g % 2 + 1)]
                    link(nc.vector.scalar_tensor_tensor(out=y, in0=xres[:, 2 * F * g:2 * F * (g + 1)], scalar=2.0, in1=y, op0=ALU.mult, op1=ALU.add), b)

                def x3_gather(g):
                    gather(("x3", (2 * g, 2 * g + 1)), [tile_(ytmp, t % 4) for t in (2 * g, 2 * g + 1)])

                def x3_stat(g):
                    x3_gather(g)
                    moments(("x3", (2 * g, 2 * g + 1)), b)

                def x3_invert(g):
                    invert(("x3", (2 * g, 2 * g + 1)), b)

                def x3T(g):
                    c = slice(2 * F * g, 2 * F * (g + 1))
                    lo_job(("x3T", g), R_hi[:, c], R_lo[:, c], b)

                def a_lo(k, g):
                    c = slice(2 * F * g, 2 * F * (g + 1))
                    lo_job(("A%d" % k, g), S_hi[:, c], S_lo[:, c], b)

                dve.wait_ge(ylo_ready.sem, ylo_ready.at(3, b))
                x3_sum(0)
                for g, e in htl[14:18]:
                    make_htl(b, g, e)
                x3_stat(0)
                for g, e in htl[18:24]:
                    make_htl(b, g, e)
                x3_invert(0)
                x3_sum(1)
                for g, e in htl[24:28]:
                    make_htl(b, g, e)
                x3_stat(1)
                for g, e in htl[28:]:
                    make_htl(b, g, e)
                x3_invert(1)
                x3T(0)
                x3_sum(2)
                x3T(1)
                x3_gather(2)
                a_lo(1, 0)
                moments(("x3", (4, 5)), b)
                x3_invert(2)
                a_lo(1, 1)
                x3_sum(3)
                x3_stat(3)
                x3_invert(3)
                for g in (2, 3):
                    x3T(g)
                    a_lo(1, g)
                i = 0
                for k in (1, 2, 3):
                    if k > 1:
                        for g in PAIRS:
                            a_lo(k, g)
                    if k == 2 and not last:
                        for q in range(4):
                            split_xT(b + 1, q)
                    if k < 3:
                        for h in range(2):
                            for f in range(FC):
                                label = ("X%d" % k, h, f)
                                dve.wait_ge(relu_ready.sem, relu_ready.at(label, b))
                                lo(label, fmajor(R_hi, h, f), fmajor(R_lo, h, f), quad(ytmp[:, 2 * F * (i % 2):2 * F * (i % 2 + 1)]), b)
                                i += 1
                for g in PAIRS:
                    norm = ("x4", (2 * g, 2 * g + 1))
                    if g >= 2 and not last:
                        for m in range(4 * (g - 2), 4 * (g - 1)):
                            refill(b + 1, 0, m)
                    dve.wait_ge(bank_done.sem, bank_done.at(("L3", g), b))
                    dve.wait_ge(biased.sem, biased.at(2 * g + 1, b))
                    if g >= 2:
                        dve.wait_ge(norm_ready.sem, norm_ready.at(("x4", (2 * g - 4, 2 * g - 3)), b))
                    for t in norm[1]:
                        nc.vector.tensor_tensor(tile_(ytmp, t % 4), psum(("L3", g))[:, F * (t % 2):F * (t % 2 + 1)], tile_(xres, t), ALU.add)\
                            .then_inc(last_read.sem, last_read.one(("L3", t)))
                    dve.wait_ge(last_read.sem, last_read.at(("L3", 2 * g + 1), b))
                    statistics(norm, [tile_(ytmp, t % 4) for t in norm[1]], b)
                    invert(norm, b)
                assert steps.n == DVE_STEPS, steps.n

            dve.wait_ge(const_in, 48)
            nc.vector.tensor_copy(eye_r[:], ytmp[:, 0:P]).then_inc(const_made, 1)
            nc.vector.memset(ones[:], 1.0).then_inc(const_made, 1)
            nc.vector.memset(eps[:], EPS_LN).then_inc(const_made, 1)
            dve.wait_ge(const_made, 3)
            for j in range(HC):
                nc.vector.tensor_scalar(ytmp[:, P * j:P * (j + 1)], cols_sb[:, 4 + j:5 + j].to_broadcast([P, P]), 1.0, None, ALU.mult).then_inc(beta_made, 1)
            def split_weights(chunks):
                for i in chunks:
                    w = raw_weight(i)
                    if i in (W_L2B, W_L2B + 1):
                        dve.wait_ge(beta_done, i - W_L2B + 1)
                        for j in range(2):
                            g = 2 * (i - W_L2B) + j
                            nc.vector.tensor_scalar(w[:, F * j:F * (j + 1)], w[:, F * j:F * (j + 1)], cols_sb[:, g:g + 1], None, ALU.mult).then_inc(w_scaled, 1)
                    dve.wait_ge(w_hi_done, W_ORDER.index(i) + 1)
                    c = slice(i * HALF, (i + 1) * HALF)
                    nc.vector.tensor_tensor(W_lo[:, c], w, W_hi[:, c].bitcast(F32), ALU.subtract).then_inc(w_split, 1)

            split_weights(W_FIRST)
            for q in range(4):
                split_xT(0, q)
            split_weights(W_THEN)
            nc.vector.tensor_copy(betaW[:], bank[7][:, 0:F]).then_inc(last_read.sem, 1)
            for m in range(0, 4):
                refill(0, 0, m)
            split_weights(W_LAST)
            for m in range(4, NT):
                refill(0, 0, m)
            with dve.Fori(0, B - 1) as b:
                graph(b, False)
            graph(B - 1, True)

        @block.gpsimd
        def _(pool):
            def sum_adj(b, h, m):
                pool.wait_ge(stage_full[slot_of(J_ADJ(h, m))], landed(J_ADJ(h, m), b))
                s = slot(slot_of(J_ADJ(h, m)))
                acc = colsum[:, HALF * h:HALF * (h + 1)]
                if m == 0:
                    apart(pool)
                    ins = nc.gpsimd.tensor_scalar(acc, s, 1.0, 0.0, ALU.mult, ALU.add)
                else:
                    pool.wait_ge(adj_summed.sem, adj_summed.at((h, m - 1), b))
                    ins = nc.gpsimd.tensor_tensor(acc, acc, s, ALU.add)
                ins.then_inc(adj_summed.sem, adj_summed.one((h, m)))

            def apply(norm, srcs, dsts, b):
                pool.wait_ge(rstd_ready.sem, rstd_ready.at(norm, b))
                apart(pool)
                i = stat_slot(norm)
                for k, (s, d) in enumerate(zip(srcs, dsts)):
                    ins = nc.gpsimd.tensor_scalar(d, s, negm[:, i + k:i + k + 1], rstd[:, i + k:i + k + 1], ALU.add, ALU.mult)
                ins.then_inc(norm_ready.sem, norm_ready.one(norm))

            def apply_tiles(norm, b):
                apply(norm, [ytmp[:, F * (t % 4):F * (t % 4 + 1)] for t in norm[1]], [xres[:, F * t:F * (t + 1)] for t in norm[1]], b)

            def graph(b, last):
                for m in range(NT):
                    sum_adj(b, 1, m)
                def add_identity(h):
                    saved = quad(colsum[:, HALF * h:HALF * (h + 1)])
                    pool.wait_ge(bank_done.sem, bank_done.at(("L0", 2 * h + 1), b))
                    nc.gpsimd.tensor_tensor(saved, diagonal(A_hi, h).bitcast(F32), diagonal(A_lo, h).bitcast(F32), ALU.add).then_inc(diag_saved.sem, diag_saved.one(h))
                    pool.wait_ge(diag_saved.sem, diag_saved.at(h, b))
                    if h == 1:
                        pool.wait_ge(diag_split.sem, diag_split.at(0, b))
                    nc.gpsimd.tensor_tensor(quad(ytmp[:, 0:HALF]), saved, eye_r[:].bitcast(F32).unsqueeze(1).to_broadcast([P, 4, P]), ALU.add)\
                        .then_inc(diag_added.sem, diag_added.one(h))

                def x1(norm):
                    apply(norm, [y0[:, F * t:F * (t + 1)] for t in norm[1]], [xres[:, F * t:F * (t + 1)] for t in norm[1]], b)

                add_identity(0)
                x1(NORMS[0])
                x1(NORMS[1])
                add_identity(1)
                x1(NORMS[2])
                def weigh(k):
                    n, e = NAT[k]
                    if k == 0:
                        pool.wait_ge(w_in, b * 16 + 16)
                        pool.wait_ge(diag_split.sem, diag_split.at(1, b))
                    if k in range(2, WEIGHED_IN_Y):
                        pool.wait_ge(weight_summed.sem, weight_summed.at(NAT[k - 2 if k < 6 else k - 1], b))
                    if k >= WEIGHED_IN_Y + SLOTS:
                        pool.wait_ge(weight_summed.sem, weight_summed.at(NAT[k - SLOTS], b))
                    pool.wait_ge(h_made.sem, h_made.at(NAT[k] if k < WEIGHED_IN_Y else NAT[min(k + 2 * NT - SLOTS - WEIGHED_IN_Y, 2 * NT - 1)], b))
                    nc.gpsimd.tensor_tensor(weighed_in(k), slab[:, N * n + HALF * e:N * n + HALF * (e + 1)].bitcast(F32), w_row[:, HALF * e:HALF * (e + 1)], ALU.mult)\
                        .then_inc(weighed.sem, weighed.one(NAT[k]))

                for k in range(WEIGHED_IN_Y):
                    weigh(k)
                for g in PAIRS:
                    apply_tiles(("x2", (2 * g, 2 * g + 1)), b)
                    for k in WEIGHED_WITH[g]:
                        weigh(k)
                for s in range(STEPS):
                    if 1 <= s <= NT:
                        apply(("h", (s - 1,)), [slot((s - 1) % SLOTS)], [slot((s - 1) % SLOTS)], b)
                    if 0 <= s - Y_LAG < NT and (s - Y_LAG) % 2:
                        g = (s - Y_LAG) // 2
                        pool.wait_ge(hi_ready.sem, hi_ready.at(("y", g), b))
                        c = slice(2 * F * g, 2 * F * (g + 1))
                        nc.gpsimd.tensor_tensor(P_lo[:, c], ytmp[:, 2 * F * (g % 2):2 * F * (g % 2 + 1)], P_hi[:, c].bitcast(F32), ALU.subtract)\
                            .then_inc(ylo_ready.sem, ylo_ready.one(g))
                for g in PAIRS:
                    apply_tiles(("x3", (2 * g, 2 * g + 1)), b)
                for t in range(NT):
                    if t % 2 == 0:
                        pool.wait_ge(bank_done.sem, bank_done.at(("x3T", t // 2), b))
                    pool.wait_ge(norm_ready.sem, norm_ready.at(("x3", (6, 7)), b))
                    c = slice(F * t, F * (t + 1))
                    nc.gpsimd.tensor_tensor(xres[:, c], xres[:, c], rows_sb[:, 4 * F:5 * F], ALU.add).then_inc(biased.sem, biased.one(t))
                for g in PAIRS:
                    if g >= 2 and not last:
                        for m in range(4 * (g - 2), 4 * (g - 1)):
                            sum_adj(b + 1, 0, m)
                    apply_tiles(("x4", (2 * g, 2 * g + 1)), b)

            for m in range(NT):
                sum_adj(0, 0, m)
            with pool.Fori(0, B - 1) as b:
                graph(b, False)
            graph(B - 1, True)


DVE_STEPS = 52


def stat_slot(norm):
    return norm[1][0] % 4


def kernel(**inputs):
    import numpy as np
    import concourse.bacc as bacc
    from concourse.bass_utils import run_bass_kernel_spmd

    g = {k: np.asarray(v) for k, v in inputs.items()}
    x, adj = g["x"], g["adj"]

    def chunk(w):
        return w.reshape(2, P, F).transpose(1, 0, 2).reshape(P, 2 * F)

    w0 = g["L0_gnn_W"]
    w0_x, w0_agg = w0[:, :F].T, w0[:, F:].T
    w1, w2 = g["L2_gnn_W1"].T, g["L2_gnn_W2"].T
    weights = [np.concatenate([w0_agg[P * c:P * (c + 1)], w0_x[P * c:P * (c + 1)]], axis=1) for c in range(2)]
    weights += [chunk(g["L1_gnn_kernel"])]
    weights += [w1[P * c:P * (c + 1)] for c in range(2)]
    weights += [chunk(w2[2 * P * c:2 * P * (c + 1)]) for c in range(2)]
    weights += [chunk(g["L3_gnn_W%d" % k]) for k in (1, 2, 3)]
    rows = np.concatenate([g["L1_gnn_bias"], g["L2_gnn_b1"], g["L2_gnn_b2"], g["L3_gnn_b3"]])
    arrays = {
        "x": x,
        "xT": x.reshape(B, NT, P, FC, P).transpose(0, 4, 1, 3, 2).reshape(B, P, NT * F),
        "adj": adj,
        "adjT": adj.transpose(0, 2, 1),
        "weights": np.stack(weights),
        "rows": np.broadcast_to(rows, (P, rows.size)),
        "cols": np.concatenate([g["L2_gnn_gamma"].reshape(HC, P).T, g["L2_gnn_beta"].reshape(HC, P).T,
                                g["L3_gnn_b1"].reshape(FC, P).T, g["L3_gnn_b2"].reshape(FC, P).T], axis=1),
        "eye": np.eye(P, dtype=np.float32),
    }
    arrays = {k: np.ascontiguousarray(v) for k, v in arrays.items()}
    nc = bacc.Bacc("TRN2", target_bir_lowering=False, num_devices=1)
    aps = [nc.dram_tensor(k + "_dram", v.shape, F32, kind="ExternalInput").ap() for k, v in arrays.items()]
    out = nc.dram_tensor("out_dram", (B, N, F), F32, kind="ExternalOutput").ap()
    build(nc, *aps, out)
    r = run_bass_kernel_spmd(nc, [{k + "_dram": v for k, v in arrays.items()}], core_ids=[0])
    return r.results[0]["out_dram"]
```
